# Optimizing a Trainium2 kernel written in Bass

```python
import numpy as np
import jax
import jax.numpy as jnp

def _softmax(x, axis=-1):
    return jax.nn.softmax(x, axis=axis)

def _gelu(x):
    return jax.nn.gelu(x, approximate=True)

def _silu(x):
    return jax.nn.silu(x)

def _sigmoid(x):
    return jax.nn.sigmoid(x)

def _layernorm(x, axis=-1, eps=1e-05):
    m = jnp.mean(x, axis=axis, keepdims=True)
    v = jnp.var(x, axis=axis, keepdims=True)
    return (x - m) / jnp.sqrt(v + eps)

def _scatter_add(tgt, idx, src, axis=0):
    return tgt.at[idx].add(src)

def _segment_sum(src, seg, n):
    return jax.ops.segment_sum(src, seg, n)
kernel_name = 'mk_gnn_resnorm_d4_gnn_r16_adb50e'

def setup_inputs(seed: int=0):
    np.random.seed(seed)
    _w = jnp.asarray

    def _rec_inputs():
        import jax
        import jax.numpy as jnp
        _gk = jax.random.key(seed)
        x = -0.0003713 + 1 * jax.random.normal(jax.random.fold_in(_gk, 1), (3125, 256), jnp.float32)
        src = jax.random.randint(jax.random.fold_in(_gk, 2), (100000,), 0, 3125, jnp.int32)
        dst = jax.random.randint(jax.random.fold_in(_gk, 3), (100000,), 0, 3125, jnp.int32)
        _o = jnp.argsort(dst, stable=True)
        src = src[_o]
        dst = dst[_o]
        edge_attr_3 = -1.09012e-05 + 0.99985 * jax.random.normal(jax.random.fold_in(_gk, 12), (100000, 3), jnp.float32)
        edge_attr_4 = 0.000126197 + 0.999763 * jax.random.normal(jax.random.fold_in(_gk, 13), (100000, 4), jnp.float32)
        edge_attr_8 = jax.random.uniform(jax.random.fold_in(_gk, 14), (100000, 8), jnp.float32, 0.0, 1)
        edge_weight = jax.random.uniform(jax.random.fold_in(_gk, 16), (100000,), jnp.float32, 0.0, 0.999998)
        return (x, src, dst, edge_attr_3, edge_attr_4, edge_attr_8, edge_weight)
    x, src, dst, edge_attr_3, edge_attr_4, edge_attr_8, edge_weight = _rec_inputs()

    def _L0_gnn_setup():
        import jax, jax.numpy as jnp
        import numpy as np
        N_NODES = 3125
        N_EDGES = 18750
        D = 256
        EPS = 1e-12

        def _gcn_layer(x, W, b, src, dst, norm, n_nodes):
            xt = x @ W
            msg = xt[src] * norm[:, None]
            agg = jax.ops.segment_sum(msg, dst, num_segments=n_nodes)
            return jax.nn.relu(agg + b)
        key = jax.random.key(seed)
        ks = jax.random.split(key, 10)
        h5_all = jax.random.normal(ks[0], (N_NODES, D), dtype=jnp.float32)
        edge_index = jax.random.randint(ks[1], (2, N_EDGES), 0, N_NODES, dtype=jnp.int64)
        edge_weight = jax.random.uniform(ks[2], (N_EDGES,), dtype=jnp.float32)
        s = 1.0 / np.sqrt(D)
        W6 = jax.random.normal(ks[3], (D, D), dtype=jnp.float32) * s
        b6 = jnp.zeros((D,), dtype=jnp.float32)
        W7 = jax.random.normal(ks[4], (D, D), dtype=jnp.float32) * s
        b7 = jnp.zeros((D,), dtype=jnp.float32)
        Wp = jax.random.normal(ks[5], (D, D), dtype=jnp.float32) * s
        bp = jnp.zeros((D,), dtype=jnp.float32)
        return {'h5_all': h5_all, 'edge_index': edge_index, 'edge_weight': edge_weight, 'W6': W6, 'b6': b6, 'W7': W7, 'b7': b7, 'Wp': Wp, 'bp': bp}
    _L0_gnn_all = _L0_gnn_setup()
    _L0_gnn_in = {k: v for k, v in _L0_gnn_all.items() if k in ('W6', 'b6', 'W7', 'b7', 'Wp', 'bp')}
    del _L0_gnn_all

    def _L1_gnn_setup():
        import jax, jax.numpy as jnp
        import numpy as np
        N_NODES = 1250
        N_EDGES = 20000
        MUL = 64
        NUM_BASIS = 8
        INV_SQRT3 = 0.5773502691896258
        EPS = 1e-05
        key = jax.random.key(seed)
        k = jax.random.split(key, 16)
        return {'node_hiddens': jax.random.normal(k[0], (N_NODES, 4 * MUL), dtype=jnp.float32), 'edge_attr': jax.random.uniform(k[1], (N_EDGES, NUM_BASIS), dtype=jnp.float32), 'edge_sh': jax.random.normal(k[2], (N_EDGES, 4), dtype=jnp.float32), 'w1_s': jax.random.normal(k[3], (MUL, MUL), dtype=jnp.float32), 'w1_v': jax.random.normal(k[4], (MUL, MUL), dtype=jnp.float32), 'wsc_s': jax.random.normal(k[5], (MUL, MUL), dtype=jnp.float32), 'wsc_v': jax.random.normal(k[6], (MUL, MUL), dtype=jnp.float32), 'w2_s': jax.random.normal(k[7], (2 * MUL, MUL), dtype=jnp.float32), 'w2_v': jax.random.normal(k[8], (2 * MUL, MUL), dtype=jnp.float32), 'fc_w1': jax.random.normal(k[9], (NUM_BASIS, 64), dtype=jnp.float32), 'fc_w2': jax.random.normal(k[10], (64, 64), dtype=jnp.float32), 'fc_w3': jax.random.normal(k[11], (64, 4 * MUL), dtype=jnp.float32), 'g_s': jnp.ones((MUL,), dtype=jnp.float32), 'g_v': jnp.ones((MUL,), dtype=jnp.float32), 'edge_index': jax.random.randint(k[12], (2, N_EDGES), 0, N_NODES)}
    _L1_gnn_all = _L1_gnn_setup()
    _L1_gnn_in = {k: v for k, v in _L1_gnn_all.items() if k in ('w1_s', 'w1_v', 'wsc_s', 'wsc_v', 'w2_s', 'w2_v', 'fc_w1', 'fc_w2', 'fc_w3', 'g_s', 'g_v')}
    del _L1_gnn_all

    def _L2_gnn_setup():
        import jax, jax.numpy as jnp
        import numpy as np
        N = 3125
        E = 25000
        IN = 256
        H = 8
        D = 32
        EF = 3
        key = jax.random.key(seed)
        ks = jax.random.split(key, 8)
        x = jax.random.normal(ks[0], (N, IN), dtype=jnp.float32)
        edge_index = jax.random.randint(ks[1], (2, E), 0, N, dtype=jnp.int64)
        edge_attr = jax.random.normal(ks[2], (E, EF), dtype=jnp.float32)
        W = jax.random.normal(ks[3], (H * D, IN), dtype=jnp.float32) * np.float32(np.sqrt(2.0 / (IN + H * D)))
        a_src = jax.random.normal(ks[4], (H, D), dtype=jnp.float32) * np.float32(np.sqrt(2.0 / (H + D)))
        a_dst = jax.random.normal(ks[5], (H, D), dtype=jnp.float32) * np.float32(np.sqrt(2.0 / (H + D)))
        edge_W = jax.random.normal(ks[6], (H * D, EF), dtype=jnp.float32) * np.float32(np.sqrt(2.0 / (EF + H * D)))
        edge_b = jnp.zeros((H * D,), dtype=jnp.float32)
        bias = jnp.zeros((H * D,), dtype=jnp.float32)
        return {'x': x, 'W': W, 'a_src': a_src, 'a_dst': a_dst, 'edge_W': edge_W, 'edge_b': edge_b, 'bias': bias, 'edge_attr': edge_attr, 'edge_index': edge_index}
    _L2_gnn_all = _L2_gnn_setup()
    _L2_gnn_in = {k: v for k, v in _L2_gnn_all.items() if k in ('W', 'a_src', 'a_dst', 'edge_W', 'edge_b', 'bias')}
    del _L2_gnn_all

    def _L3_gnn_setup():
        import jax, jax.numpy as jnp
        import numpy as np
        N_NODES = 625
        N_EDGES = 20000
        D_IN = 256
        D_OUT = 256
        key = jax.random.key(seed)
        k1, k2, k3, k4, k5 = jax.random.split(key, 5)
        row = jax.random.randint(k1, (N_EDGES,), 0, N_NODES, dtype=jnp.int32)
        col = jax.random.randint(k2, (N_EDGES,), 0, N_NODES, dtype=jnp.int32)
        X = jax.random.normal(k3, (N_NODES, D_IN), dtype=jnp.float32)
        W = jax.random.normal(k4, (D_IN, D_OUT), dtype=jnp.float32) * (1.0 / np.sqrt(D_IN))
        b = jax.random.normal(k5, (D_OUT,), dtype=jnp.float32) * 0.01
        return {'row': row, 'col': col, 'X': X, 'W': W, 'b': b}
    _L3_gnn_all = _L3_gnn_setup()
    _L3_gnn_in = {k: v for k, v in _L3_gnn_all.items() if k in ('W', 'b')}
    del _L3_gnn_all
    return {'x': x, 'src': src, 'dst': dst, 'edge_attr_3': edge_attr_3, 'edge_attr_4': edge_attr_4, 'edge_attr_8': edge_attr_8, 'edge_weight': edge_weight, 'L0_gnn_W6': _L0_gnn_in['W6'], 'L0_gnn_b6': _L0_gnn_in['b6'], 'L0_gnn_W7': _L0_gnn_in['W7'], 'L0_gnn_b7': _L0_gnn_in['b7'], 'L0_gnn_Wp': _L0_gnn_in['Wp'], 'L0_gnn_bp': _L0_gnn_in['bp'], 'L1_gnn_w1_s': _L1_gnn_in['w1_s'], 'L1_gnn_w1_v': _L1_gnn_in['w1_v'], 'L1_gnn_wsc_s': _L1_gnn_in['wsc_s'], 'L1_gnn_wsc_v': _L1_gnn_in['wsc_v'], 'L1_gnn_w2_s': _L1_gnn_in['w2_s'], 'L1_gnn_w2_v': _L1_gnn_in['w2_v'], 'L1_gnn_fc_w1': _L1_gnn_in['fc_w1'], 'L1_gnn_fc_w2': _L1_gnn_in['fc_w2'], 'L1_gnn_fc_w3': _L1_gnn_in['fc_w3'], 'L1_gnn_g_s': _L1_gnn_in['g_s'], 'L1_gnn_g_v': _L1_gnn_in['g_v'], 'L2_gnn_W': _L2_gnn_in['W'], 'L2_gnn_a_src': _L2_gnn_in['a_src'], 'L2_gnn_a_dst': _L2_gnn_in['a_dst'], 'L2_gnn_edge_W': _L2_gnn_in['edge_W'], 'L2_gnn_edge_b': _L2_gnn_in['edge_b'], 'L2_gnn_bias': _L2_gnn_in['bias'], 'L3_gnn_W': _L3_gnn_in['W'], 'L3_gnn_b': _L3_gnn_in['b']}

def reference(x, src, dst, edge_attr_3, edge_attr_4, edge_attr_8, edge_weight, L0_gnn_W6, L0_gnn_b6, L0_gnn_W7, L0_gnn_b7, L0_gnn_Wp, L0_gnn_bp, L1_gnn_w1_s, L1_gnn_w1_v, L1_gnn_wsc_s, L1_gnn_wsc_v, L1_gnn_w2_s, L1_gnn_w2_v, L1_gnn_fc_w1, L1_gnn_fc_w2, L1_gnn_fc_w3, L1_gnn_g_s, L1_gnn_g_v, L2_gnn_W, L2_gnn_a_src, L2_gnn_a_dst, L2_gnn_edge_W, L2_gnn_edge_b, L2_gnn_bias, L3_gnn_W, L3_gnn_b):
    import jax
    import jax.numpy as jnp

    def _L0_gnn_ref(h5_all, edge_index, edge_weight, W6, b6, W7, b7, Wp, bp):
        import jax, jax.numpy as jnp
        import numpy as np
        N_NODES = 3125
        N_EDGES = 18750
        D = 256
        EPS = 1e-12

        def _gcn_layer(x, W, b, src, dst, norm, n_nodes):
            xt = x @ W
            msg = xt[src] * norm[:, None]
            agg = jax.ops.segment_sum(msg, dst, num_segments=n_nodes)
            return jax.nn.relu(agg + b)
        src, dst = (edge_index[0], edge_index[1])
        deg_out = jax.ops.segment_sum(edge_weight, src, num_segments=N_NODES)
        deg_in = jax.ops.segment_sum(edge_weight, dst, num_segments=N_NODES)
        norm = edge_weight * jax.lax.rsqrt(deg_out[src] * deg_in[dst] + EPS)
        h6 = _gcn_layer(h5_all, W6, b6, src, dst, norm, N_NODES)
        h7 = _gcn_layer(h6, W7, b7, src, dst, norm, N_NODES)
        out = h7 @ Wp + bp
        return out

    def _L1_gnn_ref(node_hiddens, edge_attr, edge_sh, w1_s, w1_v, wsc_s, wsc_v, w2_s, w2_v, fc_w1, fc_w2, fc_w3, g_s, g_v, edge_index):
        import jax, jax.numpy as jnp
        import numpy as np
        N_NODES = 1250
        N_EDGES = 20000
        MUL = 64
        NUM_BASIS = 8
        INV_SQRT3 = 0.5773502691896258
        EPS = 1e-05
        N = node_hiddens.shape[0]
        xs = node_hiddens[:, :MUL]
        xv = node_hiddens[:, MUL:].reshape(N, MUL, 3)
        h = jax.nn.silu(edge_attr @ fc_w1 * (1.0 / np.sqrt(float(NUM_BASIS))))
        h = jax.nn.silu(h @ fc_w2 * (1.0 / np.sqrt(64.0)))
        w = h @ fc_w3 * (1.0 / np.sqrt(64.0))
        wA, wB, wC, wD = jnp.split(w, 4, axis=1)
        inv = 1.0 / np.sqrt(float(MUL))
        sc_s = xs @ wsc_s * inv
        sc_v = jnp.einsum('nud,uv->nvd', xv, wsc_v) * inv
        ys = xs @ w1_s * inv
        yv = jnp.einsum('nud,uv->nvd', xv, w1_v) * inv
        src = edge_index[0]
        dst = edge_index[1]
        es = ys[dst]
        ev = yv[dst]
        sh0 = edge_sh[:, :1]
        sh1 = edge_sh[:, 1:]
        m0a = wA * es * sh0
        m0b = wD * jnp.einsum('eud,ed->eu', ev, sh1) * INV_SQRT3
        m1a = wB[:, :, None] * es[:, :, None] * sh1[:, None, :]
        m1b = wC[:, :, None] * ev * sh0[:, :, None]
        mid_s = jnp.concatenate([m0a, m0b], axis=1)
        mid_v = jnp.concatenate([m1a, m1b], axis=1)
        ns = jax.ops.segment_sum(mid_s, src, num_segments=N)
        nv = jax.ops.segment_sum(mid_v, src, num_segments=N)
        deg = jax.ops.segment_sum(jnp.ones((src.shape[0],), node_hiddens.dtype), src, num_segments=N)
        dn = jax.lax.rsqrt(jnp.maximum(deg, 1.0))
        ns = ns * dn[:, None]
        nv = nv * dn[:, None, None]
        inv2 = 1.0 / np.sqrt(2.0 * MUL)
        os_ = ns @ w2_s * inv2 + sc_s
        ov = jnp.einsum('nud,uv->nvd', nv, w2_v) * inv2 + sc_v
        os_ = os_ * jax.lax.rsqrt(jnp.mean(os_ * os_, axis=1, keepdims=True) + EPS) * g_s
        rms_v = jax.lax.rsqrt(jnp.mean(ov * ov, axis=(1, 2))[:, None, None] + EPS)
        ov = ov * rms_v * g_v[None, :, None]
        return jnp.concatenate([os_, ov.reshape(N, 3 * MUL)], axis=1)

    def _L2_gnn_ref(x, W, a_src, a_dst, edge_W, edge_b, bias, edge_attr, edge_index):
        import jax, jax.numpy as jnp
        import numpy as np
        N = 3125
        E = 25000
        IN = 256
        H = 8
        D = 32
        EF = 3
        n = x.shape[0]
        h = (x @ W.T).reshape(n, H, D)
        src, dst = (edge_index[0], edge_index[1])
        h_src = h[src]
        h_dst = h[dst]
        alpha = jnp.einsum('ehd,hd->eh', h_src, a_src) + jnp.einsum('ehd,hd->eh', h_dst, a_dst)
        enc = jax.nn.relu(edge_attr @ edge_W.T + edge_b).reshape(-1, H, D)
        alpha = alpha + jnp.sum(enc * h_dst, axis=-1)
        alpha = jnp.where(alpha >= 0, alpha, 0.2 * alpha)
        amax = jax.ops.segment_max(alpha, dst, num_segments=n)
        ex = jnp.exp(alpha - amax[dst])
        denom = jax.ops.segment_sum(ex, dst, num_segments=n)
        attn = ex / jnp.maximum(denom[dst], 1e-10)
        out = jax.ops.segment_sum(h_src * attn[..., None], dst, num_segments=n)
        return out.reshape(n, H * D) + bias

    def _L3_gnn_ref(row, col, X, W, b):
        import jax, jax.numpy as jnp
        import numpy as np
        N_NODES = 625
        N_EDGES = 20000
        D_IN = 256
        D_OUT = 256
        N = X.shape[0]
        E = row.shape[0]
        deg = 1.0 + jax.ops.segment_sum(jnp.ones((E,), X.dtype), col, num_segments=N)
        dinv = jax.lax.rsqrt(deg)
        XW = X @ W + b
        scaled = XW * dinv[:, None]
        msg = jax.ops.segment_sum(scaled[col], row, num_segments=N)
        out = (msg + scaled) * dinv[:, None]
        return out
    edge_index = jnp.stack([src, dst])
    x = _layernorm(x + _L0_gnn_ref(x, edge_index, edge_weight, L0_gnn_W6, L0_gnn_b6, L0_gnn_W7, L0_gnn_b7, L0_gnn_Wp, L0_gnn_bp), axis=-1)
    x = _layernorm(x + _L1_gnn_ref(x, edge_attr_8, edge_attr_4, L1_gnn_w1_s, L1_gnn_w1_v, L1_gnn_wsc_s, L1_gnn_wsc_v, L1_gnn_w2_s, L1_gnn_w2_v, L1_gnn_fc_w1, L1_gnn_fc_w2, L1_gnn_fc_w3, L1_gnn_g_s, L1_gnn_g_v, edge_index), axis=-1)
    x = _layernorm(x + _L2_gnn_ref(x, L2_gnn_W, L2_gnn_a_src, L2_gnn_a_dst, L2_gnn_edge_W, L2_gnn_edge_b, L2_gnn_bias, edge_attr_3, edge_index), axis=-1)
    x = _layernorm(x + _L3_gnn_ref(src, dst, x, L3_gnn_W, L3_gnn_b), axis=-1)
    return x

_drawn_inputs = setup_inputs


def setup_inputs(seed=0):
    import zlib

    import numpy as np

    out = dict(_drawn_inputs(seed))
    spreads = {'L0_gnn_b6': (0.0, 0.1),
     'L0_gnn_b7': (0.0, 0.1),
     'L0_gnn_bp': (0.0, 0.1),
     'L1_gnn_g_s': (1.0, 0.2),
     'L1_gnn_g_v': (1.0, 0.2),
     'L2_gnn_edge_b': (0.0, 0.1),
     'L2_gnn_bias': (0.0, 0.1)}
    factors = {'edge_weight': 4.645, 'L0_gnn_W6': 2.812, 'L3_gnn_b': 6.321}
    for name, (base, spread) in spreads.items():
        noise = np.random.default_rng([zlib.crc32(name.encode()), seed]).standard_normal(out[name].shape)
        drawn = base * np.exp(spread * noise) if base else spread * noise
        out[name] = jnp.asarray(drawn.astype(out[name].dtype))
    for name, factor in factors.items():
        out[name] = (out[name] * factor).astype(out[name].dtype)
    return out
```

```python
from contextlib import ExitStack

import numpy as np
import concourse.bass as bass
from concourse import mybir

F32, I32 = mybir.dt.float32, mybir.dt.int32
ALU, ACT, AX = mybir.AluOpType, mybir.ActivationFunctionType, mybir.AxisListType

P = 128
N, E, D = 3125, 100000, 256
NB = -(-N // P)
NPAD = NB * P
LAST = N - (NB - 1) * P
EP = 125
EJ = E // EP
SUB = 32
NBD = NPAD // SUB
H, HD = 8, 32
MUL = 64


def up(n, m):
    return -(-n // m) * m


NCD = up((E + (P - 1) * -(-N // SUB)) // P, 16)
GS = 2
NUS = up((E + (GS * P - 1) * NB) // (GS * P), 16)
NCS = NUS * GS
RD, RS = 8, 16
D_IDX, D_DL, D_W, D_EA, D_ONE, D_DL32 = 0, 1, 2, 3, 6, 7
S_IDX, S_SL, S_SH, S_EA = 0, 1, 2, 6
TW = D + H
BIG = float(2.0 ** 100)
EPS0, EPS1 = 1e-12, 1e-5


class Queue:

    def __init__(self, eng, sem):
        self.eng, self.sem, self.count, self.waited = eng, sem, 0, {}

    def after(self, *marks):
        for m in marks:
            if m is None:
                continue
            if isinstance(m, list):
                self.after(*m)
                continue
            sem, value = m
            if self.waited.get(id(sem), 0) < value:
                self.eng.wait_ge(sem, value)
                self.waited[id(sem)] = value

    def did(self, ins):
        ins.then_inc(self.sem, 1)
        self.count += 1
        return self.sem, self.count

    def last(self):
        return (self.sem, self.count) if self.count else None


class Landing:

    def __init__(self, sem):
        self.sem, self.count = sem, 0

    def started(self, ins):
        ins.then_inc(self.sem, 16)
        self.count += 16
        return self.sem, self.count


def pipeline(n, *stages):
    for i in range(n + max(lag for lag, _ in stages)):
        for lag, f in stages:
            if 0 <= i - lag < n:
                f(i - lag)


def program(nc, t, out):
    with ExitStack() as ctx:
        def sem(name):
            return ctx.enter_context(nc.semaphore(name))

        V, A = Queue(nc.vector, sem("vector_done")), Queue(nc.scalar, sem("scalar_done"))
        T, G = Queue(nc.tensor, sem("tensor_done")), Queue(nc.gpsimd, sem("pool_done"))
        S = Queue(nc.sync, sem("sync_done"))
        v, a, pe, g, sp = V.eng, A.eng, T.eng, G.eng, S.eng
        landings = []

        def landing(name):
            landings.append(Landing(sem(name)))
            return landings[-1]

        def barrier():
            marks = [q.last() for q in (V, A, T, G)] + [(x.sem, x.count) for x in landings if x.count]
            for q in (V, A, T, G, S):
                q.after(*marks)

        def dram(name, shape, dt=F32):
            return nc.dram_tensor(name, shape, dt, kind="Internal").ap()

        def sb(name, width, dt=F32, parts=P):
            return ctx.enter_context(nc.sbuf_tensor(name, [parts, width], dt))[:, :]

        ps = [ctx.enter_context(nc.psum_tensor(f"bank{i}", [P, 512], F32))[:, :] for i in range(8)]

        rec_d_dram, rec_s_dram = dram("rec_d", (P * NCD, RD)), dram("rec_s", (P * NCS, RS))
        x_table, h6_table = dram("x_table", (NPAD, TW)), dram("h6_table", (NPAD, D))
        y_table, att_table = dram("y_table", (NPAD, D)), dram("att_table", (NPAD, TW))
        scaled_table = dram("scaled_table", (NPAD, D))
        rows_spill = dram("rows_spill", (NCD, P, D))
        din_dram = dram("din_dram", (NB, P))
        ew_dram = dram("ew_dram", (4, D))
        JD, JS = up(NCD, P) // P, up(NUS, P) // P
        b32_dram, blk_d_dram = dram("b32_dram", (P, JD), I32), dram("blk_d_dram", (P, JD), I32)
        blk_s_dram = dram("blk_s_dram", (P, JS), I32)

        ident, iota = sb("ident", P), sb("iota", P)
        lane = sb("lane", 1)
        rec_d = sb("rec_d_sb", NCD * RD)
        big = sb("big", max(NCS * RS, NCD * H + NB * TW))
        acc = sb("acc", NB * 512)
        x = sb("x_res", NB * D)
        norm = sb("norm", NCD)
        idx_s, sl_s = sb("idx_s", NCS, I32), sb("sl_s", NCS)
        deg_d, deg_s = sb("deg_d", 2 * NB), sb("deg_s", 2 * NB)
        unit_numbers = sb("unit_numbers", P * JD, I32, 3)
        b32_row, blk_d_row, blk_s_row = (unit_numbers[k:k + 1, :] for k in range(3))
        ring = sb("ring", 6100)
        wts = sb("wts", 2400)
        small = sb("small", 800)

        x3 = x.rearrange("p (b k) -> p b k", b=NB)
        recd3 = rec_d.rearrange("p (c r) -> p c r", r=RD)
        recd3i = rec_d.bitcast(I32).rearrange("p (c r) -> p c r", r=RD)

        def cut(buf, at, n, *dims):
            r = buf[:, at:at + n]
            if len(dims) == 2:
                r = r.rearrange("p (a b) -> p a b", a=dims[0])
            if len(dims) == 3:
                r = r.rearrange("p (a b c) -> p a b c", a=dims[0], b=dims[1])
            return r

        def lanes(col, n, k):
            return col.rearrange("p (n o) -> p n o", o=1).to_broadcast([col.shape[0], n, k])

        def rows(row, n, k):
            return row.rearrange("p (o k) -> p o k", o=1).to_broadcast([row.shape[0], n, k])

        class Numbers:
            def __init__(self, q, name, row, top):
                self.q, self.row, self.top = q, row, top
                self.regs = [q.eng.alloc_register(f"{name}{i}") for i in range(16)]
                self.first = None

            def at(self, i):
                if self.first != i // 16:
                    self.first = i // 16
                    self.q.eng.load(self.regs, self.row[0:1, self.first * 16:self.first * 16 + 16])
                return self.q.eng.snap(self.regs[i % 16], min_val=0, max_val=self.top)

        load_in, prefilled = landing("load_in"), landing("prefilled")
        s_w = landing("weights_in")

        m_iota = G.did(g.iota(iota, [[1, P]], base=0, channel_multiplier=0, allow_small_or_imprecise_dtypes=True))
        m_lane = G.did(g.iota(lane, [[0, 1]], base=0, channel_multiplier=1, allow_small_or_imprecise_dtypes=True))
        V.after(m_iota, m_lane)
        m_ident = V.did(v.tensor_scalar(ident, iota, lane[:, 0:1], None, ALU.is_equal))

        pad_s = big[:, 0:NCS * RS]
        m0 = V.did(v.memset(rec_d, 0.0))
        m1 = V.did(v.memset(pad_s, 0.0))
        V.after(m0, m1)
        for col in (D_DL, D_DL32):
            V.did(v.memset(recd3[:, :, col], -1.0))
        m_pad = V.did(v.memset(pad_s.rearrange("p (c r) -> p c r", r=RS)[:, :, S_SL], -1.0))
        S.after(m_pad)
        prefilled.started(sp.dma_start(rec_d_dram.rearrange("(p c) r -> p (c r)", p=P), rec_d))
        m_prefilled = prefilled.started(sp.dma_start(rec_s_dram.rearrange("(p c) r -> p (c r)", p=P), pad_s))

        S.after(m_prefilled)
        at = [0]

        def raw(width):
            r = big[0:EP, at[0]:at[0] + width]
            at[0] += width
            assert at[0] <= big.shape[1]
            return r

        src_i, dst_i, w_raw = raw(EJ).bitcast(I32), raw(EJ).bitcast(I32), raw(EJ)
        ea3_raw, ea4_raw, ea8_raw = raw(EJ * 3), raw(EJ * 4), rec_d[0:EP, 0:EJ * 8]
        for buf, name in ((src_i, "src"), (dst_i, "dst"), (w_raw, "edge_weight")):
            load_in.started(sp.dma_start(buf, t[name].rearrange("(p j) -> p j", p=EP)))
        for buf, name in ((ea4_raw, "edge_attr_4"), (ea8_raw, "edge_attr_8"), (ea3_raw, "edge_attr_3")):
            m_raw = load_in.started(sp.dma_start(buf, t[name].rearrange("(p j) k -> p (j k)", p=EP)))
        tmp_i, buckets, scan, pos = raw(EJ).bitcast(I32), raw(EJ), raw(EJ), raw(EJ)
        hit = ring[0:EP, 0:EJ].bitcast(I32)
        stage_s = acc[0:EP, 0:EJ * RS].rearrange("p (j r) -> p j r", r=RS)
        stage_d = x[0:EP, 0:EJ * RD].rearrange("p (j r) -> p j r", r=RD)
        before = ring[0:EP, 5900:5900 + P]
        ones = small[0:EP, 0:P]
        zero = small[0:EP, P:P + 1]
        V.after(m_ident, m_raw)
        A.after(m_raw)
        V.did(v.tensor_scalar(before, iota[0:EP, :], lane[0:EP, 0:1], None, ALU.is_gt))
        V.did(v.memset(ones, 1.0))
        V.did(v.memset(zero, 0.0))
        m_stage0 = [V.did(v.memset(stage_s[:, :, 14:16], 0.0)), V.did(v.memset(stage_d[:, :, D_ONE], 1.0))]

        def chain(ins):
            m = V.did(ins)
            V.after(m)
            return m

        def field(out_f, key, shift, mask):
            chain(v.tensor_scalar(tmp_i, key, shift, mask, ALU.logical_shift_right, ALU.bitwise_and))
            return chain(v.tensor_copy(out_f, tmp_i))

        ea4_3, ea8_3 = (ea4_raw.rearrange("p (j k) -> p j k", k=4), ea8_raw.rearrange("p (j k) -> p j k", k=8))
        ea3_3 = ea3_raw.rearrange("p (j k) -> p j k", k=3)
        m_attr_s = [A.did(a.copy(stage_s[:, :, S_SH:S_SH + 4], ea4_3)),
                    A.did(a.copy(stage_s[:, :, S_EA:S_EA + 8], ea8_3))]
        m_attr_d = [A.did(a.copy(stage_d[:, :, D_EA:D_EA + 3], ea3_3)),
                    A.did(a.copy(stage_d[:, :, D_W], w_raw))]
        V.did(v.tensor_copy(stage_s.bitcast(I32)[:, :, S_IDX], dst_i))
        V.did(v.tensor_copy(stage_d.bitcast(I32)[:, :, D_IDX], src_i))
        field(stage_s[:, :, S_SL], src_i, 0, P - 1)
        field(stage_d[:, :, D_DL], dst_i, 0, P - 1)
        field(stage_d[:, :, D_DL32], dst_i, 0, SUB - 1)

        tot, off = ring[0:EP, 900:1000], ring[0:EP, 1000:1100]
        units, ends = ring[:, 1100:1200], ring[:, 1200:1300]
        units_i = ring[:, 1300:1400].bitcast(I32)
        counted = ring[:, 1400:1400 + JD * NBD]
        number = ring[:, 2200:2200 + JD]
        bucket_of, bucket_i = ring[:, 2300:2300 + JD], ring[:, 2400:2400 + JD].bitcast(I32)
        block_i = ring[:, 2500:2500 + JD].bitcast(I32)

        def rank(key, shift, nb, unit_chunks, chunks, slot_row):
            unit = unit_chunks * P
            field(buckets, key, shift, (1 << 20) - 1)
            for b in range(nb):
                chain(v.tensor_scalar(scan, buckets, float(b), 0.0, ALU.is_equal, ALU.add,
                                      accum_out=tot[:, b:b + 1]))
            T.after(V.last())
            T.did(pe.matmul(ps[0][:, 0:nb], before, tot[:, 0:nb], start=True, stop=True))
            m = T.did(pe.matmul(ps[1][:, 0:nb], small[0:EP, 0:P], tot[:, 0:nb], start=True, stop=True))
            V.after(m)
            chain(v.tensor_scalar(units_i[:, 0:nb], ps[1][:, 0:nb], float(unit - 1), None, ALU.add))
            chain(v.tensor_scalar(units_i[:, 0:nb], units_i[:, 0:nb], unit.bit_length() - 1, None,
                                  ALU.logical_shift_right))
            chain(v.tensor_copy(units[:, 0:nb], units_i[:, 0:nb]))
            chain(v.tensor_tensor_scan(ends[:, 0:nb], units[:, 0:nb], small[:, P + 1:P + 2].to_broadcast([P, nb]),
                                       0.0, ALU.add, ALU.add))
            chain(v.tensor_tensor(off[:, 0:nb], ends[0:EP, 0:nb], units[0:EP, 0:nb], ALU.subtract))
            chain(v.tensor_scalar(off[:, 0:nb], off[:, 0:nb], float(unit), -1.0, ALU.mult, ALU.add))
            chain(v.tensor_tensor(off[:, 0:nb], off[:, 0:nb], ps[0][0:EP, 0:nb], ALU.add))
            for b in range(nb):
                chain(v.tensor_scalar(hit, buckets, float(b), None, ALU.is_equal))
                chain(v.tensor_tensor_scan(scan, hit, zero.to_broadcast([EP, EJ]), off[:, b:b + 1],
                                           ALU.add, ALU.add))
                chain(v.copy_predicated(pos, hit, scan))
            chain(v.tensor_copy(tmp_i, pos))
            chain(v.tensor_scalar(hit, tmp_i, P - 1, None, ALU.bitwise_and))
            chain(v.tensor_scalar(tmp_i, tmp_i, 7, None, ALU.logical_shift_right))
            chain(v.tensor_copy(scan, hit))
            chain(v.tensor_copy(pos, tmp_i))
            return chain(v.scalar_tensor_tensor(out=slot_row, in0=scan, scalar=float(chunks), in1=pos,
                                                op0=ALU.mult, op1=ALU.add))

        def bucket_numbers(nb, j):
            G.after(V.last())
            m = G.did(g.iota(number[:, 0:j], [[1, j]], base=0, channel_multiplier=j,
                             allow_small_or_imprecise_dtypes=True))
            V.after(m)
            c3 = counted[:, 0:j * nb].rearrange("p (j b) -> p j b", j=j)
            chain(v.tensor_tensor(c3, rows(ends[:, 0:nb], j, nb), lanes(number[:, 0:j], j, nb), ALU.is_le))
            chain(v.tensor_reduce(bucket_of[:, 0:j], c3, AX.X, ALU.add))
            return chain(v.tensor_scalar(bucket_i[:, 0:j], bucket_of[:, 0:j], float(nb - 1), None, ALU.min))

        chain(v.memset(small[:, P + 1:P + 2], 0.0))
        chain(v.memset(pos, 0.0))
        numbers_out, numbers_in = landing("numbers_out"), landing("numbers_in")
        scattered_s, scattered_d = landing("scattered_s"), landing("scattered_d")
        row_s, row_d = ring[0:EP, 2600:2600 + EJ].bitcast(I32), ring[0:EP, 3400:3400 + EJ].bitcast(I32)

        def scatter(row, stage, table, where, *marks):
            G.after(*marks)
            for j in range(EJ):
                m = where.started(g.indirect_dma_start(
                    out=table, out_offset=bass.IndirectOffsetOnAxis(ap=row[:, j:j + 1], axis=0),
                    in_=stage[:, j, :], in_offset=None))
            return m

        def keep_numbers(buf, table, row, n):
            S.after(V.last())
            m = numbers_out.started(sp.dma_start(table, buf))
            S.after(m)
            return numbers_in.started(sp.dma_start(row[0:1, 0:n], table.rearrange("(o p) j -> o (p j)", o=1)))

        m_row_s = rank(src_i, 7, NB, GS, NCS, row_s)
        bucket_numbers(NB, JS)
        keep_numbers(bucket_i[:, 0:JS], blk_s_dram, blk_s_row, P * JS)
        m_scattered_s = scatter(row_s, stage_s, rec_s_dram, scattered_s, m_prefilled, m_stage0, m_attr_s, m_row_s)
        m_row_d = rank(dst_i, 5, NBD, 1, NCD, row_d)
        V.after((numbers_out.sem, numbers_out.count))
        bucket_numbers(NBD, JD)
        chain(v.tensor_scalar(block_i, bucket_i, 2, None, ALU.logical_shift_right))
        keep_numbers(bucket_i, b32_dram, b32_row, P * JD)
        m_numbers = keep_numbers(block_i, blk_d_dram, blk_d_row, P * JD)
        m_scattered_d = scatter(row_d, stage_d, rec_d_dram, scattered_d, m_attr_d, m_row_d)

        BJ = 8
        low_f, high_f = buckets, scan
        for key, deg, bank in ((src_i, deg_s, 2), (dst_i, deg_d, 3)):
            field(low_f, key, 0, P - 1)
            field(high_f, key, 7, (1 << 20) - 1)
            used = [None, None]
            lo_bufs = [cut(wts[0:EP], 0, BJ * P, BJ, P), cut(wts[0:EP], BJ * P, BJ * P, BJ, P)]
            hi_bufs = [cut(ring[0:EP], 4300 + k * 2 * NB * BJ, 2 * NB * BJ, BJ, 2 * NB) for k in range(2)]
            for i in range(EJ // BJ):
                lo3, hi3, js = lo_bufs[i % 2], hi_bufs[i % 2], slice(i * BJ, i * BJ + BJ)
                V.after(used[i % 2])
                V.did(v.tensor_tensor(lo3, rows(iota[0:EP, :], BJ, P), lanes(low_f[:, js], BJ, P), ALU.is_equal))
                m = V.did(v.tensor_tensor(hi3[:, :, NB:2 * NB], rows(iota[0:EP, 0:NB], BJ, NB),
                                          lanes(high_f[:, js], BJ, NB), ALU.is_equal))
                V.after(m)
                m = V.did(v.tensor_tensor(hi3[:, :, 0:NB], hi3[:, :, NB:2 * NB], lanes(w_raw[:, js], BJ, NB),
                                          ALU.mult))
                T.after(m)
                for k in range(BJ):
                    j = i * BJ + k
                    ins = pe.matmul(ps[bank][:, 0:2 * NB], lo3[:, k, :], hi3[:, k, :], start=(j == 0),
                                    stop=(j == EJ - 1))
                used[i % 2] = T.did(ins)
            V.after(T.last())
            m_deg = chain(v.tensor_copy(deg, ps[bank][:, 0:2 * NB]))
        din_t, din_row = ring[0:NB, 5200:5200 + P], acc[:, 6400:6400 + NPAD]
        T.after(m_deg)
        m = T.did(pe.transpose(ps[4][0:NB, 0:P], deg_d[:, 0:NB], ident))
        V.after(m)
        m = chain(v.tensor_copy(din_t, ps[4][0:NB, 0:P]))
        S.after(m)
        din_out, din_in = landing("din_out"), landing("din_in")
        m = din_out.started(sp.dma_start(din_dram, din_t))
        S.after(m, m_scattered_s)
        m_din = din_in.started(sp.dma_start(
            din_row, din_dram.rearrange("(o b) p -> o (b p)", o=1).to_broadcast([P, NPAD])))
        barrier()

        x_in, rec_in = landing("x_in"), landing("rec_in")
        table_out = landing("table_out")
        stats = ring[:, 5000:5000 + NB * 6].rearrange("p (b s) -> p b s", s=6)
        mv = ring[:, 5200:5200 + NB * 2].rearrange("p (b s) -> p b s", s=2)
        rstd = ring[:, 5300:5300 + NB]

        def rsqrt_of(buf, mark):
            A.after(mark)
            m = A.did(a.activation(buf, buf, ACT.Sqrt))
            V.after(m)
            return chain(v.reciprocal(buf, buf))

        def layernorm():
            V.after(V.last())
            for b in range(NB):
                V.did(v.bn_stats(stats[:, b, :], x3[:, b, :]))
            V.after(V.last())
            for b in range(NB):
                V.did(v.bn_aggr(mv[:, b, :], stats[:, b, :]))
            V.after(V.last())
            m = chain(v.tensor_scalar(rstd, mv[:, :, 1], EPS1, None, ALU.add))
            rsqrt_of(rstd, m)
            for b in range(NB):
                V.did(v.tensor_scalar(x3[:, b, :], x3[:, b, :], mv[:, b, 0:1], rstd[:, b:b + 1],
                                      ALU.subtract, ALU.mult))
            return V.last()

        def write_table(table, view, mark):
            S.after(mark)
            return table_out.started(sp.dma_start(table.rearrange("(b p) k -> p b k", p=P), view))

        def linear(view, weight, finish):
            turned = cut(ring, 0, 512, 2, 256)
            cols = [None] * NB
            done, prod, fin = [None] * NB, [None] * NB, [None] * NB

            def turn(b):
                T.after(cols[b - 2] if b >= 2 else None)
                for k in range(2):
                    ins = pe.transpose(ps[b % 2][:, k * P:(k + 1) * P], view[:, b, k * P:(k + 1) * P], ident)
                done[b] = T.did(ins)

            def keep(b):
                A.after(done[b], prod[b - 2] if b >= 2 else None)
                cols[b] = A.did(a.copy(turned[:, b % 2, :], ps[b % 2][:, 0:D]))

            def product(b):
                T.after(cols[b], fin[b - 2] if b >= 2 else None)
                for k in range(2):
                    ins = pe.matmul(ps[2 + b % 2][:, 0:D], turned[:, b % 2, k * P:(k + 1) * P], weight[:, k, :],
                                    start=(k == 0), stop=(k == 1))
                prod[b] = T.did(ins)

            def end(b):
                V.after(prod[b])
                fin[b] = finish(b, ps[2 + b % 2][:, 0:D])

            pipeline(NB, (0, turn), (0, keep), (1, product), (2, end))

        def load(buf, src, slot=s_w):
            return slot.started(sp.dma_start(buf, src))

        def two(name):
            return t[name].rearrange("(k p) n -> p k n", p=P)

        def everywhere(name, n):
            return t[name].rearrange("(o n) -> o n", o=1).to_broadcast([P, n])

        blk_v = Numbers(V, "blk_v", blk_d_row, NB - 1)
        b32_v = Numbers(V, "b32_v", b32_row, NBD - 1)
        blk_t = Numbers(T, "blk_t", blk_d_row, NB - 1)

        w6, w7, wp = (cut(wts, k * 512, 512, 2, D) for k in range(3))
        load(w6, two("L0_gnn_W6"))
        load(w7, two("L0_gnn_W7"))
        load(wp, two("L0_gnn_Wp"))
        b6, b7, bp = (wts[:, 1536 + k * D:1536 + (k + 1) * D] for k in range(3))
        load(b6, everywhere("L0_gnn_b6", D))
        load(b7, everywhere("L0_gnn_b7", D))
        m_weights = load(bp, everywhere("L0_gnn_bp", D))
        m_rec = rec_in.started(sp.dma_start(rec_d, rec_d_dram.rearrange("(p c) r -> p (c r)", p=P)))
        m = V.did(v.memset(x, 0.0))
        S.after(m)
        x_in.started(sp.dma_start(x3[:, 0:NB - 1, :], t["x"][0:(NB - 1) * P, :].rearrange("(b p) k -> p b k", p=P)))
        m_x = x_in.started(sp.dma_start(x3[0:LAST, NB - 1, :], t["x"][(NB - 1) * P:N, :]))
        staged = cut(big, 0, NB * TW, NB, TW)
        V.after(m_x)
        V.did(v.memset(staged[:, :, D:TW], 0.0))
        V.did(v.tensor_copy(staged[:, :, 0:D], x3))
        V.after(V.last())
        m = V.did(v.tensor_copy(staged[:, :, D], deg_s[:, 0:NB]))
        m_table = write_table(x_table, staged, m)
        acc0 = cut(acc, 0, NB * D, NB, D)
        m_zero = V.did(v.memset(acc0, 0.0))

        def gcn_sums(rows_of, s_row, normed, first):
            onehot = cut(ring, 4224, 512, 4, P)
            weight, summed, added = {}, {}, {}

            def scale(c):
                V.after(normed(c), summed.get(c - 4), first)
                weight[c] = V.did(v.tensor_scalar(onehot[:, c % 4, :], iota, recd3[:, c, D_DL:D_DL + 1],
                                                  norm[:, c:c + 1], ALU.is_equal, ALU.mult))

            def product(c):
                T.after(s_row(c), weight[c], added.get(c - 4))
                summed[c] = T.did(pe.matmul(ps[c % 4][:, 0:D], onehot[:, c % 4, :], rows_of(c), start=True, stop=True))

            def add(c):
                V.after(summed[c], added.get(c - 1))
                here = acc[:, bass.ds(blk_v.at(c) * D, D)]
                added[c] = V.did(v.tensor_tensor(here, here, ps[c % 4][:, 0:D], ALU.add))

            return scale, product, add, summed, added

        RG = 16
        xg = cut(ring, 0, RG * TW, RG, TW)
        gathered = [landing(f"gathered{i}") for i in range(RG)]
        got, normed0 = {}, {}
        scale, product, add, summed, added = gcn_sums(
            lambda c: xg[:, c % RG, 0:D], lambda c: got[c], lambda c: normed0[c // 8], [m_zero, m_rec, m_weights])

        def gather_x(i):
            for c in range(8 * i, 8 * i + 8):
                G.after(summed.get(c - RG), m_table, m_rec)
                got[c] = gathered[c % RG].started(g.indirect_dma_start(
                    out=xg[:, c % RG, :], out_offset=None, in_=x_table,
                    in_offset=bass.IndirectOffsetOnAxis(ap=recd3i[:, c, D_IDX:D_IDX + 1], axis=0)))

        din_e, root = small[:, 0:16], small[:, 16:32]
        picked = cut(ring, 4224 + 512, 8 * P, 8, P)

        def edge_norm(i):
            V.after(m_rec, m_din, V.last())
            cs, at8 = range(8 * i, 8 * i + 8), slice(8 * (i % 2), 8 * (i % 2) + 8)
            for k, c in enumerate(cs):
                V.did(v.scalar_tensor_tensor(
                    out=picked[:, k, :], in0=iota, scalar=recd3[:, c, D_DL:D_DL + 1],
                    in1=acc[:, bass.ds(blk_v2.at(c) * P + 6400, P)], op0=ALU.is_equal, op1=ALU.mult))
            V.after(V.last())
            V.did(v.tensor_reduce(din_e[:, at8], picked, AX.X, ALU.add))
            V.after(V.last(), *[got[c] for c in cs])
            r0 = (8 * i) % RG
            chain(v.tensor_tensor(root[:, at8], xg[:, r0:r0 + 8, D], din_e[:, at8], ALU.mult))
            m = chain(v.tensor_scalar(root[:, at8], root[:, at8], EPS0, None, ALU.add))
            rsqrt_of(root[:, at8], m)
            normed0[i] = chain(v.tensor_tensor(norm[:, 8 * i:8 * i + 8], root[:, at8],
                                               recd3[:, 8 * i:8 * i + 8, D_W], ALU.mult))

        blk_v2 = Numbers(V, "blk_v2", blk_d_row, NB - 1)

        def eight(i):
            for c in range(8 * i, 8 * i + 8):
                scale(c)
                product(c)
                if c >= 2:
                    add(c - 2)

        pipeline(NCD // 8, (0, gather_x), (1, edge_norm), (1, eight))
        add(NCD - 2)
        add(NCD - 1)
        barrier()

        h6 = cut(big, 0, NB * D, NB, D)

        def relu_bias(view, bias):
            def finish(b, product):
                m = chain(v.tensor_tensor(view[:, b, :], product, bias, ALU.add))
                m2 = V.did(v.tensor_scalar(view[:, b, :], view[:, b, :], 0.0, None, ALU.max))
                return [m, m2]
            return finish

        linear(acc0, w6, relu_bias(h6, b6))
        m_table = write_table(h6_table, h6, V.last())
        barrier()
        m_zero = V.did(v.memset(acc0, 0.0))

        def gather_rows(table, width, index, depth, free):
            slots = cut(ring, 0, depth * width, depth, width)
            here = {}

            def stage(c):
                G.after(free(c))
                here[c] = gathered[c % depth].started(g.indirect_dma_start(
                    out=slots[:, c % depth, :], out_offset=None, in_=table,
                    in_offset=bass.IndirectOffsetOnAxis(ap=index(c), axis=0)))
            return stage, slots, here

        R2 = 12
        gather, hg, got2 = gather_rows(h6_table, D, lambda c: recd3i[:, c, D_IDX:D_IDX + 1], R2,
                                       lambda c: [m_table, summed2.get(c - R2)])
        scale, product, add, summed2, _ = gcn_sums(
            lambda c: hg[:, c % R2, :], lambda c: got2[c], lambda c: None, m_zero)
        pipeline(NCD, (0, gather), (6, scale), (6, product), (8, add))
        barrier()

        h7 = h6
        linear(acc0, w7, relu_bias(h7, b7))
        V.after(V.last())
        T.after(V.last())

        def residual_bias(bias):
            def finish(b, product):
                m = chain(v.tensor_tensor(x3[:, b, :], x3[:, b, :], product, ALU.add))
                m2 = V.did(v.tensor_tensor(x3[:, b, :], x3[:, b, :], bias, ALU.add))
                return [m, m2]
            return finish

        linear(h7, wp, residual_bias(bp))
        layernorm()
        barrier()

        recs3 = cut(big, 0, NCS * RS, NCS, RS)
        m_recs = rec_in.started(sp.dma_start(big[:, 0:NCS * RS], rec_s_dram.rearrange("(p c) r -> p (c r)", p=P)))
        w1 = wts[0:MUL, 0:2 * MUL]
        wsc = wts[0:MUL, 128:128 + 2 * MUL]
        w2 = wts[:, 256:256 + 2 * MUL]
        fc1 = cut(wts, 384, 512, 4, P)
        fc2 = wts[:, 896:896 + P]
        fc3 = wts[:, 1024:1024 + D]
        gain_s, gain_v = wts[:, 1280:1280 + MUL], wts[:, 1344:1344 + MUL]
        m = V.did(v.memset(wts[:, 384:1024], 0.0))
        S.after(m)
        load(w1[:, 0:MUL], t["L1_gnn_w1_s"])
        load(w1[:, MUL:2 * MUL], t["L1_gnn_w1_v"])
        load(wsc[:, 0:MUL], t["L1_gnn_wsc_s"])
        load(wsc[:, MUL:2 * MUL], t["L1_gnn_wsc_v"])
        load(w2[:, 0:MUL], t["L1_gnn_w2_s"])
        load(w2[:, MUL:2 * MUL], t["L1_gnn_w2_v"])
        for k in range(8):
            load(fc1[k * RS + S_EA:k * RS + S_EA + 8, k // 2, (k % 2) * MUL:(k % 2) * MUL + MUL], t["L1_gnn_fc_w1"])
        for k in range(2):
            load(fc2[k * MUL:(k + 1) * MUL, k * MUL:(k + 1) * MUL], t["L1_gnn_fc_w2"])
            load(fc3[k * MUL:(k + 1) * MUL, :], t["L1_gnn_fc_w3"])
        load(gain_s, everywhere("L1_gnn_g_s", MUL))
        m_weights = load(gain_v, everywhere("L1_gnn_g_v", MUL))
        V.after(m_weights, m_recs)
        T.after(m_weights, m_recs)
        chain(v.tensor_scalar(fc3, fc3, 0.125, None, ALU.mult))
        V.did(v.tensor_copy(idx_s, recs3.bitcast(I32)[:, :, S_IDX]))
        m_idx = V.did(v.tensor_copy(sl_s, recs3[:, :, S_SL]))
        T.after(m_idx)

        acc1 = cut(acc, 0, NB * 512, NB, 512)

        def vector_parts(bank, b):
            for q in range(4):
                part = x3[:, b, 0:MUL] if q == 0 else x3[:, b, MUL + q - 1:4 * MUL:3]
                ins = pe.transpose(bank[0:MUL, q * P:(q + 1) * P], part, ident)
            return T.did(ins)

        def parts_product(bank, at0, turned, weights):
            for q in range(4):
                w = weights[:, 0:MUL] if q == 0 else weights[:, MUL:2 * MUL]
                ins = pe.matmul(bank[:, at0 + q * MUL:at0 + (q + 1) * MUL], turned[0:MUL, q * P:(q + 1) * P], w,
                                start=True, stop=True)
            return T.did(ins)

        turned1 = cut(ring, 0, 1024, 2, 512)
        tn, kp, pr, fi = {}, {}, {}, {}

        def y_turn(b):
            T.after(kp.get(b - 2))
            tn[b] = vector_parts(ps[b % 2], b)

        def y_keep(b):
            A.after(tn[b], pr.get(b - 2))
            kp[b] = A.did(a.copy(turned1[0:MUL, b % 2, :], ps[b % 2][0:MUL, :]))

        def y_product(b):
            T.after(kp[b], fi.get(b - 2))
            pr[b] = parts_product(ps[2 + b % 2], 0, turned1[:, b % 2, :], w1)

        def y_end(b):
            V.after(pr[b])
            fi[b] = V.did(v.tensor_scalar(acc1[:, b, 0:D], ps[2 + b % 2][:, 0:D], 0.125, None, ALU.mult))

        pipeline(NB, (0, y_turn), (0, y_keep), (1, y_product), (2, y_end))
        m_table = write_table(y_table, acc1[:, :, 0:D], V.last())
        barrier()
        m_zero = V.did(v.memset(acc, 0.0))

        RY = 7
        gather, yg, got_y = gather_rows(y_table, D, lambda c: idx_s[:, c:c + 1], RY,
                                        lambda c: [m_table, m_idx, mixed.get(c - RY)])
        o = RY * D
        mid = cut(ring, o, 1024, 2, 512)
        o += 1024
        rec_t = cut(ring, o, 256, 2, P)
        o += 256
        h1 = cut(ring, o, 1024, 2, 512)
        o += 1024
        h2 = cut(ring, o, 1024, 2, 512)
        o += 1024
        dot3 = cut(ring, o, 192, 3, MUL)
        o += 192
        dot1, wb = ring[:, o:o + MUL], ring[:, o + MUL:o + 2 * MUL]
        o += 2 * MUL
        oh1 = cut(ring, o, 2 * P, 2, P)
        assert o + 2 * P <= ring.shape[1]
        c_rt, c_rk, c_1, c_s1, c_2, c_s2 = {}, {}, {}, {}, {}, {}
        w_ready, mixed, mids, oh_at, sum1, added1 = {}, {}, {}, {}, {}, {}
        blk_s = Numbers(V, "blk_s", blk_s_row, NB - 1)

        def mlp_in(i):
            T.after(c_rk.get(i - 1))
            c_rt[i] = T.did(pe.transpose(ps[0][:, 0:P], big[:, i * P:(i + 1) * P], ident))
            A.after(c_rt[i], c_1.get(i - 2))
            c_rk[i] = A.did(a.copy(rec_t[:, i % 2, :], ps[0][:, 0:P]))

        def mlp_1(i):
            T.after(c_rk[i], c_s1.get(i - 1))
            for j in range(4):
                ins = pe.matmul(ps[1][:, j * P:(j + 1) * P], fc1[:, j, :], rec_t[:, i % 2, :], start=True, stop=True)
            c_1[i] = T.did(ins)
            A.after(c_1[i], c_2.get(i - 2))
            c_s1[i] = A.did(a.activation(h1[:, i % 2, :], ps[1], ACT.Silu, scale=float(1.0 / np.sqrt(8.0))))

        def mlp_2(i):
            T.after(c_s1[i], c_s2.get(i - 1))
            c_2[i] = T.did(pe.matmul(ps[2], fc2, h1[:, i % 2, :], start=True, stop=True))
            A.after(c_2[i], w_ready.get(8 * (i - 2) + 7))
            c_s2[i] = A.did(a.activation(h2[:, i % 2, :], ps[2], ACT.Silu, scale=0.125))

        def edge_weights(c):
            i, k = c // 8, c % 8
            half = slice((k % 2) * MUL, (k % 2) * MUL + MUL)
            T.after(c_s2[i], mixed.get(c - 3))
            w_ready[c] = T.did(pe.matmul(ps[3 + c % 3][:, 0:D], h2[half, i % 2, (k // 2) * P:(k // 2) * P + P],
                                         fc3[half, :], start=True, stop=True))

        def messages(c):
            w, y = ps[3 + c % 3], yg[:, c % RY, :]
            es, ev = y[:, 0:MUL], y[:, MUL:4 * MUL].rearrange("p (d u) -> p d u", d=3)
            sh0, sh1 = recs3[:, c, S_SH:S_SH + 1], recs3[:, c, S_SH + 1:S_SH + 4]
            m4 = mid[:, c % 2, :].rearrange("p (q u) -> p q u", q=4)
            V.after(got_y[c])
            V.after(mids.get(c - 1))
            t1 = V.did(v.tensor_tensor(dot3, ev, lanes(sh1, 3, MUL), ALU.mult))
            V.after(sum1.get(c - 2))
            oh_at[c] = V.did(v.tensor_scalar(oh1[:, c % 2, :], iota, sl_s[:, c:c + 1], None, ALU.is_equal))
            V.after(w_ready[c])
            t2 = V.did(v.tensor_tensor(wb, w[:, MUL:2 * MUL], es, ALU.mult))
            V.after(t1)
            t3 = V.did(v.tensor_reduce(dot1, dot3.rearrange("p d u -> p u d"), AX.X, ALU.add))
            V.did(v.scalar_tensor_tensor(out=m4[:, 0, 0:MUL], in0=w[:, 0:MUL], scalar=sh0, in1=es,
                                         op0=ALU.mult, op1=ALU.mult))
            V.did(v.scalar_tensor_tensor(out=m4[:, 1:4, MUL:P], in0=rows(w[:, 2 * MUL:3 * MUL], 3, MUL), scalar=sh0,
                                         in1=ev, op0=ALU.mult, op1=ALU.mult))
            V.after(t2)
            V.did(v.tensor_tensor(m4[:, 1:4, 0:MUL], rows(wb, 3, MUL), lanes(sh1, 3, MUL), ALU.mult))
            V.after(t3)
            mids[c] = mixed[c] = V.did(v.scalar_tensor_tensor(
                out=m4[:, 0, MUL:P], in0=w[:, 3 * MUL:4 * MUL], scalar=0.5773502691896258, in1=dot1,
                op0=ALU.mult, op1=ALU.mult))

        def sums(c):
            u = c // GS
            T.after(mids[c], oh_at[c], added1.get(u - 2) if c % GS == 0 else None)
            sum1[c] = T.did(pe.matmul(ps[6 + u % 2], oh1[:, c % 2, :], mid[:, c % 2, :], start=(c % GS == 0),
                                      stop=(c % GS == GS - 1)))

        def add_unit(c):
            if c % GS == GS - 1:
                u = c // GS
                V.after(sum1[c], added1.get(u - 1), m_zero)
                here = acc[:, bass.ds(blk_s.at(u) * 512, 512)]
                added1[u] = V.did(v.tensor_tensor(here, here, ps[6 + u % 2], ALU.add))

        def every8(stage, k):
            return lambda c: stage(c // 8) if c % 8 == k else None

        pipeline(NCS, (0, every8(mlp_in, 0)), (2, every8(mlp_1, 0)), (4, every8(mlp_2, 0)), (3, gather),
                 (7, edge_weights), (8, messages), (9, sums), (10, add_unit))
        barrier()

        o1 = cut(big, 0, NB * D, NB, D)
        dn = small[:, 0:NB]
        chain(v.tensor_scalar(dn, deg_s[:, NB:2 * NB], 1.0, None, ALU.max))
        rsqrt_of(dn, V.last())
        chain(v.tensor_scalar(dn, dn, float(1.0 / np.sqrt(2.0 * MUL)), None, ALU.mult))
        sq, ss = cut(ring, 2100, D, D), cut(small, 50, 2 * NB, 2, NB)
        turned_a, turned_x = cut(ring, 0, 1024, 2, 512), cut(ring, 1024, 1024, 2, 512)
        tn, kp, pr, fi = {}, {}, {}, {}

        def o_turn(b):
            T.after(kp.get(b - 1))
            for q in range(4):
                pe.transpose(ps[0][:, q * P:(q + 1) * P], acc1[:, b, q * P:(q + 1) * P], ident)
            tn[b] = vector_parts(ps[1], b)

        def o_keep(b):
            A.after(tn[b], pr.get(b - 2))
            A.did(a.copy(turned_a[:, b % 2, :], ps[0]))
            kp[b] = A.did(a.copy(turned_x[0:MUL, b % 2, :], ps[1][0:MUL, :]))

        def o_product(b):
            T.after(kp[b], fi.get(b - 2))
            for q in range(4):
                pe.matmul(ps[2 + b % 2][:, q * MUL:(q + 1) * MUL], turned_a[:, b % 2, q * P:(q + 1) * P],
                          w2[:, 0:MUL] if q == 0 else w2[:, MUL:2 * MUL], start=True, stop=True)
            pr[b] = parts_product(ps[2 + b % 2], D, turned_x[:, b % 2, :], wsc)

        def o_end(b):
            V.after(pr[b])
            m = V.did(v.tensor_scalar(o1[:, b, :], ps[2 + b % 2][:, 0:D], dn[:, b:b + 1], None, ALU.mult))
            V.after(m)
            fi[b] = V.did(v.scalar_tensor_tensor(out=o1[:, b, :], in0=ps[2 + b % 2][:, D:2 * D], scalar=0.125,
                                                 in1=o1[:, b, :], op0=ALU.mult, op1=ALU.add))
            A.after(fi[b], A.last())
            m = A.did(a.activation(sq[:, 0:MUL], o1[:, b, 0:MUL], ACT.Square, accum_out=ss[:, 0, b:b + 1]))
            A.after(m)
            A.did(a.activation(sq[:, MUL:D], o1[:, b, MUL:D], ACT.Square, accum_out=ss[:, 1, b:b + 1]))

        pipeline(NB, (0, o_turn), (0, o_keep), (1, o_product), (2, o_end))
        V.after(A.last(), V.last())
        chain(v.tensor_scalar(ss[:, 0, :], ss[:, 0, :], 1.0 / MUL, EPS1, ALU.mult, ALU.add))
        chain(v.tensor_scalar(ss[:, 1, :], ss[:, 1, :], 1.0 / (3 * MUL), EPS1, ALU.mult, ALU.add))
        rsqrt_of(small[:, 50:50 + 2 * NB], V.last())
        for b in range(NB):
            ov = o1[:, b, MUL:D].rearrange("p (d u) -> p d u", d=3)
            xv = x3[:, b, MUL:D].rearrange("p (u d) -> p d u", d=3)
            V.did(v.scalar_tensor_tensor(out=o1[:, b, 0:MUL], in0=o1[:, b, 0:MUL], scalar=ss[:, 0, b:b + 1],
                                         in1=gain_s, op0=ALU.mult, op1=ALU.mult))
            m = V.did(v.scalar_tensor_tensor(out=ov, in0=ov, scalar=ss[:, 1, b:b + 1], in1=rows(gain_v, 3, MUL),
                                             op0=ALU.mult, op1=ALU.mult))
            V.after(m)
            V.did(v.tensor_tensor(x3[:, b, 0:MUL], x3[:, b, 0:MUL], o1[:, b, 0:MUL], ALU.add))
            V.did(v.tensor_tensor(xv, xv, ov, ALU.add))
        layernorm()
        barrier()

        alpha = cut(big, 0, NCD * H, NCD, H)
        h_at = NCD * H
        hdst = cut(big, h_at, NB * TW, NB, TW)
        hsrc = cut(acc, 0, NB * TW, NB, TW)
        wexp = cut(acc, NB * TW, 16 * D, 16, D)
        w_att, w_att_t = cut(wts, 0, 512, 2, D), cut(wts, 512, 512, 2, D)
        a_src, a_dst, bias = wts[:, 1024:1280], wts[:, 1280:1536], wts[:, 1536:1792]
        top, top_t = small[:, 0:2 * NBD], small[:, 2 * NBD:4 * NBD]
        m_z = V.did(v.memset(wexp, 0.0))
        load(w_att, two("L2_gnn_W"))
        load(a_src, t["L2_gnn_a_src"].rearrange("(o h) d -> o (h d)", o=1).to_broadcast([P, D]))
        load(a_dst, t["L2_gnn_a_dst"].rearrange("(o h) d -> o (h d)", o=1).to_broadcast([P, D]))
        m_weights = load(bias, everywhere("L2_gnn_bias", D))
        ew_out = landing("ew_out")
        with nc.allow_non_contiguous_dma("the transposed edge weights, once"):
            ew_out.started(sp.dma_start(ew_dram[0:3, :], t["L2_gnn_edge_W"].rearrange("n f -> f n")))
        m = ew_out.started(sp.dma_start(ew_dram[3:4, :], t["L2_gnn_edge_b"].rearrange("(o n) -> o n", o=1)))
        S.after(m, m_z)
        for k in range(16):
            m_wexp = load(wexp[k * RD + D_EA:k * RD + D_EA + 4, k, :], ew_dram)
        T.after(m_weights)
        V.after(m_weights, m_wexp)
        for ki in range(2):
            for ko in range(2):
                ins = pe.transpose(ps[4 + ki][:, ko * P:(ko + 1) * P], w_att[:, ko, ki * P:(ki + 1) * P], ident)
        V.after(T.did(ins))
        for ki in range(2):
            m = V.did(v.tensor_copy(w_att_t[:, ki, :], ps[4 + ki][:, 0:D]))
        T.after(m)
        logit = ring[:, 2048:2048 + D]

        def attention_tables(b, product):
            V.did(v.tensor_copy(hsrc[:, b, 0:D], product))
            m = V.did(v.tensor_copy(hdst[:, b, 0:D], product))
            for a_vec, where in ((a_src, hsrc), (a_dst, hdst)):
                chain(v.tensor_tensor(logit, product, a_vec, ALU.mult))
                chain(v.tensor_reduce(where[:, b, D:TW], logit.rearrange("p (h d) -> p h d", h=H), AX.X, ALU.add))
            return V.last()

        linear(x3, w_att_t, attention_tables)
        m_table = write_table(att_table, hsrc, V.last())
        m_top = V.did(v.memset(top, -BIG))
        T.after(m_wexp, V.last())

        R3 = 8
        gather, ag, got_a = gather_rows(att_table, TW, lambda c: recd3i[:, c, D_IDX:D_IDX + 1], R3,
                                        lambda c: [m_table, spilled.get(c - R3), logits.get(c - R3)])
        o = R3 * TW
        oh2 = cut(ring, o, 3 * P, 3, P)
        oh2_t = cut(ring, o + 3 * P, 3 * P, 3, P)
        o += 6 * P
        rec_t2 = cut(ring, o, 2 * P, 2, P)
        o += 2 * P
        enc = cut(ring, o, 2 * D, 2, D)
        o += 2 * D
        prod2, spread = ring[:, o:o + D], cut(ring, o + D, 2 * D, 2, D)
        o += 3 * D
        miss = ring[:, o:o + SUB]
        red, lg = ring[:, o + 32:o + 40], ring[:, o + 40:o + 48]
        mx = cut(ring, o + 48, 4, 2, 2)
        assert o + 60 <= ring.shape[1]
        spill = [landing(f"spill{i}") for i in range(R3)]
        spilled, logits, ohd, oht, ohk, rt2, rk2 = {}, {}, {}, {}, {}, {}, {}
        hd_at, enc_at, enc_ok, masked, mtop, maxed = {}, {}, {}, {}, {}, {}

        def spill_rows(c):
            S.after(got_a[c])
            spilled[c] = spill[c % R3].started(sp.dma_start(rows_spill[c], ag[:, c % R3, 0:D]))

        def one_hot(c, turned_read):
            V.after(oht.get(c - 3), *turned_read(c - 3))
            ohd[c] = V.did(v.tensor_scalar(oh2[:, c % 3, :], iota, recd3[:, c, D_DL:D_DL + 1], None, ALU.is_equal))
            T.after(ohd[c], ohk.get(c - 1))
            oht[c] = T.did(pe.transpose(ps[1][:, 0:P], oh2[:, c % 3, :], ident))
            A.after(oht[c], *turned_read(c - 3))
            ohk[c] = A.did(a.copy(oh2_t[:, c % 3, :], ps[1][:, 0:P]))

        def turn_records(c):
            if c % 16 == 0:
                i = c // 16
                T.after(rk2.get(i - 1))
                rt2[i] = T.did(pe.transpose(ps[0][:, 0:P], rec_d[:, i * P:(i + 1) * P], ident))
                A.after(rt2[i], enc_at.get(16 * (i - 1) - 1))
                rk2[i] = A.did(a.copy(rec_t2[:, i % 2, :], ps[0][:, 0:P]))

        def node_and_edge_parts(c):
            T.after(rk2[c // 16], enc_ok.get(c - 2))
            enc_at[c] = T.did(pe.matmul(ps[4 + c % 2][:, 0:D], rec_t2[:, (c // 16) % 2, :], wexp[:, c % 16, :],
                                        start=True, stop=True))
            A.after(enc_at[c], logits.get(c - 2))
            enc_ok[c] = A.did(a.activation(enc[:, c % 2, :], ps[4 + c % 2][:, 0:D], ACT.Relu))
            T.after(ohk[c], logits.get(c - 2))
            hd_at[c] = T.did(pe.matmul(ps[2 + c % 2][:, 0:TW], oh2_t[:, c % 3, :],
                                       big[:, bass.ds(blk_t.at(c) * TW + h_at, TW)], start=True, stop=True))

        def edge_logits(c):
            hd = ps[2 + c % 2]
            V.after(hd_at[c], enc_ok[c], got_a[c], V.last())
            chain(v.tensor_tensor(prod2, hd[:, 0:D], enc[:, c % 2, :], ALU.mult))
            V.did(v.tensor_scalar(miss, iota[:, 0:SUB], recd3[:, c, D_DL32:D_DL32 + 1], -BIG,
                                  ALU.not_equal, ALU.mult))
            chain(v.tensor_tensor(lg, hd[:, D:TW], ag[:, c % R3, D:TW], ALU.add))
            chain(v.tensor_reduce(red, prod2.rearrange("p (h d) -> p h d", h=H), AX.X, ALU.add))
            chain(v.tensor_tensor(lg, lg, red, ALU.add))
            logits[c] = chain(v.scalar_tensor_tensor(out=alpha[:, c, :], in0=lg, scalar=0.2, in1=lg,
                                                     op0=ALU.mult, op1=ALU.max))
            V.after(mtop.get(c - 2))
            masked[c] = V.did(v.tensor_tensor(spread[:, c % 2, :].rearrange("p (h n) -> p h n", h=H),
                                              lanes(alpha[:, c, :], H, SUB), rows(miss, H, SUB), ALU.add))

        def turn_masked(c):
            T.after(masked[c], maxed.get(c - 2))
            for k in range(2):
                ins = pe.transpose(ps[6 + c % 2][:, k * P:(k + 1) * P], spread[:, c % 2, k * P:(k + 1) * P], ident)
            mtop[c] = T.did(ins)

        def node_max(c):
            V.after(mtop[c], m_top)
            maxed[c] = V.did(v.tensor_reduce(mx[:, c % 2, :], ps[6 + c % 2][:, 0:D].rearrange("p (k e) -> p k e", k=2),
                                             AX.X, ALU.max))
            V.after(maxed[c])
            here = small[:, bass.ds(b32_v.at(c) * 2, 2)]
            chain(v.tensor_tensor(here, here, mx[:, c % 2, :], ALU.max))

        pipeline(NCD, (0, gather), (3, spill_rows), (4, turn_records), (4, lambda c: one_hot(c, lambda k: [hd_at.get(k)])),
                 (5, node_and_edge_parts), (6, edge_logits), (7, turn_masked), (8, node_max))
        barrier()

        top4 = top.rearrange("p (b s k) -> p b s k", s=4, k=2)
        top_t4 = top_t.rearrange("p (b k q) -> p b k q", k=2, q=4)
        for q in range(4):
            for s in range(4):
                V.did(v.tensor_copy(top_t4[s * SUB:(s + 1) * SUB, :, :, q], top4[q * SUB:(q + 1) * SUB, :, s, :]))
        m_top = V.last()
        m_zero = V.did(v.memset(hsrc, 0.0))
        RB = 6
        hs = cut(ring, 0, RB * D, RB, D)
        o = RB * D
        oh2 = cut(ring, o, 3 * P, 3, P)
        oh2_t = cut(ring, o + 3 * P, 3 * P, 3, P)
        o += 6 * P
        msg = cut(ring, o, 3 * TW, 3, TW)
        o += 3 * TW
        below = cut(ring, o, 2 * H, 2, H)
        back = {}
        ohd.clear(), oht.clear(), ohk.clear()
        tops, lows, exps, msgs, sum2, added2 = {}, {}, {}, {}, {}, {}
        blk_v.first = blk_t.first = None

        def read_rows(c):
            S.after(msgs.get(c - RB))
            back[c] = spill[c % R3].started(sp.dma_start(hs[:, c % RB, :], rows_spill[c]))

        def chunk_tops(c):
            T.after(ohk[c], lows.get(c - 2), m_top)
            tops[c] = T.did(pe.matmul(ps[2 + c % 2][:, 0:H], oh2_t[:, c % 3, :],
                                      small[:, bass.ds(blk_t.at(c) * H + 2 * NBD, H)], start=True, stop=True))

        def exponents(c):
            V.after(tops[c], exps.get(c - 2))
            lows[c] = V.did(v.tensor_tensor(below[:, c % 2, :], alpha[:, c, :], ps[2 + c % 2][:, 0:H], ALU.subtract))
            V.after(lows[c])
            m = V.did(v.tensor_scalar(below[:, c % 2, :], below[:, c % 2, :], 0.0, None, ALU.min))
            A.after(m, sum2.get(c - 3))
            exps[c] = A.did(a.activation(msg[:, c % 3, D:TW], below[:, c % 2, :], ACT.Exp))

        def weighted(c):
            V.after(exps[c], back[c], sum2.get(c - 3))
            msgs[c] = V.did(v.tensor_tensor(msg[:, c % 3, 0:D].rearrange("p (h d) -> p h d", h=H),
                                            hs[:, c % RB, :].rearrange("p (h d) -> p h d", h=H),
                                            lanes(msg[:, c % 3, D:TW], H, HD), ALU.mult))

        def sum_messages(c):
            T.after(msgs[c], added2.get(c - 2))
            sum2[c] = T.did(pe.matmul(ps[4 + c % 2][:, 0:TW], oh3[:, c % 8, :], msg[:, c % 3, :], start=True, stop=True))

        oh3 = cut(ring, o + 2 * H, 8 * P, 8, P)
        assert o + 2 * H + 8 * P <= ring.shape[1]

        def one_hot_b(c):
            V.after(sum2.get(c - 8))
            ohd[c] = V.did(v.tensor_scalar(oh3[:, c % 8, :], iota, recd3[:, c, D_DL:D_DL + 1], None, ALU.is_equal))
            T.after(ohd[c], ohk.get(c - 1))
            oht[c] = T.did(pe.transpose(ps[1][:, 0:P], oh3[:, c % 8, :], ident))
            A.after(oht[c], tops.get(c - 3))
            ohk[c] = A.did(a.copy(oh2_t[:, c % 3, :], ps[1][:, 0:P]))

        def add_messages(c):
            V.after(sum2[c], added2.get(c - 1), m_zero)
            here = acc[:, bass.ds(blk_v.at(c) * TW, TW)]
            added2[c] = V.did(v.tensor_tensor(here, here, ps[4 + c % 2][:, 0:TW], ALU.add))

        pipeline(NCD, (0, read_rows), (1, one_hot_b), (2, chunk_tops), (3, exponents), (4, weighted),
                 (5, sum_messages), (6, add_messages))
        V.after(V.last())
        den = ring[:, 0:NB * H].rearrange("p (b h) -> p b h", h=H)
        barrier()
        chain(v.tensor_scalar(den, hsrc[:, :, D:TW], 1e-10, None, ALU.max))
        chain(v.reciprocal(den, den))
        for b in range(NB):
            o2 = hsrc[:, b, 0:D]
            m = V.did(v.tensor_tensor(o2.rearrange("p (h d) -> p h d", h=H), o2.rearrange("p (h d) -> p h d", h=H),
                                      lanes(den[:, b, :], H, HD), ALU.mult))
            V.did(v.tensor_tensor(x3[:, b, :], x3[:, b, :], bias, ALU.add))
            V.after(V.last())
            V.did(v.tensor_tensor(x3[:, b, :], x3[:, b, :], o2, ALU.add))
        layernorm()
        barrier()

        w3, b3 = cut(wts, 0, 512, 2, D), wts[:, 512:512 + D]
        load(w3, two("L3_gnn_W"))
        m_weights = load(b3, everywhere("L3_gnn_b", D))
        dinv = small[:, 0:NB]
        scaled = cut(big, 0, NB * D, NB, D)
        chain(v.tensor_scalar(dinv, deg_d[:, NB:2 * NB], 1.0, None, ALU.add))
        rsqrt_of(dinv, V.last())
        T.after(m_weights)
        V.after(m_weights)

        def scale_rows(b, product):
            chain(v.tensor_tensor(scaled[:, b, :], product, b3, ALU.add))
            return chain(v.tensor_scalar(scaled[:, b, :], scaled[:, b, :], dinv[:, b:b + 1], None, ALU.mult))

        linear(x3, w3, scale_rows)
        m_table = write_table(scaled_table, scaled, V.last())
        m_zero = V.did(v.memset(acc0, 0.0))
        R4 = 12
        gather, sg, got4 = gather_rows(scaled_table, D, lambda c: idx_s[:, c:c + 1], R4,
                                       lambda c: [m_table, sum4.get(c - R4)])
        oh4 = cut(ring, R4 * D, 4 * P, 4, P)
        sum4, oh4_at, added4 = {}, {}, {}
        blk_s.first = None

        def one_hot4(c):
            V.after(sum4.get(c - 4))
            oh4_at[c] = V.did(v.tensor_scalar(oh4[:, c % 4, :], iota, sl_s[:, c:c + 1], None, ALU.is_equal))

        def sums4(c):
            u = c // GS
            T.after(oh4_at[c], got4[c], added4.get(u - 4) if c % GS == 0 else None)
            sum4[c] = T.did(pe.matmul(ps[4 + u % 4][:, 0:D], oh4[:, c % 4, :], sg[:, c % R4, :],
                                      start=(c % GS == 0), stop=(c % GS == GS - 1)))

        def add4(c):
            if c % GS == GS - 1:
                u = c // GS
                V.after(sum4[c], added4.get(u - 1), m_zero)
                here = acc[:, bass.ds(blk_s.at(u) * D, D)]
                added4[u] = V.did(v.tensor_tensor(here, here, ps[4 + u % 4][:, 0:D], ALU.add))

        barrier()
        pipeline(NCS, (0, gather), (5, one_hot4), (6, sums4), (8, add4))
        barrier()
        for b in range(NB):
            m = V.did(v.tensor_tensor(acc0[:, b, :], acc0[:, b, :], scaled[:, b, :], ALU.add))
            V.after(m)
            V.did(v.scalar_tensor_tensor(out=x3[:, b, :], in0=acc0[:, b, :], scalar=dinv[:, b:b + 1],
                                         in1=x3[:, b, :], op0=ALU.mult, op1=ALU.add))
        m = layernorm()
        S.after(m)
        stored = landing("stored")
        stored.started(sp.dma_start(out[0:(NB - 1) * P, :].rearrange("(b p) k -> p b k", p=P), x3[:, 0:NB - 1, :]))
        S.after(stored.started(sp.dma_start(out[(NB - 1) * P:N, :], x3[0:LAST, NB - 1, :])))
        barrier()


_INS = ['x', 'src', 'dst', 'edge_attr_3', 'edge_attr_4', 'edge_attr_8', 'edge_weight', 'L0_gnn_W6', 'L0_gnn_b6',
        'L0_gnn_W7', 'L0_gnn_b7', 'L0_gnn_Wp', 'L0_gnn_bp', 'L1_gnn_w1_s', 'L1_gnn_w1_v', 'L1_gnn_wsc_s',
        'L1_gnn_wsc_v', 'L1_gnn_w2_s', 'L1_gnn_w2_v', 'L1_gnn_fc_w1', 'L1_gnn_fc_w2', 'L1_gnn_fc_w3', 'L1_gnn_g_s',
        'L1_gnn_g_v', 'L2_gnn_W', 'L2_gnn_a_src', 'L2_gnn_a_dst', 'L2_gnn_edge_W', 'L2_gnn_edge_b', 'L2_gnn_bias',
        'L3_gnn_W', 'L3_gnn_b']


def kernel(**inputs):
    import concourse.bacc as bacc
    from concourse.bass_utils import run_bass_kernel_spmd

    nc = bacc.Bacc("TRN2", target_bir_lowering=False, num_devices=1)
    arrays, tensors = {}, {}
    for name in _INS:
        arr = np.ascontiguousarray(inputs[name])
        arrays[f"in_{name}"] = arr
        tensors[name] = nc.dram_tensor(f"in_{name}", arr.shape, mybir.dt.from_np(arr.dtype), kind="ExternalInput").ap()
    result = nc.dram_tensor("result", (N, D), F32, kind="ExternalOutput").ap()
    program(nc, tensors, result)
    r = run_bass_kernel_spmd(nc, [arrays], core_ids=[0])
    return r.results[0]["result"]
```

```python
from contextlib import ExitStack

import numpy as np
import concourse.bass as bass
from concourse import mybir

F32, I32 = mybir.dt.float32, mybir.dt.int32
ALU, ACT, AX = mybir.AluOpType, mybir.ActivationFunctionType, mybir.AxisListType

P = 128
N, E, D = 3125, 100000, 256
NB = -(-N // P)
NPAD = NB * P
LAST = N - (NB - 1) * P
EP = 125
EJ = E // EP
SUB = 32
NBD = NPAD // SUB
H, HD = 8, 32
MUL = 64


def up(n, m):
    return -(-n // m) * m


NCD = up((E + (P - 1) * -(-N // SUB)) // P, 16)
GS = 2
NUS = up((E + (GS * P - 1) * NB) // (GS * P), 16)
NCS = NUS * GS
RD, RS = 8, 16
D_IDX, D_DL, D_W, D_EA, D_ONE, D_DL32 = 0, 1, 2, 3, 6, 7
S_IDX, S_SL, S_SH, S_EA = 0, 1, 2, 6
TW = D + H
BIG = float(2.0 ** 100)
EPS0, EPS1 = 1e-12, 1e-5


class Queue:

    def __init__(self, eng, sem):
        self.eng, self.sem, self.count, self.waited = eng, sem, 0, {}

    def after(self, *marks):
        for m in marks:
            if m is None:
                continue
            if isinstance(m, list):
                self.after(*m)
                continue
            sem, value = m
            if self.waited.get(id(sem), 0) < value:
                self.eng.wait_ge(sem, value)
                self.waited[id(sem)] = value

    def did(self, ins):
        ins.then_inc(self.sem, 1)
        self.count += 1
        return self.sem, self.count

    def last(self):
        return (self.sem, self.count) if self.count else None


class Marks(dict):

    def get(self, i):
        return None if i < 0 else self[i]


class Landing:

    def __init__(self, sem):
        self.sem, self.count = sem, 0

    def started(self, ins):
        ins.then_inc(self.sem, 16)
        self.count += 16
        return self.sem, self.count


def pipeline(n, *stages):
    for i in range(n + max(lag for lag, _ in stages)):
        for lag, f in stages:
            if 0 <= i - lag < n:
                f(i - lag)


def program(nc, t, out):
    with ExitStack() as ctx:
        def sem(name):
            return ctx.enter_context(nc.semaphore(name))

        V, A = Queue(nc.vector, sem("vector_done")), Queue(nc.scalar, sem("scalar_done"))
        T, G = Queue(nc.tensor, sem("tensor_done")), Queue(nc.gpsimd, sem("pool_done"))
        S = Queue(nc.sync, sem("sync_done"))
        v, a, pe, g, sp = V.eng, A.eng, T.eng, G.eng, S.eng
        landings = []

        def landing(name):
            landings.append(Landing(sem(name)))
            return landings[-1]

        def barrier():
            marks = [q.last() for q in (V, A, T, G)] + [(x.sem, x.count) for x in landings if x.count]
            for q in (V, A, T, G, S):
                q.after(*marks)

        def dram(name, shape, dt=F32):
            return nc.dram_tensor(name, shape, dt, kind="Internal").ap()

        def sb(name, width, dt=F32, parts=P):
            return ctx.enter_context(nc.sbuf_tensor(name, [parts, width], dt))[:, :]

        ps = [ctx.enter_context(nc.psum_tensor(f"bank{i}", [P, 512], F32))[:, :] for i in range(8)]

        rec_d_dram, rec_s_dram = dram("rec_d", (P * NCD, RD)), dram("rec_s", (P * NCS, RS))
        x_table, h6_table = dram("x_table", (NPAD, TW)), dram("h6_table", (NPAD, D))
        y_table, att_table = dram("y_table", (NPAD, D)), dram("att_table", (NPAD, TW))
        scaled_table = dram("scaled_table", (NPAD, D))
        rows_spill = dram("rows_spill", (NCD, P, D))
        din_dram = dram("din_dram", (NB, P))
        ew_dram = dram("ew_dram", (4, D))
        JD, JS = up(NCD, P) // P, up(NUS, P) // P
        b32_dram, blk_d_dram = dram("b32_dram", (P, JD), I32), dram("blk_d_dram", (P, JD), I32)
        blk_s_dram = dram("blk_s_dram", (P, JS), I32)

        ident, iota = sb("ident", P), sb("iota", P)
        lane = sb("lane", 1)
        rec_d = sb("rec_d_sb", NCD * RD)
        big = sb("big", max(NCS * RS, NCD * H + NB * TW))
        acc = sb("acc", NB * 512)
        x = sb("x_res", NB * D)
        norm = sb("norm", NCD)
        idx_s, sl_s = sb("idx_s", NCS, I32), sb("sl_s", NCS)
        deg_d, deg_s = sb("deg_d", 2 * NB), sb("deg_s", 2 * NB)
        unit_numbers = sb("unit_numbers", P * JD, I32, 3)
        b32_row, blk_d_row, blk_s_row = (unit_numbers[k:k + 1, :] for k in range(3))
        ring = sb("ring", 6100)
        wts = sb("wts", 2432)
        small = sb("small", 800)

        x3 = x.rearrange("p (b k) -> p b k", b=NB)
        recd3 = rec_d.rearrange("p (c r) -> p c r", r=RD)
        recd3i = rec_d.bitcast(I32).rearrange("p (c r) -> p c r", r=RD)

        def cut(buf, at, n, *dims):
            r = buf[:, at:at + n]
            if len(dims) == 2:
                r = r.rearrange("p (a b) -> p a b", a=dims[0])
            if len(dims) == 3:
                r = r.rearrange("p (a b c) -> p a b c", a=dims[0], b=dims[1])
            return r

        def lanes(col, n, k):
            return col.rearrange("p (n o) -> p n o", o=1).to_broadcast([col.shape[0], n, k])

        def rows(row, n, k):
            return row.rearrange("p (o k) -> p o k", o=1).to_broadcast([row.shape[0], n, k])

        class Numbers:
            def __init__(self, q, name, row, top):
                self.q, self.row, self.top = q, row, top
                self.regs = [q.eng.alloc_register(f"{name}{i}") for i in range(16)]
                self.first = None

            def at(self, i):
                if self.first != i // 16:
                    self.first = i // 16
                    self.q.eng.load(self.regs, self.row[0:1, self.first * 16:self.first * 16 + 16])
                return self.q.eng.snap(self.regs[i % 16], min_val=0, max_val=self.top)

        load_in, prefilled = landing("load_in"), landing("prefilled")
        s_w = landing("weights_in")

        m_iota = G.did(g.iota(iota, [[1, P]], base=0, channel_multiplier=0, allow_small_or_imprecise_dtypes=True))
        m_lane = G.did(g.iota(lane, [[0, 1]], base=0, channel_multiplier=1, allow_small_or_imprecise_dtypes=True))
        V.after(m_iota, m_lane)
        m_ident = V.did(v.tensor_scalar(ident, iota, lane[:, 0:1], None, ALU.is_equal))

        pad_s = big[:, 0:NCS * RS]
        m0 = G.did(g.memset(rec_d, 0.0))
        m1 = G.did(g.memset(pad_s, 0.0))
        G.after(m0, m1)
        for col in (D_DL, D_DL32):
            G.did(g.memset(recd3[:, :, col], -1.0))
        m_pad = G.did(g.memset(pad_s.rearrange("p (c r) -> p c r", r=RS)[:, :, S_SL], -1.0))
        src_i, src_in = idx_s[0:EP, 0:EJ], landing("src_in")
        m_src = src_in.started(sp.dma_start(src_i, t["src"].rearrange("(p j) -> p j", p=EP)))
        S.after(m_pad)
        prefilled.started(sp.dma_start(rec_d_dram.rearrange("(p c) r -> p (c r)", p=P), rec_d))
        m_prefilled = prefilled.started(sp.dma_start(rec_s_dram.rearrange("(p c) r -> p (c r)", p=P), pad_s))

        S.after(m_prefilled)
        at = [0]

        def raw(width):
            r = big[0:EP, at[0]:at[0] + width]
            at[0] += width
            assert at[0] <= big.shape[1]
            return r

        dst_i, w_raw = raw(EJ).bitcast(I32), raw(EJ)
        ea3_raw, ea4_raw, ea8_raw = raw(EJ * 3), raw(EJ * 4), rec_d[0:EP, 0:EJ * 8]
        for buf, name in ((dst_i, "dst"), (w_raw, "edge_weight")):
            load_in.started(sp.dma_start(buf, t[name].rearrange("(p j) -> p j", p=EP)))
        for buf, name in ((ea4_raw, "edge_attr_4"), (ea8_raw, "edge_attr_8"), (ea3_raw, "edge_attr_3")):
            m_raw = load_in.started(sp.dma_start(buf, t[name].rearrange("(p j) k -> p (j k)", p=EP)))
        buckets, scan, pos = sl_s[0:EP, 0:EJ], norm[0:EP, 0:EJ], wts[0:EP, 0:EJ]
        tmp_i = wts[0:EP, EJ:2 * EJ].bitcast(I32)
        lo_bufs = [cut(raw(1024), 0, 1024, 8, P) for _ in range(2)]
        hit = ring[0:EP, 0:EJ].bitcast(I32)
        stage_s = acc[0:EP, 0:EJ * RS].rearrange("p (j r) -> p j r", r=RS)
        stage_d = x[0:EP, 0:EJ * RD].rearrange("p (j r) -> p j r", r=RD)
        before = ring[0:EP, 5900:5900 + P]
        ones = small[0:EP, 0:P]
        zero = small[0:EP, P:P + 1]
        V.after(m_ident, m_src)
        A.after(m_raw)
        V.did(v.tensor_scalar(before, iota[0:EP, :], lane[0:EP, 0:1], None, ALU.is_gt))
        V.did(v.memset(ones, 1.0))
        V.did(v.memset(zero, 0.0))

        def chain(ins):
            m = V.did(ins)
            V.after(m)
            return m

        def field(out_f, key, shift, mask):
            chain(v.tensor_scalar(tmp_i, key, shift, mask, ALU.logical_shift_right, ALU.bitwise_and))
            return chain(v.tensor_copy(out_f, tmp_i))

        ea4_3, ea8_3 = (ea4_raw.rearrange("p (j k) -> p j k", k=4), ea8_raw.rearrange("p (j k) -> p j k", k=8))
        ea3_3 = ea3_raw.rearrange("p (j k) -> p j k", k=3)
        m_attr_s = [A.did(a.copy(stage_s[:, :, S_SH:S_SH + 4], ea4_3)),
                    A.did(a.copy(stage_s[:, :, S_EA:S_EA + 8], ea8_3))]
        m_attr_d = [A.did(a.copy(stage_d[:, :, D_EA:D_EA + 3], ea3_3)),
                    A.did(a.copy(stage_d[:, :, D_W], w_raw))]

        def stage_keys():
            V.after(m_raw)
            V.did(v.memset(stage_s[:, :, 14:16], 0.0))
            V.did(v.memset(stage_d[:, :, D_ONE], 1.0))
            V.did(v.tensor_copy(stage_s.bitcast(I32)[:, :, S_IDX], dst_i))
            V.did(v.tensor_copy(stage_d.bitcast(I32)[:, :, D_IDX], src_i))
            field(stage_s[:, :, S_SL], src_i, 0, P - 1)
            field(stage_d[:, :, D_DL], dst_i, 0, P - 1)
            return field(stage_d[:, :, D_DL32], dst_i, 0, SUB - 1)

        tot, off = ring[0:EP, 900:1000], ring[0:EP, 1000:1100]
        units, ends = ring[:, 1100:1200], ring[:, 1200:1300]
        units_i = ring[:, 1300:1400].bitcast(I32)
        counted = ring[:, 1400:1400 + JD * NBD]
        number = ring[:, 2200:2200 + JD]
        bucket_of, bucket_i = ring[:, 2300:2300 + JD], ring[:, 2400:2400 + JD].bitcast(I32)
        block_i = ring[:, 2500:2500 + JD].bitcast(I32)

        def rank(key, shift, nb, unit_chunks, chunks, slot_row):
            unit = unit_chunks * P
            field(buckets, key, shift, (1 << 20) - 1)
            for b in range(nb):
                chain(v.tensor_scalar(scan, buckets, float(b), 0.0, ALU.is_equal, ALU.add,
                                      accum_out=tot[:, b:b + 1]))
            T.after(V.last())
            T.did(pe.matmul(ps[0][:, 0:nb], before, tot[:, 0:nb], start=True, stop=True))
            m = T.did(pe.matmul(ps[1][:, 0:nb], small[0:EP, 0:P], tot[:, 0:nb], start=True, stop=True))
            V.after(m)
            chain(v.tensor_scalar(units_i[:, 0:nb], ps[1][:, 0:nb], float(unit - 1), None, ALU.add))
            chain(v.tensor_scalar(units_i[:, 0:nb], units_i[:, 0:nb], unit.bit_length() - 1, None,
                                  ALU.logical_shift_right))
            chain(v.tensor_copy(units[:, 0:nb], units_i[:, 0:nb]))
            chain(v.tensor_tensor_scan(ends[:, 0:nb], units[:, 0:nb], small[:, P + 1:P + 2].to_broadcast([P, nb]),
                                       0.0, ALU.add, ALU.add))
            chain(v.tensor_tensor(off[:, 0:nb], ends[0:EP, 0:nb], units[0:EP, 0:nb], ALU.subtract))
            chain(v.tensor_scalar(off[:, 0:nb], off[:, 0:nb], float(unit), -1.0, ALU.mult, ALU.add))
            chain(v.tensor_tensor(off[:, 0:nb], off[:, 0:nb], ps[0][0:EP, 0:nb], ALU.add))
            for b in range(nb):
                chain(v.tensor_scalar(hit, buckets, float(b), None, ALU.is_equal))
                chain(v.tensor_tensor_scan(scan, hit, zero.to_broadcast([EP, EJ]), off[:, b:b + 1],
                                           ALU.add, ALU.add))
                chain(v.copy_predicated(pos, hit, scan))
            chain(v.tensor_copy(tmp_i, pos))
            chain(v.tensor_scalar(hit, tmp_i, P - 1, None, ALU.bitwise_and))
            chain(v.tensor_scalar(tmp_i, tmp_i, 7, None, ALU.logical_shift_right))
            chain(v.tensor_copy(scan, hit))
            chain(v.tensor_copy(pos, tmp_i))
            return chain(v.scalar_tensor_tensor(out=slot_row, in0=scan, scalar=float(chunks), in1=pos,
                                                op0=ALU.mult, op1=ALU.add))

        def bucket_numbers(nb, j):
            G.after(V.last())
            m = G.did(g.iota(number[:, 0:j], [[1, j]], base=0, channel_multiplier=j,
                             allow_small_or_imprecise_dtypes=True))
            V.after(m)
            c3 = counted[:, 0:j * nb].rearrange("p (j b) -> p j b", j=j)
            chain(v.tensor_tensor(c3, rows(ends[:, 0:nb], j, nb), lanes(number[:, 0:j], j, nb), ALU.is_le))
            chain(v.tensor_reduce(bucket_of[:, 0:j], c3, AX.X, ALU.add))
            return chain(v.tensor_scalar(bucket_i[:, 0:j], bucket_of[:, 0:j], float(nb - 1), None, ALU.min))

        chain(v.memset(small[:, P + 1:P + 2], 0.0))
        chain(v.memset(pos, 0.0))
        numbers_out, numbers_in = landing("numbers_out"), landing("numbers_in")
        scattered_s, scattered_d = landing("scattered_s"), landing("scattered_d")
        row_s, row_d = ring[0:EP, 2600:2600 + EJ].bitcast(I32), ring[0:EP, 3400:3400 + EJ].bitcast(I32)

        def scatter(row, stage, table, where, *marks):
            G.after(*marks)
            for j in range(EJ):
                m = where.started(g.indirect_dma_start(
                    out=table, out_offset=bass.IndirectOffsetOnAxis(ap=row[:, j:j + 1], axis=0),
                    in_=stage[:, j, :], in_offset=None))
            return m

        def keep_numbers(buf, table, row, n):
            S.after(V.last())
            m = numbers_out.started(sp.dma_start(table, buf))
            S.after(m)
            return numbers_in.started(sp.dma_start(row[0:1, 0:n], table.rearrange("(o p) j -> o (p j)", o=1)))

        m_row_s = rank(src_i, 7, NB, GS, NCS, row_s)
        m_keys = stage_keys()
        bucket_numbers(NB, JS)
        keep_numbers(bucket_i[:, 0:JS], blk_s_dram, blk_s_row, P * JS)
        m_scattered_s = scatter(row_s, stage_s, rec_s_dram, scattered_s, m_prefilled, m_keys, m_attr_s, m_row_s)
        m_row_d = rank(dst_i, 5, NBD, 1, NCD, row_d)
        V.after((numbers_out.sem, numbers_out.count))
        bucket_numbers(NBD, JD)
        chain(v.tensor_scalar(block_i, bucket_i, 2, None, ALU.logical_shift_right))
        keep_numbers(bucket_i, b32_dram, b32_row, P * JD)
        m_numbers = keep_numbers(block_i, blk_d_dram, blk_d_row, P * JD)
        m_scattered_d = scatter(row_d, stage_d, rec_d_dram, scattered_d, m_attr_d, m_row_d)

        BJ = 8
        low_f, high_f = buckets, scan
        for key, deg, bank in ((src_i, deg_s, 2), (dst_i, deg_d, 3)):
            field(low_f, key, 0, P - 1)
            field(high_f, key, 7, (1 << 20) - 1)
            used = [None, None]
            hi_bufs = [cut(ring[0:EP], 4300 + k * 2 * NB * BJ, 2 * NB * BJ, BJ, 2 * NB) for k in range(2)]
            for i in range(EJ // BJ):
                lo3, hi3, js = lo_bufs[i % 2], hi_bufs[i % 2], slice(i * BJ, i * BJ + BJ)
                V.after(used[i % 2])
                V.did(v.tensor_tensor(lo3, rows(iota[0:EP, :], BJ, P), lanes(low_f[:, js], BJ, P), ALU.is_equal))
                m = V.did(v.tensor_tensor(hi3[:, :, NB:2 * NB], rows(iota[0:EP, 0:NB], BJ, NB),
                                          lanes(high_f[:, js], BJ, NB), ALU.is_equal))
                V.after(m)
                m = V.did(v.tensor_tensor(hi3[:, :, 0:NB], hi3[:, :, NB:2 * NB], lanes(w_raw[:, js], BJ, NB),
                                          ALU.mult))
                T.after(m)
                for k in range(BJ):
                    j = i * BJ + k
                    ins = pe.matmul(ps[bank][:, 0:2 * NB], lo3[:, k, :], hi3[:, k, :], start=(j == 0),
                                    stop=(j == EJ - 1))
                used[i % 2] = T.did(ins)
            V.after(T.last())
            m_deg = chain(v.tensor_copy(deg, ps[bank][:, 0:2 * NB]))
        din_t, din_row = ring[0:NB, 5200:5200 + P], acc[:, 6400:6400 + NPAD]
        T.after(m_deg)
        m = T.did(pe.transpose(ps[4][0:NB, 0:P], deg_d[:, 0:NB], ident))
        V.after(m)
        m = chain(v.tensor_copy(din_t, ps[4][0:NB, 0:P]))
        S.after(m)
        din_out, din_in = landing("din_out"), landing("din_in")
        m = din_out.started(sp.dma_start(din_dram, din_t))
        S.after(m, m_scattered_s)
        m_din = din_in.started(sp.dma_start(
            din_row, din_dram.rearrange("(o b) p -> o (b p)", o=1).to_broadcast([P, NPAD])))
        barrier()

        x_in, rec_in = landing("x_in"), landing("rec_in")
        table_out = landing("table_out")
        stats = ring[:, 5000:5000 + NB * 6].rearrange("p (b s) -> p b s", s=6)
        mv = ring[:, 5200:5200 + NB * 2].rearrange("p (b s) -> p b s", s=2)
        rstd = ring[:, 5300:5300 + NB]

        def rsqrt_of(buf, mark):
            A.after(mark)
            m = A.did(a.activation(buf, buf, ACT.Sqrt))
            V.after(m)
            return chain(v.reciprocal(buf, buf))

        def layernorm():
            V.after(V.last())
            for b in range(NB):
                V.did(v.bn_stats(stats[:, b, :], x3[:, b, :]))
            V.after(V.last())
            for b in range(NB):
                V.did(v.bn_aggr(mv[:, b, :], stats[:, b, :]))
            V.after(V.last())
            m = chain(v.tensor_scalar(rstd, mv[:, :, 1], EPS1, None, ALU.add))
            rsqrt_of(rstd, m)
            for b in range(NB):
                V.did(v.tensor_scalar(x3[:, b, :], x3[:, b, :], mv[:, b, 0:1], rstd[:, b:b + 1],
                                      ALU.subtract, ALU.mult))
            return V.last()

        def write_table(table, view, mark):
            S.after(mark)
            return table_out.started(sp.dma_start(table.rearrange("(b p) k -> p b k", p=P), view))

        def linear(view, weight, finish):
            turned = cut(ring, 0, 1024, 4, 256)
            cols, done, prod, fin = Marks(), Marks(), Marks(), Marks()

            def turn(b):
                T.after(cols.get(b - 4))
                for k in range(2):
                    ins = pe.transpose(ps[b % 4][:, k * P:(k + 1) * P], view[:, b, k * P:(k + 1) * P], ident)
                done[b] = T.did(ins)

            def keep(b):
                A.after(done[b], prod.get(b - 4))
                cols[b] = A.did(a.copy(turned[:, b % 4, :], ps[b % 4][:, 0:D]))

            def product(b):
                T.after(cols[b], fin.get(b - 4))
                for k in range(2):
                    ins = pe.matmul(ps[4 + b % 4][:, 0:D], turned[:, b % 4, k * P:(k + 1) * P], weight[:, k, :],
                                    start=(k == 0), stop=(k == 1))
                prod[b] = T.did(ins)

            def end(b):
                V.after(prod[b])
                fin[b] = finish(b, ps[4 + b % 4][:, 0:D])

            pipeline(NB, (0, turn), (0, keep), (2, product), (3, end))

        def load(buf, src, slot=s_w):
            return slot.started(sp.dma_start(buf, src))

        def two(name):
            return t[name].rearrange("(k p) n -> p k n", p=P)

        def everywhere(name, n):
            return t[name].rearrange("(o n) -> o n", o=1).to_broadcast([P, n])

        blk_v = Numbers(V, "blk_v", blk_d_row, NB - 1)
        b32_v = Numbers(V, "b32_v", b32_row, NBD - 1)
        blk_t = Numbers(T, "blk_t", blk_d_row, NB - 1)

        w6, w7, wp = (cut(wts, k * 512, 512, 2, D) for k in range(3))
        load(w6, two("L0_gnn_W6"))
        load(w7, two("L0_gnn_W7"))
        load(wp, two("L0_gnn_Wp"))
        b6, b7, bp = (wts[:, 1536 + k * D:1536 + (k + 1) * D] for k in range(3))
        load(b6, everywhere("L0_gnn_b6", D))
        load(b7, everywhere("L0_gnn_b7", D))
        m_weights = load(bp, everywhere("L0_gnn_bp", D))
        m_rec = rec_in.started(sp.dma_start(rec_d, rec_d_dram.rearrange("(p c) r -> p (c r)", p=P)))
        m = V.did(v.memset(x, 0.0))
        S.after(m)
        x_in.started(sp.dma_start(x3[:, 0:NB - 1, :], t["x"][0:(NB - 1) * P, :].rearrange("(b p) k -> p b k", p=P)))
        m_x = x_in.started(sp.dma_start(x3[0:LAST, NB - 1, :], t["x"][(NB - 1) * P:N, :]))
        staged = cut(big, 0, NB * TW, NB, TW)
        V.after(m_x)
        V.did(v.memset(staged[:, :, D:TW], 0.0))
        V.did(v.tensor_copy(staged[:, :, 0:D], x3))
        V.after(V.last())
        m = V.did(v.tensor_copy(staged[:, :, D], deg_s[:, 0:NB]))
        m_table = write_table(x_table, staged, m)
        acc0 = cut(acc, 0, NB * D, NB, D)
        m_zero = V.did(v.memset(acc0, 0.0))

        def gcn_sums(rows_of, s_row, first, onehot, weighted, nbuf):
            weight, summed, added = Marks(), Marks(), Marks()

            def scale(c):
                weight[c] = weighted(c, onehot[:, c % nbuf, :], summed.get(c - nbuf))

            def product(c):
                T.after(s_row(c), weight[c], added.get(c - 8))
                summed[c] = T.did(pe.matmul(ps[c % 8][:, 0:D], onehot[:, c % nbuf, :], rows_of(c),
                                            start=True, stop=True))

            def add(c):
                V.after(summed[c], added.get(c - 1), first)
                here = acc[:, bass.ds(blk_v.at(c) * D, D)]
                added[c] = V.did(v.tensor_tensor(here, here, ps[c % 8][:, 0:D], ALU.add))

            return scale, product, add, summed, added

        RG = 24
        xg = cut(big, NB * TW, RG * TW, RG, TW)
        onehot = cut(ring, 0, 1024, 8, P)
        dst_hot = [cut(ring, 1024 * (1 + k), 1024, 8, P) for k in range(3)]
        picked = cut(ring, 4096, 8 * P, 8, P)
        gathered = [landing(f"gathered{i}") for i in range(RG)]
        got, normed, half_normed, hot_at = Marks(), Marks(), Marks(), Marks()

        def weigh_by_scalar(c, slot, free):
            A.after(normed[c // 8], free)
            return A.did(a.mul(slot, dst_hot[c // 8 % 3][:, c % 8, :], norm[:, c:c + 1]))

        scale, product, add, summed, added = gcn_sums(
            lambda c: xg[:, c % RG, 0:D], lambda c: got[c], [m_zero, m_rec, m_weights], onehot, weigh_by_scalar, 8)

        def gather_x(c):
            G.after(summed.get(c - RG), m_table, m_rec)
            got[c] = gathered[c % RG].started(g.indirect_dma_start(
                out=xg[:, c % RG, :], out_offset=None, in_=x_table,
                in_offset=bass.IndirectOffsetOnAxis(ap=recd3i[:, c, D_IDX:D_IDX + 1], axis=0)))

        din_e, root = small[:, 0:8], small[:, 16:32]
        blk_v2 = Numbers(V, "blk_v2", blk_d_row, NB - 1)
        din_at, weighed = Marks(), Marks()

        def dst_one_hots(i):
            V.after(m_rec, m_din, weighed.get(8 * i - 17))
            hot_at[i] = V.did(v.tensor_tensor(dst_hot[i % 3], rows(iota, 8, P),
                                              lanes(recd3[:, 8 * i:8 * i + 8, D_DL], 8, P), ALU.is_equal))

        def pick_din(c):
            V.after(hot_at[c // 8], din_at.get(c // 8 - 1))
            V.did(v.tensor_tensor(picked[:, c % 8, :], dst_hot[c // 8 % 3][:, c % 8, :],
                                  acc[:, bass.ds(blk_v2.at(c) * P + 6400, P)], ALU.mult))

        def edge_norm(i):
            V.after(V.last())
            din_at[i] = chain(v.tensor_reduce(din_e, picked, AX.X, ALU.add))
            V.after(*[got[c] for c in range(8 * i, 8 * i + 8)])
            r0, at8 = (8 * i) % RG, root[:, 8 * (i % 2):8 * (i % 2) + 8]
            chain(v.tensor_tensor(at8, xg[:, r0:r0 + 8, D], din_e, ALU.mult))
            A.after(chain(v.tensor_scalar(at8, at8, EPS0, None, ALU.add)))
            half_normed[i] = A.did(a.activation(at8, at8, ACT.Sqrt))

        def edge_norm_end(i):
            at8 = root[:, 8 * (i % 2):8 * (i % 2) + 8]
            V.after(half_normed[i])
            chain(v.reciprocal(at8, at8))
            normed[i] = V.did(v.tensor_tensor(norm[:, 8 * i:8 * i + 8], at8, recd3[:, 8 * i:8 * i + 8, D_W], ALU.mult))

        def scale_counted(c):
            scale(c)
            weighed[c] = A.last()

        def every(n, stage, k):
            return lambda c: stage(c // n) if c % n == k else None

        pipeline(NCD, (0, gather_x), (2, every(8, dst_one_hots, 0)), (3, pick_din), (3, every(8, edge_norm, 7)),
                 (4, every(8, edge_norm_end, 7)), (12, scale_counted), (13, product), (16, add))
        barrier()

        h6 = cut(big, 0, NB * D, NB, D)

        def relu_bias(view, bias):
            def finish(b, product):
                m = chain(v.tensor_tensor(view[:, b, :], product, bias, ALU.add))
                V.did(v.tensor_scalar(view[:, b, :], view[:, b, :], 0.0, None, ALU.max))
                return m
            return finish

        linear(acc0, w6, relu_bias(h6, b6))
        m_table = write_table(h6_table, h6, V.last())
        barrier()
        m_zero = V.did(v.memset(acc0, 0.0))

        def gather_rows(table, width, index, depth, free, spare=0):
            slots = cut(ring, 0, depth * (spare + width), depth, spare + width)
            here = Marks()

            def stage(c):
                G.after(free(c))
                here[c] = gathered[c % depth].started(g.indirect_dma_start(
                    out=slots[:, c % depth, spare:], out_offset=None, in_=table,
                    in_offset=bass.IndirectOffsetOnAxis(ap=index(c), axis=0)))
            return stage, slots, here

        R2 = 12
        gather, hg, got2 = gather_rows(h6_table, D, lambda c: recd3i[:, c, D_IDX:D_IDX + 1], R2,
                                       lambda c: [m_table, summed2.get(c - R2)])

        def weigh(c, slot, free):
            V.after(free)
            return V.did(v.tensor_scalar(slot, iota, recd3[:, c, D_DL:D_DL + 1], norm[:, c:c + 1],
                                         ALU.is_equal, ALU.mult))

        scale, product, add, summed2, _ = gcn_sums(
            lambda c: hg[:, c % R2, :], lambda c: got2[c], m_zero, cut(ring, R2 * D, 512, 4, P), weigh, 4)
        pipeline(NCD, (0, gather), (6, scale), (6, product), (8, add))
        barrier()

        h7 = h6
        linear(acc0, w7, relu_bias(h7, b7))
        V.after(V.last())
        T.after(V.last())

        def residual_bias(bias):
            def finish(b, product):
                m = chain(v.tensor_tensor(x3[:, b, :], x3[:, b, :], product, ALU.add))
                V.did(v.tensor_tensor(x3[:, b, :], x3[:, b, :], bias, ALU.add))
                return m
            return finish

        linear(h7, wp, residual_bias(bp))
        layernorm()
        barrier()

        recs3 = cut(big, 0, NCS * RS, NCS, RS)
        m_recs = rec_in.started(sp.dma_start(big[:, 0:NCS * RS], rec_s_dram.rearrange("(p c) r -> p (c r)", p=P)))
        w1 = wts[0:MUL, 0:2 * MUL]
        wsc = wts[0:MUL, 128:128 + 2 * MUL]
        w2 = wts[:, 256:256 + 2 * MUL]
        fc1 = cut(wts, 384, 512, 4, P)
        fc2 = wts[:, 896:896 + P]
        fc3 = wts[:, 1024:1024 + D]
        gain_s, gain_v = wts[:, 1280:1280 + MUL], wts[:, 1344:1344 + MUL]
        m = V.did(v.memset(wts[:, 384:1024], 0.0))
        S.after(m)
        load(w1[:, 0:MUL], t["L1_gnn_w1_s"])
        load(w1[:, MUL:2 * MUL], t["L1_gnn_w1_v"])
        load(wsc[:, 0:MUL], t["L1_gnn_wsc_s"])
        load(wsc[:, MUL:2 * MUL], t["L1_gnn_wsc_v"])
        load(w2[:, 0:MUL], t["L1_gnn_w2_s"])
        load(w2[:, MUL:2 * MUL], t["L1_gnn_w2_v"])
        for k in range(8):
            load(fc1[k * RS + S_EA:k * RS + S_EA + 8, k // 2, (k % 2) * MUL:(k % 2) * MUL + MUL], t["L1_gnn_fc_w1"])
        for k in range(2):
            load(fc2[k * MUL:(k + 1) * MUL, k * MUL:(k + 1) * MUL], t["L1_gnn_fc_w2"])
            for to, part in enumerate((0, 2, 3, 1)):
                load(fc3[k * MUL:(k + 1) * MUL, to * MUL:(to + 1) * MUL],
                     t["L1_gnn_fc_w3"][:, part * MUL:(part + 1) * MUL])
        load(gain_s, everywhere("L1_gnn_g_s", MUL))
        m_weights = load(gain_v, everywhere("L1_gnn_g_v", MUL))
        V.after(m_weights, m_recs)
        T.after(m_weights, m_recs)
        chain(v.tensor_scalar(fc3, fc3, 0.125, None, ALU.mult))
        chain(v.tensor_scalar(fc3[:, 2 * MUL:3 * MUL], fc3[:, 2 * MUL:3 * MUL], 0.5773502691896258, None, ALU.mult))
        V.did(v.tensor_copy(idx_s, recs3.bitcast(I32)[:, :, S_IDX]))
        m_idx = V.did(v.tensor_copy(sl_s, recs3[:, :, S_SL]))
        T.after(m_idx)

        acc1 = cut(acc, 0, NB * 512, NB, 512)

        def vector_parts(bank, b):
            for q in range(4):
                part = x3[:, b, 0:MUL] if q == 0 else x3[:, b, MUL + q - 1:4 * MUL:3]
                ins = pe.transpose(bank[0:MUL, q * P:(q + 1) * P], part, ident)
            return T.did(ins)

        def parts_product(bank, at0, turned, weights):
            for q in range(4):
                w = weights[:, 0:MUL] if q == 0 else weights[:, MUL:2 * MUL]
                ins = pe.matmul(bank[:, at0 + q * MUL:at0 + (q + 1) * MUL], turned[0:MUL, q * P:(q + 1) * P], w,
                                start=True, stop=True)
            return T.did(ins)

        turned1 = cut(ring, 0, 1024, 2, 512)
        tn, kp, pr, fi = Marks(), Marks(), Marks(), Marks()

        def y_turn(b):
            T.after(kp.get(b - 2))
            tn[b] = vector_parts(ps[b % 2], b)

        def y_keep(b):
            A.after(tn[b], pr.get(b - 2))
            kp[b] = A.did(a.copy(turned1[0:MUL, b % 2, :], ps[b % 2][0:MUL, :]))

        def y_product(b):
            T.after(kp[b], fi.get(b - 2))
            pr[b] = parts_product(ps[2 + b % 2], 0, turned1[:, b % 2, :], w1)

        def y_end(b):
            V.after(pr[b])
            fi[b] = V.did(v.tensor_scalar(acc1[:, b, 0:D], ps[2 + b % 2][:, 0:D], 0.125, None, ALU.mult))

        pipeline(NB, (0, y_turn), (0, y_keep), (1, y_product), (2, y_end))
        m_table = write_table(y_table, acc1[:, :, 0:D], V.last())
        barrier()
        m_zero = V.did(v.memset(acc, 0.0))

        RY = 7
        gather, yg, got_y = gather_rows(y_table, D, lambda c: idx_s[:, c:c + 1], RY,
                                        lambda c: [m_table, m_idx, mixed.get(c - RY)], MUL)
        o = RY * (MUL + D)
        mid = cut(ring, o, 2 * 576, 2, 576)
        o += 2 * 576
        rec_t = cut(ring, o, 256, 2, P)
        o += 256
        h1 = ring[:, o:o + 512]
        o += 512
        h2 = cut(ring, o, 1024, 2, 512)
        o += 1024
        dots = cut(ring, o, 2 * 192, 2, 192)
        o += 2 * 192
        y_sh0 = cut(ring, o, 2 * D, 2, D)
        assert o + 2 * D <= ring.shape[1]
        oh1 = [cut(wts, 1408 + 512 * k, 512, 4, P) for k in range(2)]
        c_rt, c_rk, c_1, c_s1, c_2, c_s2 = Marks(), Marks(), Marks(), Marks(), Marks(), Marks()
        w_ready, mixed, mids, oh_at, sum1, added1 = Marks(), Marks(), Marks(), Marks(), Marks(), Marks()
        blk_s = Numbers(V, "blk_s", blk_s_row, NB - 1)

        def mlp_in(i):
            T.after(c_rk.get(i - 1))
            c_rt[i] = T.did(pe.transpose(ps[0][:, 0:P], big[:, i * P:(i + 1) * P], ident))
            A.after(c_rt[i], c_1.get(i - 2))
            c_rk[i] = A.did(a.copy(rec_t[:, i % 2, :], ps[0][:, 0:P]))

        def mlp_1(i):
            T.after(c_rk[i], c_s1.get(i - 1))
            for j in range(4):
                ins = pe.matmul(ps[1][:, j * P:(j + 1) * P], fc1[:, j, :], rec_t[:, i % 2, :], start=True, stop=True)
            c_1[i] = T.did(ins)
            A.after(c_1[i], c_2.get(i - 1))
            c_s1[i] = A.did(a.activation(h1, ps[1], ACT.Silu, scale=float(1.0 / np.sqrt(8.0))))

        def mlp_2(i):
            T.after(c_s1[i], c_s2.get(i - 1))
            c_2[i] = T.did(pe.matmul(ps[2], fc2, h1, start=True, stop=True))
            A.after(c_2[i], w_ready.get(8 * (i - 2) + 7))
            c_s2[i] = A.did(a.activation(h2[:, i % 2, :], ps[2], ACT.Silu, scale=0.125))

        def edge_weights(c):
            i, k = c // 8, c % 8
            half = slice((k % 2) * MUL, (k % 2) * MUL + MUL)
            T.after(c_s2[i], mixed.get(c - 3))
            w_ready[c] = T.did(pe.matmul(ps[3 + c % 3][:, 0:D], h2[half, i % 2, (k // 2) * P:(k // 2) * P + P],
                                         fc3[half, :], start=True, stop=True))

        scaled_y, hot1, reduced = Marks(), Marks(), Marks()

        def scale_y(c):
            y = yg[:, c % RY, MUL:]
            A.after(got_y[c], mixed.get(c - 2))
            A.did(a.mul(y_sh0[:, c % 2, :], y, recs3[:, c, S_SH:S_SH + 1]))
            for d in range(3):
                scaled_y[c] = A.did(a.mul(dots[:, c % 2, d * MUL:(d + 1) * MUL], y[:, (1 + d) * MUL:(2 + d) * MUL],
                                          recs3[:, c, S_SH + 1 + d:S_SH + 2 + d]))

        def one_hot1(c):
            if c % 4 == 0:
                i = c // 4
                V.after(sum1.get(c - 5))
                hot1[i] = V.did(v.tensor_tensor(oh1[i % 2], rows(iota, 4, P), lanes(sl_s[:, c:c + 4], 4, P),
                                                ALU.is_equal))

        def messages(c):
            w, slot, m, ys = ps[3 + c % 3], yg[:, c % RY, :], mid[:, c % 2, :], y_sh0[:, c % 2, :]
            vec = m[:, 0:3 * P].rearrange("p (d s u) -> p d s u", d=3, s=2)
            V.after(scaled_y[c])
            red = V.did(v.tensor_reduce(slot[:, 0:MUL], dots[:, c % 2, :].rearrange("p (d u) -> p u d", d=3), AX.X,
                                        ALU.add))
            V.after(w_ready[c], sum1.get(c - 2))
            V.did(v.tensor_tensor(vec[:, :, 1, :], rows(w[:, MUL:2 * MUL], 3, MUL),
                                  ys[:, MUL:D].rearrange("p (d u) -> p d u", d=3), ALU.mult))
            V.after(red)
            t2 = V.did(v.tensor_tensor(m[:, 448:576], w[:, 2 * MUL:4 * MUL], slot[:, 0:2 * MUL], ALU.mult))
            V.did(v.tensor_tensor(m[:, 384:448], w[:, 0:MUL], ys[:, 0:MUL], ALU.mult))
            V.after(t2)
            mids[c] = mixed[c] = V.did(v.tensor_tensor(
                vec[:, :, 0, :], rows(m[:, 512:576], 3, MUL), lanes(recs3[:, c, S_SH + 1:S_SH + 4], 3, MUL), ALU.mult))

        def sums(c):
            u = c // GS
            T.after(mids[c], hot1[c // 4], added1.get(u - 2) if c % GS == 0 else None)
            sum1[c] = T.did(pe.matmul(ps[6 + u % 2], oh1[c // 4 % 2][:, c % 4, :], mid[:, c % 2, 0:512], start=(c % GS == 0),
                                      stop=(c % GS == GS - 1)))

        def add_unit(c):
            if c % GS == GS - 1:
                u = c // GS
                V.after(sum1[c], added1.get(u - 1), m_zero)
                here = acc[:, bass.ds(blk_s.at(u) * 512, 512)]
                added1[u] = V.did(v.tensor_tensor(here, here, ps[6 + u % 2], ALU.add))

        pipeline(NCS, (4, gather), (9, scale_y), (8, edge_weights), (0, every(8, mlp_in, 0)), (2, every(8, mlp_1, 0)),
                 (4, every(8, mlp_2, 0)), (9, one_hot1), (10, messages), (10, sums), (12, add_unit))
        barrier()

        o1 = cut(big, 0, NB * D, NB, D)
        dn = small[:, 0:NB]
        chain(v.tensor_scalar(dn, deg_s[:, NB:2 * NB], 1.0, None, ALU.max))
        rsqrt_of(dn, V.last())
        chain(v.tensor_scalar(dn, dn, float(1.0 / np.sqrt(2.0 * MUL)), None, ALU.mult))
        sq, ss = cut(ring, 2100, D, D), cut(small, 50, 2 * NB, 2, NB)
        turned_a, turned_x = cut(ring, 0, 1024, 2, 512), cut(ring, 1024, 1024, 2, 512)
        tn, kp, pr, fi = Marks(), Marks(), Marks(), Marks()

        def o_turn(b):
            T.after(kp.get(b - 1))
            for q in range(4):
                at1 = 3 * P if q == 0 else (q - 1) * P
                pe.transpose(ps[0][:, q * P:(q + 1) * P], acc1[:, b, at1:at1 + P], ident)
            tn[b] = vector_parts(ps[1], b)

        def o_keep(b):
            A.after(tn[b], pr.get(b - 2))
            A.did(a.copy(turned_a[:, b % 2, :], ps[0]))
            kp[b] = A.did(a.copy(turned_x[0:MUL, b % 2, :], ps[1][0:MUL, :]))

        def o_product(b):
            T.after(kp[b], fi.get(b - 2))
            for q in range(4):
                pe.matmul(ps[2 + b % 2][:, q * MUL:(q + 1) * MUL], turned_a[:, b % 2, q * P:(q + 1) * P],
                          w2[:, 0:MUL] if q == 0 else w2[:, MUL:2 * MUL], start=True, stop=True)
            pr[b] = parts_product(ps[2 + b % 2], D, turned_x[:, b % 2, :], wsc)

        def o_end(b):
            V.after(pr[b])
            m = V.did(v.tensor_scalar(o1[:, b, :], ps[2 + b % 2][:, 0:D], dn[:, b:b + 1], None, ALU.mult))
            V.after(m)
            fi[b] = V.did(v.scalar_tensor_tensor(out=o1[:, b, :], in0=ps[2 + b % 2][:, D:2 * D], scalar=0.125,
                                                 in1=o1[:, b, :], op0=ALU.mult, op1=ALU.add))
            A.after(fi[b], A.last())
            m = A.did(a.activation(sq[:, 0:MUL], o1[:, b, 0:MUL], ACT.Square, accum_out=ss[:, 0, b:b + 1]))
            A.after(m)
            A.did(a.activation(sq[:, MUL:D], o1[:, b, MUL:D], ACT.Square, accum_out=ss[:, 1, b:b + 1]))

        pipeline(NB, (0, o_turn), (0, o_keep), (1, o_product), (2, o_end))
        V.after(A.last(), V.last())
        chain(v.tensor_scalar(ss[:, 0, :], ss[:, 0, :], 1.0 / MUL, EPS1, ALU.mult, ALU.add))
        chain(v.tensor_scalar(ss[:, 1, :], ss[:, 1, :], 1.0 / (3 * MUL), EPS1, ALU.mult, ALU.add))
        rsqrt_of(small[:, 50:50 + 2 * NB], V.last())
        for b in range(NB):
            ov = o1[:, b, MUL:D].rearrange("p (d u) -> p d u", d=3)
            xv = x3[:, b, MUL:D].rearrange("p (u d) -> p d u", d=3)
            V.did(v.scalar_tensor_tensor(out=o1[:, b, 0:MUL], in0=o1[:, b, 0:MUL], scalar=ss[:, 0, b:b + 1],
                                         in1=gain_s, op0=ALU.mult, op1=ALU.mult))
            m = V.did(v.scalar_tensor_tensor(out=ov, in0=ov, scalar=ss[:, 1, b:b + 1], in1=rows(gain_v, 3, MUL),
                                             op0=ALU.mult, op1=ALU.mult))
            V.after(m)
            V.did(v.tensor_tensor(x3[:, b, 0:MUL], x3[:, b, 0:MUL], o1[:, b, 0:MUL], ALU.add))
            V.did(v.tensor_tensor(xv, xv, ov, ALU.add))
        layernorm()
        barrier()

        alpha = cut(big, 0, NCD * H, NCD, H)
        h_at = NCD * H
        hdst = cut(big, h_at, NB * TW, NB, TW)
        hsrc = cut(acc, 0, NB * TW, NB, TW)
        wexp = cut(acc, NB * TW, 16 * D, 16, D)
        w_att, w_att_t = cut(wts, 0, 512, 2, D), cut(wts, 512, 512, 2, D)
        a_src, a_dst, bias = wts[:, 1024:1280], wts[:, 1280:1536], wts[:, 1536:1792]
        top, top_t = small[:, 0:2 * NBD], small[:, 2 * NBD:4 * NBD]
        m_z = V.did(v.memset(wexp, 0.0))
        load(w_att, two("L2_gnn_W"))
        load(a_src, t["L2_gnn_a_src"].rearrange("(o h) d -> o (h d)", o=1).to_broadcast([P, D]))
        load(a_dst, t["L2_gnn_a_dst"].rearrange("(o h) d -> o (h d)", o=1).to_broadcast([P, D]))
        m_weights = load(bias, everywhere("L2_gnn_bias", D))
        ew_out = landing("ew_out")
        with nc.allow_non_contiguous_dma("the transposed edge weights, once"):
            ew_out.started(sp.dma_start(ew_dram[0:3, :], t["L2_gnn_edge_W"].rearrange("n f -> f n")))
        m = ew_out.started(sp.dma_start(ew_dram[3:4, :], t["L2_gnn_edge_b"].rearrange("(o n) -> o n", o=1)))
        S.after(m, m_z)
        for k in range(16):
            m_wexp = load(wexp[k * RD + D_EA:k * RD + D_EA + 4, k, :], ew_dram)
        T.after(m_weights)
        V.after(m_weights, m_wexp)
        for ki in range(2):
            for ko in range(2):
                ins = pe.transpose(ps[4 + ki][:, ko * P:(ko + 1) * P], w_att[:, ko, ki * P:(ki + 1) * P], ident)
        V.after(T.did(ins))
        for ki in range(2):
            m = V.did(v.tensor_copy(w_att_t[:, ki, :], ps[4 + ki][:, 0:D]))
        T.after(m)
        logit = ring[:, 2048:2048 + D]

        def attention_tables(b, product):
            A.after((T.sem, T.count), V.last())
            A.did(a.copy(hsrc[:, b, 0:D], product))
            V.after(A.did(a.copy(hdst[:, b, 0:D], product)))
            for a_vec, where in ((a_src, hsrc), (a_dst, hdst)):
                chain(v.tensor_tensor(logit, hdst[:, b, 0:D], a_vec, ALU.mult))
                chain(v.tensor_reduce(where[:, b, D:TW], logit.rearrange("p (h d) -> p h d", h=H), AX.X, ALU.add))
            return V.last()

        linear(x3, w_att_t, attention_tables)
        m_table = write_table(att_table, hsrc, V.last())
        m_top = V.did(v.memset(top, -BIG))
        T.after(m_wexp, V.last())

        R3 = 12
        gather, ag, got_a = gather_rows(att_table, TW, lambda c: recd3i[:, c, D_IDX:D_IDX + 1], R3,
                                        lambda c: [m_table, spilled.get(c - R3), used2.get(c - R3)])
        o = R3 * TW
        oh2_t = cut(ring, o, 8 * P, 8, P)
        o += 8 * P
        rec_t2 = cut(ring, o, 2 * P, 2, P)
        o += 2 * P
        enc = cut(ring, o, 3 * D, 3, D)
        o += 3 * D
        prod2 = cut(ring, o, 2 * D, 2, D)
        o += 2 * D
        miss = cut(ring, o, 4 * SUB, 4, SUB)
        o += 4 * SUB
        red4, lg4, mx = cut(ring, o, 64, 8, H), cut(ring, o + 64, 64, 8, H), cut(ring, o + 128, 16, 2, 8)
        assert o + 144 <= ring.shape[1]
        o = NB * TW + 16 * D
        oh2 = [cut(acc, o + k * 512, 512, 4, P) for k in range(2)]
        spread = cut(acc, o + 1024, 1024, 4, D)
        assert o + 2048 <= acc.shape[1]
        spill = [landing(f"spill{i}") for i in range(R3)]
        spilled, logits, hot2, oht, ohk, rt2, rk2 = Marks(), Marks(), Marks(), Marks(), Marks(), Marks(), Marks()
        hd_at, enc_at, enc_ok, used2, masked, mtop, maxed = Marks(), Marks(), Marks(), Marks(), Marks(), Marks(), Marks()

        def spill_rows(c):
            S.after(got_a[c])
            spilled[c] = spill[c % R3].started(sp.dma_start(rows_spill[c], ag[:, c % R3, 0:D]))

        def one_hot4x(i):
            V.after(oht.get(i - 2))
            hot2[i] = V.did(v.tensor_tensor(oh2[i % 2], rows(iota, 4, P),
                                            lanes(recd3[:, 4 * i:4 * i + 4, D_DL], 4, P), ALU.is_equal))

        def turn_one_hots(i, hot, free, bank_read=None):
            T.after(hot2[i], ohk.get(i - 1), bank_read)
            for k in range(4):
                ins = pe.transpose(ps[0][:, k * P:(k + 1) * P], hot[:, k, :], ident)
            oht[i] = T.did(ins)
            A.after(oht[i], free)
            ohk[i] = A.did(a.copy(oh2_t[:, 4 * (i % 2):4 * (i % 2) + 4, :].rearrange("p k e -> p (k e)"), ps[0]))

        def turn_records(c):
            if c % 16 == 0:
                i = c // 16
                T.after(ohk.get(c // 4 - 1))
                rt2[i] = T.did(pe.transpose(ps[0][:, 0:P], rec_d[:, i * P:(i + 1) * P], ident))
                A.after(rt2[i], enc_at.get(16 * (i - 1) - 1))
                rk2[i] = A.did(a.copy(rec_t2[:, i % 2, :], ps[0][:, 0:P]))

        def node_and_edge_parts(c):
            T.after(rk2[c // 16], enc_ok.get(c - 2))
            enc_at[c] = T.did(pe.matmul(ps[4 + c % 2][:, 0:D], rec_t2[:, (c // 16) % 2, :], wexp[:, c % 16, :],
                                        start=True, stop=True))
            A.after(enc_at[c], used2.get(c - 3))
            enc_ok[c] = A.did(a.activation(enc[:, c % 3, :], ps[4 + c % 2][:, 0:D], ACT.Relu))
            T.after(ohk[c // 4], used2.get(c - 3))
            hd_at[c] = T.did(pe.matmul(ps[1 + c % 3][:, 0:TW], oh2_t[:, c % 8, :],
                                       big[:, bass.ds(blk_t.at(c) * TW + h_at, TW)], start=True, stop=True))

        def edge_product(c):
            hd = ps[1 + c % 3]
            V.after(hd_at[c], enc_ok[c], got_a[c], reduced2.get(c - 2), logits.get(c // 4 - 2))
            made[c] = V.did(v.tensor_tensor(prod2[:, c % 2, :], hd[:, 0:D], enc[:, c % 3, :], ALU.mult))
            used2[c] = V.did(v.tensor_tensor(lg4[:, c % 8, :], hd[:, D:TW], ag[:, c % R3, D:TW], ALU.add))

        def edge_dot(c):
            V.after(made[c], logits.get(c // 4 - 2))
            reduced2[c] = V.did(v.tensor_reduce(
                red4[:, c % 8, :], prod2[:, c % 2, :].rearrange("p (h d) -> p h d", h=H), AX.X, ALU.add))

        def edge_logits(i):
            V.after(masked.get(4 * i - 1))
            V.did(v.tensor_tensor(miss, rows(iota[:, 0:SUB], 4, SUB),
                                  lanes(recd3[:, 4 * i:4 * i + 4, D_DL32], 4, SUB), ALU.not_equal))
            V.after(reduced2[4 * i + 3])
            lg = lg4[:, 4 * (i % 2):4 * (i % 2) + 4, :]
            chain(v.tensor_tensor(lg, lg, red4[:, 4 * (i % 2):4 * (i % 2) + 4, :], ALU.add))
            logits[i] = V.did(v.scalar_tensor_tensor(out=alpha[:, 4 * i:4 * i + 4, :], in0=lg, scalar=0.2, in1=lg,
                                                     op0=ALU.mult, op1=ALU.max))
            V.after(logits[i], mtop.get(4 * i - 1))
            for k in range(4):
                masked[4 * i + k] = V.did(v.scalar_tensor_tensor(
                    out=spread[:, k, :].rearrange("p (h n) -> p h n", h=H), in0=rows(miss[:, k, :], H, SUB),
                    scalar=-BIG, in1=lanes(alpha[:, 4 * i + k, :], H, SUB), op0=ALU.mult, op1=ALU.add))

        made = Marks()
        reduced2 = Marks()

        def turn_masked(c):
            T.after(masked[c], maxed.get(c // 4 - 1))
            for k in range(2):
                ins = pe.transpose(ps[6 + c % 4 // 2][:, (2 * (c % 2) + k) * P:(2 * (c % 2) + k + 1) * P],
                                   spread[:, c % 4, k * P:(k + 1) * P], ident)
            mtop[c] = T.did(ins)

        def node_max(i):
            for k in range(2):
                V.after(mtop[4 * i + 2 * k + 1], m_top, kept.get(4 * i - 5))
                maxed[i] = V.did(v.tensor_reduce(mx[:, i % 2, 4 * k:4 * k + 4],
                                                 ps[6 + k].rearrange("p (k e) -> p k e", e=P), AX.X, ALU.max))

        def keep_max(c):
            V.after(maxed[c // 4], V.last() if c % 4 == 0 else None, kept.get(c - 1))
            here = small[:, bass.ds(b32_v.at(c) * 2, 2)]
            kept[c] = V.did(v.tensor_tensor(here, here, mx[:, c // 4 % 2, 2 * (c % 4):2 * (c % 4) + 2], ALU.max))

        kept = Marks()

        def four(stage):
            def all4(i):
                for c in range(4 * i, 4 * i + 4):
                    stage(c)
            return all4

        def turns(i):
            turn_records(4 * i)
            turn_one_hots(i, oh2[i % 2], hd_at.get(4 * i - 5), rk2[i // 4])

        pipeline(NCD, (0, gather), (3, spill_rows), (2, every(4, one_hot4x, 0)), (4, every(4, turns, 0)),
                 (8, node_and_edge_parts), (9, edge_product), (10, edge_dot), (11, every(4, edge_logits, 3)),
                 (13, every(4, four(turn_masked), 3)), (15, every(4, node_max, 3)), (19, keep_max))
        barrier()

        top4 = top.rearrange("p (b s k) -> p b s k", s=4, k=2)
        top_t4 = top_t.rearrange("p (b k q) -> p b k q", k=2, q=4)
        for q in range(4):
            for s in range(4):
                V.did(v.tensor_copy(top_t4[s * SUB:(s + 1) * SUB, :, :, q], top4[q * SUB:(q + 1) * SUB, :, s, :]))
        m_top = V.last()
        m_zero = V.did(v.memset(hsrc, 0.0))
        RB = 16
        hs = cut(acc, NB * TW + 2048, RB * D, RB, D)
        spill += [landing(f"spill{i}") for i in range(R3, RB)]
        o = 0
        oh2_t = cut(ring, o, 8 * P, 8, P)
        o += 8 * P
        msg = cut(ring, o, 8 * TW, 8, TW)
        o += 8 * TW
        below = cut(ring, o, 8 * H, 8, H)
        assert o + 8 * H <= ring.shape[1]
        oh3 = [cut(acc, NB * TW + k * 512, 512, 4, P) for k in range(4)]
        back = Marks()
        hot2.clear(), oht.clear(), ohk.clear()
        tops, lows, exps, msgs, sum2, added2 = Marks(), Marks(), Marks(), Marks(), Marks(), Marks()
        blk_v.first = blk_t.first = None

        def read_rows(c):
            S.after(msgs.get(c - RB))
            back[c] = spill[c % RB].started(sp.dma_start(hs[:, c % RB, :], rows_spill[c]))

        def one_hot_b(i):
            V.after(sum2.get(4 * i - 13))
            hot2[i] = V.did(v.tensor_tensor(oh3[i % 4], rows(iota, 4, P),
                                            lanes(recd3[:, 4 * i:4 * i + 4, D_DL], 4, P), ALU.is_equal))

        def gather_tops(c):
            T.after(ohk[c // 4], lows.get(c // 4 - 2), m_top)
            tops[c] = T.did(pe.matmul(ps[2 + c // 4 % 2][:, (c % 4) * H:(c % 4 + 1) * H], oh2_t[:, c % 8, :],
                                      small[:, bass.ds(blk_t.at(c) * H + 2 * NBD, H)], start=True, stop=True))

        def exponents(i):
            low = below[:, 4 * (i % 2):4 * (i % 2) + 4, :]
            V.after(tops[4 * i + 3], exps.get(i - 2))
            lows[i] = V.did(v.tensor_tensor(low, alpha[:, 4 * i:4 * i + 4, :],
                                            ps[2 + i % 2][:, 0:4 * H].rearrange("p (c h) -> p c h", h=H),
                                            ALU.subtract))
            V.after(lows[i])
            m = V.did(v.tensor_scalar(low, low, 0.0, None, ALU.min))
            A.after(m, sum2.get(4 * i - 5))
            exps[i] = A.did(a.activation(msg[:, 4 * (i % 2):4 * (i % 2) + 4, D:TW], low, ACT.Exp))

        def weighted(c):
            V.after(exps[c // 4], back[c], sum2.get(c - 8))
            msgs[c] = V.did(v.tensor_tensor(msg[:, c % 8, 0:D].rearrange("p (h d) -> p h d", h=H),
                                            hs[:, c % RB, :].rearrange("p (h d) -> p h d", h=H),
                                            lanes(msg[:, c % 8, D:TW], H, HD), ALU.mult))

        def sum_messages(c):
            T.after(msgs[c], added2.get(c - 4))
            sum2[c] = T.did(pe.matmul(ps[4 + c % 4][:, 0:TW], oh3[c // 4 % 4][:, c % 4, :], msg[:, c % 8, :],
                                      start=True, stop=True))

        def add_messages(c):
            V.after(sum2[c], added2.get(c - 1), m_zero)
            here = acc[:, bass.ds(blk_v.at(c) * TW, TW)]
            added2[c] = V.did(v.tensor_tensor(here, here, ps[4 + c % 4][:, 0:TW], ALU.add))

        def turns_b(i):
            turn_one_hots(i, oh3[i % 4], tops.get(4 * i - 5))

        pipeline(NCD, (0, read_rows), (0, every(4, one_hot_b, 0)), (2, every(4, turns_b, 0)), (3, gather_tops),
                 (5, every(4, exponents, 3)), (10, weighted), (10, sum_messages), (13, add_messages))
        V.after(V.last())
        den = ring[:, 0:NB * H].rearrange("p (b h) -> p b h", h=H)
        barrier()
        chain(v.tensor_scalar(den, hsrc[:, :, D:TW], 1e-10, None, ALU.max))
        chain(v.reciprocal(den, den))
        for b in range(NB):
            o2 = hsrc[:, b, 0:D]
            m = V.did(v.tensor_tensor(o2.rearrange("p (h d) -> p h d", h=H), o2.rearrange("p (h d) -> p h d", h=H),
                                      lanes(den[:, b, :], H, HD), ALU.mult))
            V.did(v.tensor_tensor(x3[:, b, :], x3[:, b, :], bias, ALU.add))
            V.after(V.last())
            V.did(v.tensor_tensor(x3[:, b, :], x3[:, b, :], o2, ALU.add))
        layernorm()
        barrier()

        w3, b3 = cut(wts, 0, 512, 2, D), wts[:, 512:512 + D]
        load(w3, two("L3_gnn_W"))
        m_weights = load(b3, everywhere("L3_gnn_b", D))
        dinv = small[:, 0:NB]
        scaled = cut(big, 0, NB * D, NB, D)
        chain(v.tensor_scalar(dinv, deg_d[:, NB:2 * NB], 1.0, None, ALU.add))
        rsqrt_of(dinv, V.last())
        T.after(m_weights)
        V.after(m_weights)

        def scale_rows(b, product):
            chain(v.tensor_tensor(scaled[:, b, :], product, b3, ALU.add))
            return chain(v.tensor_scalar(scaled[:, b, :], scaled[:, b, :], dinv[:, b:b + 1], None, ALU.mult))

        linear(x3, w3, scale_rows)
        m_table = write_table(scaled_table, scaled, V.last())
        m_zero = V.did(v.memset(acc0, 0.0))
        R4 = 12
        gather, sg, got4 = gather_rows(scaled_table, D, lambda c: idx_s[:, c:c + 1], R4,
                                       lambda c: [m_table, sum4.get(c - R4)])
        oh4 = cut(ring, R4 * D, 4 * P, 4, P)
        sum4, oh4_at, added4 = Marks(), Marks(), Marks()
        blk_s.first = None

        def one_hot4(c):
            V.after(sum4.get(c - 4))
            oh4_at[c] = V.did(v.tensor_scalar(oh4[:, c % 4, :], iota, sl_s[:, c:c + 1], None, ALU.is_equal))

        def sums4(c):
            u = c // GS
            T.after(oh4_at[c], got4[c], added4.get(u - 4) if c % GS == 0 else None)
            sum4[c] = T.did(pe.matmul(ps[4 + u % 4][:, 0:D], oh4[:, c % 4, :], sg[:, c % R4, :],
                                      start=(c % GS == 0), stop=(c % GS == GS - 1)))

        def add4(c):
            if c % GS == GS - 1:
                u = c // GS
                V.after(sum4[c], added4.get(u - 1), m_zero)
                here = acc[:, bass.ds(blk_s.at(u) * D, D)]
                added4[u] = V.did(v.tensor_tensor(here, here, ps[4 + u % 4][:, 0:D], ALU.add))

        barrier()
        pipeline(NCS, (0, gather), (5, one_hot4), (6, sums4), (8, add4))
        barrier()
        for b in range(NB):
            m = V.did(v.tensor_tensor(acc0[:, b, :], acc0[:, b, :], scaled[:, b, :], ALU.add))
            V.after(m)
            V.did(v.scalar_tensor_tensor(out=x3[:, b, :], in0=acc0[:, b, :], scalar=dinv[:, b:b + 1],
                                         in1=x3[:, b, :], op0=ALU.mult, op1=ALU.add))
        m = layernorm()
        S.after(m)
        stored = landing("stored")
        stored.started(sp.dma_start(out[0:(NB - 1) * P, :].rearrange("(b p) k -> p b k", p=P), x3[:, 0:NB - 1, :]))
        S.after(stored.started(sp.dma_start(out[(NB - 1) * P:N, :], x3[0:LAST, NB - 1, :])))
        barrier()


_INS = ['x', 'src', 'dst', 'edge_attr_3', 'edge_attr_4', 'edge_attr_8', 'edge_weight', 'L0_gnn_W6', 'L0_gnn_b6',
        'L0_gnn_W7', 'L0_gnn_b7', 'L0_gnn_Wp', 'L0_gnn_bp', 'L1_gnn_w1_s', 'L1_gnn_w1_v', 'L1_gnn_wsc_s',
        'L1_gnn_wsc_v', 'L1_gnn_w2_s', 'L1_gnn_w2_v', 'L1_gnn_fc_w1', 'L1_gnn_fc_w2', 'L1_gnn_fc_w3', 'L1_gnn_g_s',
        'L1_gnn_g_v', 'L2_gnn_W', 'L2_gnn_a_src', 'L2_gnn_a_dst', 'L2_gnn_edge_W', 'L2_gnn_edge_b', 'L2_gnn_bias',
        'L3_gnn_W', 'L3_gnn_b']


def kernel(**inputs):
    import concourse.bacc as bacc
    from concourse.bass_utils import run_bass_kernel_spmd

    nc = bacc.Bacc("TRN2", target_bir_lowering=False, num_devices=1)
    arrays, tensors = Marks(), Marks()
    for name in _INS:
        arr = np.ascontiguousarray(inputs[name])
        arrays[f"in_{name}"] = arr
        tensors[name] = nc.dram_tensor(f"in_{name}", arr.shape, mybir.dt.from_np(arr.dtype), kind="ExternalInput").ap()
    result = nc.dram_tensor("result", (N, D), F32, kind="ExternalOutput").ap()
    program(nc, tensors, result)
    r = run_bass_kernel_spmd(nc, [arrays], core_ids=[0])
    return r.results[0]["result"]
```

```python
from contextlib import ExitStack

import numpy as np
import concourse.bass as bass
from concourse import mybir

F32, I32 = mybir.dt.float32, mybir.dt.int32
ALU, ACT, AX = mybir.AluOpType, mybir.ActivationFunctionType, mybir.AxisListType

P = 128
N, E, D = 3125, 100000, 256
NB = -(-N // P)
NPAD = NB * P
LAST = N - (NB - 1) * P
EP = 125
EJ = E // EP
SUB = 32
NBD = NPAD // SUB
H, HD = 8, 32
MUL = 64


def up(n, m):
    return -(-n // m) * m


NCD = up((E + (P - 1) * -(-N // SUB)) // P, 16)
GS = 2
NUS = up((E + (GS * P - 1) * NB) // (GS * P), 16)
NCS = NUS * GS
RD, RS = 8, 16
D_IDX, D_DL, D_W, D_EA, D_ONE, D_DL32 = 0, 1, 2, 3, 6, 7
S_IDX, S_SL, S_SH, S_EA = 0, 1, 2, 6
TW = D + H
BIG = float(2.0 ** 100)
EPS0, EPS1 = 1e-12, 1e-5


class Queue:

    def __init__(self, eng, sem):
        self.eng, self.sem, self.count, self.waited = eng, sem, 0, {}

    def after(self, *marks):
        for m in marks:
            if m is None:
                continue
            if isinstance(m, list):
                self.after(*m)
                continue
            sem, value = m
            if self.waited.get(id(sem), 0) < value:
                self.eng.wait_ge(sem, value)
                self.waited[id(sem)] = value

    def did(self, ins):
        ins.then_inc(self.sem, 1)
        self.count += 1
        return self.sem, self.count

    def last(self):
        return (self.sem, self.count) if self.count else None


class Marks(dict):

    def get(self, i):
        return None if i < 0 else self[i]


class Landing:

    def __init__(self, sem):
        self.sem, self.count = sem, 0

    def started(self, ins):
        ins.then_inc(self.sem, 16)
        self.count += 16
        return self.sem, self.count


def pipeline(n, *stages):
    for i in range(n + max(lag for lag, _ in stages)):
        for lag, f in stages:
            if 0 <= i - lag < n:
                f(i - lag)


def program(nc, t, out):
    with ExitStack() as ctx:
        def sem(name):
            return ctx.enter_context(nc.semaphore(name))

        V, A = Queue(nc.vector, sem("vector_done")), Queue(nc.scalar, sem("scalar_done"))
        T, G = Queue(nc.tensor, sem("tensor_done")), Queue(nc.gpsimd, sem("pool_done"))
        S = Queue(nc.sync, sem("sync_done"))
        v, a, pe, g, sp = V.eng, A.eng, T.eng, G.eng, S.eng
        landings = []

        def landing(name):
            landings.append(Landing(sem(name)))
            return landings[-1]

        def barrier():
            marks = [q.last() for q in (V, A, T, G)] + [(x.sem, x.count) for x in landings if x.count]
            for q in (V, A, T, G, S):
                q.after(*marks)

        def dram(name, shape, dt=F32):
            return nc.dram_tensor(name, shape, dt, kind="Internal").ap()

        def sb(name, width, dt=F32, parts=P):
            return ctx.enter_context(nc.sbuf_tensor(name, [parts, width], dt))[:, :]

        ps = [ctx.enter_context(nc.psum_tensor(f"bank{i}", [P, 512], F32))[:, :] for i in range(8)]

        rec_d_dram, rec_s_dram = dram("rec_d", (P * NCD, RD)), dram("rec_s", (P * NCS, RS))
        x_table, h6_table = dram("x_table", (NPAD, TW)), dram("h6_table", (NPAD, D))
        y_table, att_table = dram("y_table", (NPAD, D)), dram("att_table", (NPAD, TW))
        scaled_table = dram("scaled_table", (NPAD, D))
        rows_spill = dram("rows_spill", (NCD, P, D))
        weights_dram = dram("weights_dram", (NCS, P, D))
        din_dram = dram("din_dram", (NB, P))
        ew_dram = dram("ew_dram", (4, D))
        JD, JS = up(NCD, P) // P, up(NUS, P) // P
        b32_dram, blk_d_dram = dram("b32_dram", (P, JD), I32), dram("blk_d_dram", (P, JD), I32)
        blk_s_dram = dram("blk_s_dram", (P, JS), I32)

        ident, iota = sb("ident", P), sb("iota", P)
        lane = sb("lane", 1)
        rec_d = sb("rec_d_sb", NCD * RD)
        big = sb("big", max(NCS * RS, NCD * H + NB * TW))
        acc = sb("acc", NB * 512)
        x = sb("x_res", NB * D)
        norm = sb("norm", NCD)
        idx_s, sl_s = sb("idx_s", NCS, I32), sb("sl_s", NCS)
        deg_d, deg_s = sb("deg_d", 2 * NB), sb("deg_s", 2 * NB)
        unit_numbers = sb("unit_numbers", P * JD, I32, 3)
        b32_row, blk_d_row, blk_s_row = (unit_numbers[k:k + 1, :] for k in range(3))
        ring = sb("ring", 6100)
        wts = sb("wts", 2432)
        small = sb("small", 800)

        x3 = x.rearrange("p (b k) -> p b k", b=NB)
        recd3 = rec_d.rearrange("p (c r) -> p c r", r=RD)
        recd3i = rec_d.bitcast(I32).rearrange("p (c r) -> p c r", r=RD)

        def cut(buf, at, n, *dims):
            r = buf[:, at:at + n]
            if len(dims) == 2:
                r = r.rearrange("p (a b) -> p a b", a=dims[0])
            if len(dims) == 3:
                r = r.rearrange("p (a b c) -> p a b c", a=dims[0], b=dims[1])
            return r

        def lanes(col, n, k):
            return col.rearrange("p (n o) -> p n o", o=1).to_broadcast([col.shape[0], n, k])

        def rows(row, n, k):
            return row.rearrange("p (o k) -> p o k", o=1).to_broadcast([row.shape[0], n, k])

        class Numbers:
            def __init__(self, q, name, row, top):
                self.q, self.row, self.top = q, row, top
                self.regs = [q.eng.alloc_register(f"{name}{i}") for i in range(16)]
                self.first = None

            def at(self, i):
                if self.first != i // 16:
                    self.first = i // 16
                    self.q.eng.load(self.regs, self.row[0:1, self.first * 16:self.first * 16 + 16])
                return self.q.eng.snap(self.regs[i % 16], min_val=0, max_val=self.top)

        load_in, prefilled = landing("load_in"), landing("prefilled")
        s_w = landing("weights_in")

        def load(buf, src, slot=s_w):
            return slot.started(sp.dma_start(buf, src))

        m_iota = G.did(g.iota(iota, [[1, P]], base=0, channel_multiplier=0, allow_small_or_imprecise_dtypes=True))
        m_lane = G.did(g.iota(lane, [[0, 1]], base=0, channel_multiplier=1, allow_small_or_imprecise_dtypes=True))
        V.after(m_iota, m_lane)
        m_ident = V.did(v.tensor_scalar(ident, iota, lane[:, 0:1], None, ALU.is_equal))

        pad_s = big[:, 0:NCS * RS]
        m0 = G.did(g.memset(rec_d, 0.0))
        m1 = G.did(g.memset(pad_s, 0.0))
        G.after(m0, m1)
        for col in (D_DL, D_DL32):
            G.did(g.memset(recd3[:, :, col], -1.0))
        m_pad = G.did(g.memset(pad_s.rearrange("p (c r) -> p c r", r=RS)[:, :, S_SL], -1.0))
        src_i, src_in = idx_s[0:EP, 0:EJ], landing("src_in")
        m_src = src_in.started(sp.dma_start(src_i, t["src"].rearrange("(p j) -> p j", p=EP)))
        S.after(m_pad)
        prefilled.started(sp.dma_start(rec_d_dram.rearrange("(p c) r -> p (c r)", p=P), rec_d))
        m_prefilled = prefilled.started(sp.dma_start(rec_s_dram.rearrange("(p c) r -> p (c r)", p=P), pad_s))

        S.after(m_prefilled)
        at = [0]

        def raw(width):
            r = big[0:EP, at[0]:at[0] + width]
            at[0] += width
            assert at[0] <= big.shape[1]
            return r

        dst_i, w_raw = raw(EJ).bitcast(I32), raw(EJ)
        ea3_raw, ea4_raw, ea8_raw = raw(EJ * 3), raw(EJ * 4), rec_d[0:EP, 0:EJ * 8]
        for buf, name in ((dst_i, "dst"), (w_raw, "edge_weight")):
            load_in.started(sp.dma_start(buf, t[name].rearrange("(p j) -> p j", p=EP)))
        for buf, name in ((ea4_raw, "edge_attr_4"), (ea8_raw, "edge_attr_8"), (ea3_raw, "edge_attr_3")):
            m_raw = load_in.started(sp.dma_start(buf, t[name].rearrange("(p j) k -> p (j k)", p=EP)))
        buckets, scan, pos = sl_s[0:EP, 0:EJ], norm[0:EP, 0:EJ], wts[0:EP, 0:EJ]
        tmp_i = wts[0:EP, EJ:2 * EJ].bitcast(I32)
        lo_bufs = [cut(raw(1024), 0, 1024, 8, P) for _ in range(2)]
        hit = ring[0:EP, 0:EJ].bitcast(I32)
        stage_s = acc[0:EP, 0:EJ * RS].rearrange("p (j r) -> p j r", r=RS)
        stage_d = x[0:EP, 0:EJ * RD].rearrange("p (j r) -> p j r", r=RD)
        before = ring[0:EP, 5900:5900 + P]
        ones = small[0:EP, 0:P]
        zero = small[0:EP, P:P + 1]
        V.after(m_ident, m_src)
        A.after(m_raw)
        V.did(v.tensor_scalar(before, iota[0:EP, :], lane[0:EP, 0:1], None, ALU.is_gt))
        V.did(v.memset(ones, 1.0))
        V.did(v.memset(zero, 0.0))

        def chain(ins):
            m = V.did(ins)
            V.after(m)
            return m

        def field(out_f, key, shift, mask):
            chain(v.tensor_scalar(tmp_i, key, shift, mask, ALU.logical_shift_right, ALU.bitwise_and))
            return chain(v.tensor_copy(out_f, tmp_i))

        ea4_3, ea8_3 = (ea4_raw.rearrange("p (j k) -> p j k", k=4), ea8_raw.rearrange("p (j k) -> p j k", k=8))
        ea3_3 = ea3_raw.rearrange("p (j k) -> p j k", k=3)
        m_attr_s = [A.did(a.copy(stage_s[:, :, S_SH:S_SH + 4], ea4_3)),
                    A.did(a.copy(stage_s[:, :, S_EA:S_EA + 8], ea8_3))]
        m_attr_d = [A.did(a.copy(stage_d[:, :, D_EA:D_EA + 3], ea3_3)),
                    A.did(a.copy(stage_d[:, :, D_W], w_raw))]

        def stage_keys():
            V.after(m_raw)
            V.did(v.memset(stage_s[:, :, 14:16], 0.0))
            V.did(v.memset(stage_d[:, :, D_ONE], 1.0))
            V.did(v.tensor_copy(stage_s.bitcast(I32)[:, :, S_IDX], dst_i))
            V.did(v.tensor_copy(stage_d.bitcast(I32)[:, :, D_IDX], src_i))
            field(stage_s[:, :, S_SL], src_i, 0, P - 1)
            field(stage_d[:, :, D_DL], dst_i, 0, P - 1)
            return field(stage_d[:, :, D_DL32], dst_i, 0, SUB - 1)

        tot, off = ring[0:EP, 900:1000], ring[0:EP, 1000:1100]
        units, ends = ring[:, 1100:1200], ring[:, 1200:1300]
        units_i = ring[:, 1300:1400].bitcast(I32)
        counted = ring[:, 1400:1400 + JD * NBD]
        unit_of = {j: ring[:, 2200 + 16 * k:2200 + 16 * k + j] for k, j in enumerate((JS, JD))}
        for j, number in unit_of.items():
            m_number = G.did(g.iota(number, [[1, j]], base=0, channel_multiplier=j,
                                    allow_small_or_imprecise_dtypes=True))
        bucket_of, bucket_i = ring[:, 2300:2300 + JD], ring[:, 2400:2400 + JD].bitcast(I32)
        block_i = ring[:, 2500:2500 + JD].bitcast(I32)

        def rank(key, shift, nb, unit_chunks, chunks, slot_row):
            unit = unit_chunks * P
            field(buckets, key, shift, (1 << 20) - 1)
            for b in range(nb):
                chain(v.tensor_scalar(scan, buckets, float(b), 0.0, ALU.is_equal, ALU.add,
                                      accum_out=tot[:, b:b + 1]))
            T.after(V.last())
            T.did(pe.matmul(ps[0][:, 0:nb], before, tot[:, 0:nb], start=True, stop=True))
            m = T.did(pe.matmul(ps[1][:, 0:nb], small[0:EP, 0:P], tot[:, 0:nb], start=True, stop=True))
            V.after(m)
            chain(v.tensor_scalar(units_i[:, 0:nb], ps[1][:, 0:nb], float(unit - 1), None, ALU.add))
            chain(v.tensor_scalar(units_i[:, 0:nb], units_i[:, 0:nb], unit.bit_length() - 1, None,
                                  ALU.logical_shift_right))
            chain(v.tensor_copy(units[:, 0:nb], units_i[:, 0:nb]))
            chain(v.tensor_tensor_scan(ends[:, 0:nb], units[:, 0:nb], small[:, P + 1:P + 2].to_broadcast([P, nb]),
                                       0.0, ALU.add, ALU.add))
            chain(v.tensor_tensor(off[:, 0:nb], ends[0:EP, 0:nb], units[0:EP, 0:nb], ALU.subtract))
            chain(v.tensor_scalar(off[:, 0:nb], off[:, 0:nb], float(unit), -1.0, ALU.mult, ALU.add))
            chain(v.tensor_tensor(off[:, 0:nb], off[:, 0:nb], ps[0][0:EP, 0:nb], ALU.add))
            for b in range(nb):
                chain(v.tensor_scalar(hit, buckets, float(b), None, ALU.is_equal))
                chain(v.tensor_tensor_scan(scan, hit, zero.to_broadcast([EP, EJ]), off[:, b:b + 1],
                                           ALU.add, ALU.add))
                chain(v.copy_predicated(pos, hit, scan))
            chain(v.tensor_copy(tmp_i, pos))
            chain(v.tensor_scalar(hit, tmp_i, P - 1, None, ALU.bitwise_and))
            chain(v.tensor_scalar(tmp_i, tmp_i, 7, None, ALU.logical_shift_right))
            chain(v.tensor_copy(scan, hit))
            chain(v.tensor_copy(pos, tmp_i))
            return chain(v.scalar_tensor_tensor(out=slot_row, in0=scan, scalar=float(chunks), in1=pos,
                                                op0=ALU.mult, op1=ALU.add))

        def bucket_numbers(nb, j):
            number = unit_of[j]
            V.after(m_number)
            c3 = counted[:, 0:j * nb].rearrange("p (j b) -> p j b", j=j)
            chain(v.tensor_tensor(c3, rows(ends[:, 0:nb], j, nb), lanes(number, j, nb), ALU.is_le))
            chain(v.tensor_reduce(bucket_of[:, 0:j], c3, AX.X, ALU.add))
            return chain(v.tensor_scalar(bucket_i[:, 0:j], bucket_of[:, 0:j], float(nb - 1), None, ALU.min))

        chain(v.memset(small[:, P + 1:P + 2], 0.0))
        chain(v.memset(pos, 0.0))
        numbers_out, numbers_in = landing("numbers_out"), landing("numbers_in")
        scattered_s, scattered_d = landing("scattered_s"), landing("scattered_d")
        row_s, row_d = ring[0:EP, 2600:2600 + EJ].bitcast(I32), ring[0:EP, 3400:3400 + EJ].bitcast(I32)

        def scatter(row, stage, table, where, *marks):
            G.after(*marks)
            for j in range(EJ):
                m = where.started(g.indirect_dma_start(
                    out=table, out_offset=bass.IndirectOffsetOnAxis(ap=row[:, j:j + 1], axis=0),
                    in_=stage[:, j, :], in_offset=None))
            return m

        def keep_numbers(buf, table, row, n):
            S.after(V.last())
            m = numbers_out.started(sp.dma_start(table, buf))
            S.after(m)
            return numbers_in.started(sp.dma_start(row[0:1, 0:n], table.rearrange("(o p) j -> o (p j)", o=1)))

        m_row_s = rank(src_i, 7, NB, GS, NCS, row_s)
        m_keys = stage_keys()
        bucket_numbers(NB, JS)
        keep_numbers(bucket_i[:, 0:JS], blk_s_dram, blk_s_row, P * JS)
        m_scattered_s = scatter(row_s, stage_s, rec_s_dram, scattered_s, m_prefilled, m_keys, m_attr_s, m_row_s)
        m_row_d = rank(dst_i, 5, NBD, 1, NCD, row_d)
        V.after((numbers_out.sem, numbers_out.count))
        bucket_numbers(NBD, JD)
        chain(v.tensor_scalar(block_i, bucket_i, 2, None, ALU.logical_shift_right))
        keep_numbers(bucket_i, b32_dram, b32_row, P * JD)
        m_numbers = keep_numbers(block_i, blk_d_dram, blk_d_row, P * JD)
        m_scattered_d = scatter(row_d, stage_d, rec_d_dram, scattered_d, m_attr_d, m_row_d)

        BJ, DIN = 8, 9600
        low_f, high_f = buckets, scan
        for key, deg, bank in ((src_i, deg_s, 2), (dst_i, deg_d, 3)):
            field(low_f, key, 0, P - 1)
            field(high_f, key, 7, (1 << 20) - 1)
            used = [None, None]
            hi_bufs = [cut(ring[0:EP], 4300 + k * 2 * NB * BJ, 2 * NB * BJ, BJ, 2 * NB) for k in range(2)]
            for i in range(EJ // BJ):
                lo3, hi3, js = lo_bufs[i % 2], hi_bufs[i % 2], slice(i * BJ, i * BJ + BJ)
                V.after(used[i % 2])
                V.did(v.tensor_tensor(lo3, rows(iota[0:EP, :], BJ, P), lanes(low_f[:, js], BJ, P), ALU.is_equal))
                m = V.did(v.tensor_tensor(hi3[:, :, NB:2 * NB], rows(iota[0:EP, 0:NB], BJ, NB),
                                          lanes(high_f[:, js], BJ, NB), ALU.is_equal))
                V.after(m)
                m = V.did(v.tensor_tensor(hi3[:, :, 0:NB], hi3[:, :, NB:2 * NB], lanes(w_raw[:, js], BJ, NB),
                                          ALU.mult))
                T.after(m)
                for k in range(BJ):
                    j = i * BJ + k
                    ins = pe.matmul(ps[bank][:, 0:2 * NB], lo3[:, k, :], hi3[:, k, :], start=(j == 0),
                                    stop=(j == EJ - 1))
                used[i % 2] = T.did(ins)
            V.after(T.last())
            m_deg = chain(v.tensor_copy(deg, ps[bank][:, 0:2 * NB]))

        o = 0
        rec_b = cut(acc, o, 3 * P, 3, P)
        o += 3 * P
        rec_t = cut(acc, o, 2 * P, 2, P)
        o += 2 * P
        h1 = cut(acc, o, 2 * 512, 2, 512)
        o += 2 * 512
        h2 = cut(acc, o, 2 * 512, 2, 512)
        o += 2 * 512
        RW = 16
        w_out = cut(acc, o, RW * D, RW, D)
        o += RW * D
        fc1 = cut(acc, o, 512, 4, P)
        o += 512
        fc2, fc3 = acc[:, o:o + P], acc[:, o + P:o + P + D]
        o += P + D
        assert o <= DIN
        fc_in = landing("fc_in")
        S.after(m_scattered_s)
        V.after(m_scattered_s)
        S.after(V.did(v.memset(acc[:, o - 512 - P - D:o], 0.0)))
        for k in range(8):
            load(fc1[k * RS + S_EA:k * RS + S_EA + 8, k // 2, (k % 2) * MUL:(k % 2) * MUL + MUL], t["L1_gnn_fc_w1"],
                 fc_in)
        for k in range(2):
            load(fc2[k * MUL:(k + 1) * MUL, k * MUL:(k + 1) * MUL], t["L1_gnn_fc_w2"], fc_in)
            for to, part in enumerate((0, 2, 3, 1)):
                m_fc = load(fc3[k * MUL:(k + 1) * MUL, to * MUL:(to + 1) * MUL],
                            t["L1_gnn_fc_w3"][:, part * MUL:(part + 1) * MUL], fc_in)
        V.after(m_fc)
        chain(v.tensor_scalar(fc3, fc3, 0.125, None, ALU.mult))
        T.after(chain(v.tensor_scalar(fc3[:, 2 * MUL:3 * MUL], fc3[:, 2 * MUL:3 * MUL], 0.5773502691896258, None,
                                      ALU.mult)))
        rec_b_in = [landing(f"rec_b_in{k}") for k in range(3)]
        w_stored = [landing(f"w_stored{k}") for k in range(2)]
        rb, c_rt, c_rk, c_1, c_s1, c_2, c_s2, w_at, w_kept, w_gone = (Marks() for _ in range(10))

        def read_records(i):
            S.after(c_rt.get(i - 3), w_kept.get(8 * (i - 3) + 7))
            rb[i] = rec_b_in[i % 3].started(sp.dma_start(
                rec_b[:, i % 3, :], rec_s_dram.rearrange("(p c) r -> p (c r)", p=P)[:, i * P:(i + 1) * P]))

        def mlp_in(i):
            T.after(rb[i], c_rk.get(i - 1))
            c_rt[i] = T.did(pe.transpose(ps[0][:, 0:P], rec_b[:, i % 3, :], ident))
            A.after(c_rt[i], c_1.get(i - 2))
            c_rk[i] = A.did(a.copy(rec_t[:, i % 2, :], ps[0][:, 0:P]))

        def mlp_1(i):
            T.after(c_rk[i], c_s1.get(i - 1))
            for j in range(4):
                ins = pe.matmul(ps[1][:, j * P:(j + 1) * P], fc1[:, j, :], rec_t[:, i % 2, :], start=True, stop=True)
            c_1[i] = T.did(ins)
            A.after(c_1[i], c_2.get(i - 2))
            c_s1[i] = A.did(a.activation(h1[:, i % 2, :], ps[1], ACT.Silu, scale=float(1.0 / np.sqrt(8.0))))

        def mlp_2(i):
            T.after(c_s1[i], c_s2.get(i - 1))
            c_2[i] = T.did(pe.matmul(ps[4], fc2, h1[:, i % 2, :], start=True, stop=True))
            A.after(c_2[i], w_at.get(8 * (i - 2) + 7))
            c_s2[i] = A.did(a.activation(h2[:, i % 2, :], ps[4], ACT.Silu, scale=0.125))

        def edge_weights(c):
            i, k = c // 8, c % 8
            half = slice((k % 2) * MUL, (k % 2) * MUL + MUL)
            T.after(c_s2[i], w_kept.get(c - 3))
            w_at[c] = T.did(pe.matmul(ps[5 + c % 3][:, 0:D], h2[half, i % 2, (k // 2) * P:(k // 2) * P + P],
                                      fc3[half, :], start=True, stop=True))
            A.after(w_at[c], rb[i], w_gone.get(c // 8 - 2))
            A.did(a.mul(w_out[:, c % RW, 0:2 * MUL], ps[5 + c % 3][:, 0:2 * MUL],
                        rec_b[:, i % 3, k * RS + S_SH:k * RS + S_SH + 1]))
            w_kept[c] = A.did(a.copy(w_out[:, c % RW, 2 * MUL:D], ps[5 + c % 3][:, 2 * MUL:D]))

        def store_weights(i):
            S.after(w_kept[8 * i + 7])
            w_gone[i] = w_stored[i % 2].started(sp.dma_start(
                weights_dram[8 * i:8 * i + 8].rearrange("c p k -> p c k"), w_out[:, 8 * (i % 2):8 * (i % 2) + 8, :]))

        def every(n, stage, k):
            return lambda c: stage(c // n) if c % n == k else None

        pipeline(NCS, (0, every(8, read_records, 0)), (5, every(8, mlp_in, 0)), (7, every(8, mlp_1, 0)),
                 (10, every(8, mlp_2, 0)), (14, edge_weights), (15, every(8, store_weights, 7)))
        din_t, din_row = ring[0:NB, 5200:5200 + P], acc[:, DIN:DIN + NPAD]
        T.after(m_deg)
        m = T.did(pe.transpose(ps[4][0:NB, 0:P], deg_d[:, 0:NB], ident))
        V.after(m)
        m = chain(v.tensor_copy(din_t, ps[4][0:NB, 0:P]))
        S.after(m)
        din_out, din_in = landing("din_out"), landing("din_in")
        m = din_out.started(sp.dma_start(din_dram, din_t))
        S.after(m, m_scattered_s)
        m_din = din_in.started(sp.dma_start(
            din_row, din_dram.rearrange("(o b) p -> o (b p)", o=1).to_broadcast([P, NPAD])))
        barrier()

        x_in, rec_in = landing("x_in"), landing("rec_in")
        table_out = landing("table_out")
        stats = ring[:, 5000:5000 + NB * 6].rearrange("p (b s) -> p b s", s=6)
        mv = ring[:, 5200:5200 + NB * 2].rearrange("p (b s) -> p b s", s=2)
        rstd = ring[:, 5300:5300 + NB]

        def rsqrt_of(buf, mark):
            A.after(mark)
            m = A.did(a.activation(buf, buf, ACT.Sqrt))
            V.after(m)
            return chain(v.reciprocal(buf, buf))

        def layernorm():
            V.after(V.last())
            for b in range(NB):
                V.did(v.bn_stats(stats[:, b, :], x3[:, b, :]))
            V.after(V.last())
            for b in range(NB):
                V.did(v.bn_aggr(mv[:, b, :], stats[:, b, :]))
            V.after(V.last())
            m = chain(v.tensor_scalar(rstd, mv[:, :, 1], EPS1, None, ALU.add))
            rsqrt_of(rstd, m)
            for b in range(NB):
                V.did(v.tensor_scalar(x3[:, b, :], x3[:, b, :], mv[:, b, 0:1], rstd[:, b:b + 1],
                                      ALU.subtract, ALU.mult))
            return V.last()

        def write_table(table, view, mark):
            S.after(mark)
            return table_out.started(sp.dma_start(table.rearrange("(b p) k -> p b k", p=P), view))

        def linear(view, weight, finish):
            turned = cut(ring, 0, 1024, 4, 256)
            cols, done, prod, fin = Marks(), Marks(), Marks(), Marks()

            def turn(b):
                T.after(cols.get(b - 4))
                for k in range(2):
                    ins = pe.transpose(ps[b % 4][:, k * P:(k + 1) * P], view[:, b, k * P:(k + 1) * P], ident)
                done[b] = T.did(ins)

            def keep(b):
                A.after(done[b], prod.get(b - 4))
                cols[b] = A.did(a.copy(turned[:, b % 4, :], ps[b % 4][:, 0:D]))

            def product(b):
                T.after(cols[b], fin.get(b - 4))
                for k in range(2):
                    ins = pe.matmul(ps[4 + b % 4][:, 0:D], turned[:, b % 4, k * P:(k + 1) * P], weight[:, k, :],
                                    start=(k == 0), stop=(k == 1))
                prod[b] = T.did(ins)

            def end(b):
                V.after(prod[b])
                fin[b] = finish(b, ps[4 + b % 4][:, 0:D])

            pipeline(NB, (0, turn), (0, keep), (2, product), (3, end))

        def two(name):
            return t[name].rearrange("(k p) n -> p k n", p=P)

        def everywhere(name, n):
            return t[name].rearrange("(o n) -> o n", o=1).to_broadcast([P, n])

        blk_v = Numbers(V, "blk_v", blk_d_row, NB - 1)
        b32_v = Numbers(V, "b32_v", b32_row, NBD - 1)
        blk_t = Numbers(T, "blk_t", blk_d_row, NB - 1)

        w6, w7, wp = (cut(wts, k * 512, 512, 2, D) for k in range(3))
        load(w6, two("L0_gnn_W6"))
        load(w7, two("L0_gnn_W7"))
        load(wp, two("L0_gnn_Wp"))
        b6, b7, bp = (wts[:, 1536 + k * D:1536 + (k + 1) * D] for k in range(3))
        load(b6, everywhere("L0_gnn_b6", D))
        load(b7, everywhere("L0_gnn_b7", D))
        m_weights = load(bp, everywhere("L0_gnn_bp", D))
        m_rec = rec_in.started(sp.dma_start(rec_d, rec_d_dram.rearrange("(p c) r -> p (c r)", p=P)))
        m = V.did(v.memset(x, 0.0))
        S.after(m)
        x_in.started(sp.dma_start(x3[:, 0:NB - 1, :], t["x"][0:(NB - 1) * P, :].rearrange("(b p) k -> p b k", p=P)))
        m_x = x_in.started(sp.dma_start(x3[0:LAST, NB - 1, :], t["x"][(NB - 1) * P:N, :]))
        staged = cut(big, 0, NB * TW, NB, TW)
        V.after(m_x)
        V.did(v.memset(staged[:, :, D:TW], 0.0))
        V.did(v.tensor_copy(staged[:, :, 0:D], x3))
        V.after(V.last())
        m = V.did(v.tensor_copy(staged[:, :, D], deg_s[:, 0:NB]))
        m_table = write_table(x_table, staged, m)
        acc0 = cut(acc, 0, NB * D, NB, D)
        m_zero = V.did(v.memset(acc0, 0.0))

        def gcn_sums(rows_of, s_row, first, onehot, weighted, nbuf):
            weight, summed, added = Marks(), Marks(), Marks()

            def scale(c):
                weight[c] = weighted(c, onehot[:, c % nbuf, :], summed.get(c - nbuf))

            def product(c):
                T.after(s_row(c), weight[c], added.get(c - 8))
                summed[c] = T.did(pe.matmul(ps[c % 8][:, 0:D], onehot[:, c % nbuf, :], rows_of(c),
                                            start=True, stop=True))

            def add(c):
                V.after(summed[c], added.get(c - 1), first)
                here = acc[:, bass.ds(blk_v.at(c) * D, D)]
                added[c] = V.did(v.tensor_tensor(here, here, ps[c % 8][:, 0:D], ALU.add))

            return scale, product, add, summed, added

        RG = 24
        xg = cut(big, NB * TW, RG * TW, RG, TW)
        onehot = cut(ring, 0, 1024, 8, P)
        dst_hot = [cut(ring, 1024 * (1 + k), 1024, 8, P) for k in range(3)]
        picked = cut(ring, 4096, 8 * P, 8, P)
        gathered = [landing(f"gathered{i}") for i in range(RG)]
        got, normed, half_normed, hot_at = Marks(), Marks(), Marks(), Marks()

        def weigh_by_scalar(c, slot, free):
            A.after(normed[c // 8], free)
            return A.did(a.mul(slot, dst_hot[c // 8 % 3][:, c % 8, :], norm[:, c:c + 1]))

        scale, product, add, summed, added = gcn_sums(
            lambda c: xg[:, c % RG, 0:D], lambda c: got[c], [m_zero, m_rec, m_weights], onehot, weigh_by_scalar, 8)

        def gather_x(c):
            G.after(summed.get(c - RG), m_table, m_rec)
            got[c] = gathered[c % RG].started(g.indirect_dma_start(
                out=xg[:, c % RG, :], out_offset=None, in_=x_table,
                in_offset=bass.IndirectOffsetOnAxis(ap=recd3i[:, c, D_IDX:D_IDX + 1], axis=0)))

        din_e, root = small[:, 0:8], small[:, 16:32]
        blk_v2 = Numbers(V, "blk_v2", blk_d_row, NB - 1)
        din_at, weighed = Marks(), Marks()

        def dst_one_hots(i):
            V.after(m_rec, m_din, weighed.get(8 * i - 17))
            hot_at[i] = V.did(v.tensor_tensor(dst_hot[i % 3], rows(iota, 8, P),
                                              lanes(recd3[:, 8 * i:8 * i + 8, D_DL], 8, P), ALU.is_equal))

        def pick_din(c):
            V.after(hot_at[c // 8], din_at.get(c // 8 - 1))
            V.did(v.tensor_tensor(picked[:, c % 8, :], dst_hot[c // 8 % 3][:, c % 8, :],
                                  acc[:, bass.ds(blk_v2.at(c) * P + DIN, P)], ALU.mult))

        def edge_norm(i):
            V.after(V.last())
            din_at[i] = chain(v.tensor_reduce(din_e, picked, AX.X, ALU.add))
            V.after(*[got[c] for c in range(8 * i, 8 * i + 8)])
            r0, at8 = (8 * i) % RG, root[:, 8 * (i % 2):8 * (i % 2) + 8]
            chain(v.tensor_tensor(at8, xg[:, r0:r0 + 8, D], din_e, ALU.mult))
            A.after(chain(v.tensor_scalar(at8, at8, EPS0, None, ALU.add)))
            half_normed[i] = A.did(a.activation(at8, at8, ACT.Sqrt))

        def edge_norm_end(i):
            at8 = root[:, 8 * (i % 2):8 * (i % 2) + 8]
            V.after(half_normed[i])
            chain(v.reciprocal(at8, at8))
            normed[i] = V.did(v.tensor_tensor(norm[:, 8 * i:8 * i + 8], at8, recd3[:, 8 * i:8 * i + 8, D_W], ALU.mult))

        def scale_counted(c):
            scale(c)
            weighed[c] = A.last()

        pipeline(NCD, (0, gather_x), (2, every(8, dst_one_hots, 0)), (3, pick_din), (3, every(8, edge_norm, 7)),
                 (4, every(8, edge_norm_end, 7)), (12, scale_counted), (13, product), (16, add))
        barrier()

        h6 = cut(big, 0, NB * D, NB, D)

        def relu_bias(view, bias):
            def finish(b, product):
                m = chain(v.tensor_tensor(view[:, b, :], product, bias, ALU.add))
                V.did(v.tensor_scalar(view[:, b, :], view[:, b, :], 0.0, None, ALU.max))
                return m
            return finish

        linear(acc0, w6, relu_bias(h6, b6))
        m_table = write_table(h6_table, h6, V.last())
        barrier()
        m_zero = V.did(v.memset(acc0, 0.0))

        def gather_rows(table, width, index, depth, free, spare=0):
            slots = cut(ring, 0, depth * (spare + width), depth, spare + width)
            here = Marks()

            def stage(c):
                G.after(free(c))
                here[c] = gathered[c % depth].started(g.indirect_dma_start(
                    out=slots[:, c % depth, spare:], out_offset=None, in_=table,
                    in_offset=bass.IndirectOffsetOnAxis(ap=index(c), axis=0)))
            return stage, slots, here

        R2 = 12
        gather, hg, got2 = gather_rows(h6_table, D, lambda c: recd3i[:, c, D_IDX:D_IDX + 1], R2,
                                       lambda c: [m_table, summed2.get(c - R2)])

        def weigh(c, slot, free):
            V.after(free)
            return V.did(v.tensor_scalar(slot, iota, recd3[:, c, D_DL:D_DL + 1], norm[:, c:c + 1],
                                         ALU.is_equal, ALU.mult))

        scale, product, add, summed2, _ = gcn_sums(
            lambda c: hg[:, c % R2, :], lambda c: got2[c], m_zero, cut(ring, R2 * D, 512, 4, P), weigh, 4)
        pipeline(NCD, (0, gather), (6, scale), (6, product), (8, add))
        barrier()

        h7 = h6
        linear(acc0, w7, relu_bias(h7, b7))
        V.after(V.last())
        T.after(V.last())

        def residual_bias(bias):
            def finish(b, product):
                m = chain(v.tensor_tensor(x3[:, b, :], x3[:, b, :], product, ALU.add))
                V.did(v.tensor_tensor(x3[:, b, :], x3[:, b, :], bias, ALU.add))
                return m
            return finish

        linear(h7, wp, residual_bias(bp))
        layernorm()
        barrier()

        recs3 = cut(big, 0, NCS * RS, NCS, RS)
        m_recs = rec_in.started(sp.dma_start(big[:, 0:NCS * RS], rec_s_dram.rearrange("(p c) r -> p (c r)", p=P)))
        w1 = wts[0:MUL, 0:2 * MUL]
        wsc = wts[0:MUL, 128:128 + 2 * MUL]
        w2 = wts[:, 256:256 + 2 * MUL]
        gain_s, gain_v = wts[:, 1280:1280 + MUL], wts[:, 1344:1344 + MUL]
        load(w1[:, 0:MUL], t["L1_gnn_w1_s"])
        load(w1[:, MUL:2 * MUL], t["L1_gnn_w1_v"])
        load(wsc[:, 0:MUL], t["L1_gnn_wsc_s"])
        load(wsc[:, MUL:2 * MUL], t["L1_gnn_wsc_v"])
        load(w2[:, 0:MUL], t["L1_gnn_w2_s"])
        load(w2[:, MUL:2 * MUL], t["L1_gnn_w2_v"])
        load(gain_s, everywhere("L1_gnn_g_s", MUL))
        m_weights = load(gain_v, everywhere("L1_gnn_g_v", MUL))
        V.after(m_weights, m_recs)
        T.after(m_weights, m_recs)
        V.did(v.tensor_copy(idx_s, recs3.bitcast(I32)[:, :, S_IDX]))
        m_idx = V.did(v.tensor_copy(sl_s, recs3[:, :, S_SL]))
        T.after(m_idx)

        acc1 = cut(acc, 0, NB * 512, NB, 512)

        def vector_parts(bank, b):
            for q in range(4):
                part = x3[:, b, 0:MUL] if q == 0 else x3[:, b, MUL + q - 1:4 * MUL:3]
                ins = pe.transpose(bank[0:MUL, q * P:(q + 1) * P], part, ident)
            return T.did(ins)

        def parts_product(bank, at0, turned, weights):
            for q in range(4):
                w = weights[:, 0:MUL] if q == 0 else weights[:, MUL:2 * MUL]
                ins = pe.matmul(bank[:, at0 + q * MUL:at0 + (q + 1) * MUL], turned[0:MUL, q * P:(q + 1) * P], w,
                                start=True, stop=True)
            return T.did(ins)

        turned1 = cut(ring, 0, 1024, 2, 512)
        tn, kp, pr, fi = Marks(), Marks(), Marks(), Marks()

        def y_turn(b):
            T.after(kp.get(b - 2))
            tn[b] = vector_parts(ps[b % 2], b)

        def y_keep(b):
            A.after(tn[b], pr.get(b - 2))
            kp[b] = A.did(a.copy(turned1[0:MUL, b % 2, :], ps[b % 2][0:MUL, :]))

        def y_product(b):
            T.after(kp[b], fi.get(b - 2))
            pr[b] = parts_product(ps[2 + b % 2], 0, turned1[:, b % 2, :], w1)

        def y_end(b):
            V.after(pr[b])
            fi[b] = V.did(v.tensor_scalar(acc1[:, b, 0:D], ps[2 + b % 2][:, 0:D], 0.125, None, ALU.mult))

        pipeline(NB, (0, y_turn), (0, y_keep), (1, y_product), (2, y_end))
        m_table = write_table(y_table, acc1[:, :, 0:D], V.last())
        barrier()
        m_zero = V.did(v.memset(acc, 0.0))

        RY = 7
        gather, yg, got_y = gather_rows(y_table, D, lambda c: idx_s[:, c:c + 1], RY,
                                        lambda c: [m_table, m_idx, mixed.get(c - RY)], MUL)
        o = RY * (MUL + D)
        mid = cut(ring, o, 2 * 576, 2, 576)
        o += 2 * 576
        dots = cut(ring, o, 2 * 192, 2, 192)
        o += 2 * 192
        W1 = 8
        w_rows = cut(ring, o, W1 * D, W1, D)
        o += W1 * D
        assert o <= ring.shape[1]
        weights_in = [landing(f"weights_in{k}") for k in range(W1)]
        oh1 = [cut(wts, 1408 + 512 * k, 512, 4, P) for k in range(2)]
        w_ready, mixed, mids, sum1, added1 = Marks(), Marks(), Marks(), Marks(), Marks()
        blk_s = Numbers(V, "blk_s", blk_s_row, NB - 1)

        def read_weights(c):
            S.after(mixed.get(c - W1))
            w_ready[c] = weights_in[c % W1].started(sp.dma_start(w_rows[:, c % W1, :], weights_dram[c]))

        scaled_y, hot1, reduced = Marks(), Marks(), Marks()

        def scale_y(c):
            y = yg[:, c % RY, MUL:]
            A.after(got_y[c], reduced.get(c - 2))
            for d in range(3):
                scaled_y[c] = A.did(a.mul(dots[:, c % 2, d * MUL:(d + 1) * MUL], y[:, (1 + d) * MUL:(2 + d) * MUL],
                                          recs3[:, c, S_SH + 1 + d:S_SH + 2 + d]))

        def one_hot1(c):
            i, hot = c // 4, oh1[c // 4 % 2]
            if c % 4 == 0:
                A.after(sum1.get(c - 5))
            A.did(a.activation(hot[:, c % 4, :], iota, ACT.Abs, bias=neg_sl[:, c:c + 1]))
            if c % 4 == 3:
                A.after(A.last())
                hot1[i] = A.did(a.activation(hot, hot, ACT.Relu, bias=1.0, scale=-1.0))

        def messages(c):
            w, slot, m = w_rows[:, c % W1, :], yg[:, c % RY, :], mid[:, c % 2, :]
            vec = m[:, 0:3 * P].rearrange("p (d s u) -> p d s u", d=3, s=2)
            V.after(scaled_y[c])
            red = reduced[c] = V.did(v.tensor_reduce(
                slot[:, 0:MUL], dots[:, c % 2, :].rearrange("p (d u) -> p u d", d=3), AX.X, ALU.add))
            V.after(w_ready[c], sum1.get(c - 2))
            V.did(v.tensor_tensor(vec[:, :, 1, :], rows(w[:, MUL:2 * MUL], 3, MUL),
                                  slot[:, 2 * MUL:].rearrange("p (d u) -> p d u", d=3), ALU.mult))
            V.after(red)
            t2 = V.did(v.tensor_tensor(m[:, 448:576], w[:, 2 * MUL:4 * MUL], slot[:, 0:2 * MUL], ALU.mult))
            V.did(v.tensor_tensor(m[:, 384:448], w[:, 0:MUL], slot[:, MUL:2 * MUL], ALU.mult))
            mixed[c] = V.last()
            q = G if c % 2 else V
            q.after(t2)
            out3, in3 = vec[:, :, 0, :], rows(m[:, 512:576], 3, MUL)
            sh3 = lanes(recs3[:, c, S_SH + 1:S_SH + 4], 3, MUL)
            if c % 2:
                q.after(sum1.get(c - 2))
            mids[c] = q.did(q.eng.tensor_tensor(out3, in3, sh3, ALU.mult))

        def sums(c):
            u = c // GS
            T.after(mids[c], mixed[c], hot1[c // 4], added1.get(u - 2) if c % GS == 0 else None)
            sum1[c] = T.did(pe.matmul(ps[6 + u % 2], oh1[c // 4 % 2][:, c % 4, :], mid[:, c % 2, 0:512],
                                      start=(c % GS == 0), stop=(c % GS == GS - 1)))

        def add_unit(c):
            if c % GS == GS - 1:
                u = c // GS
                V.after(sum1[c], added1.get(u - 1), m_zero)
                here = acc[:, bass.ds(blk_s.at(u) * 512, 512)]
                added1[u] = V.did(v.tensor_tensor(here, here, ps[6 + u % 2], ALU.add))

        neg_sl = norm[:, 0:NCS]
        A.after(m_recs, V.did(v.tensor_scalar(neg_sl, sl_s, -1.0, None, ALU.mult)))
        G.after(m_recs)
        pipeline(NCS, (1, read_weights), (2, gather), (7, scale_y), (5, one_hot1), (8, messages), (9, sums),
                 (11, add_unit))
        barrier()

        o1 = cut(big, 0, NB * D, NB, D)
        dn = small[:, 0:NB]
        chain(v.tensor_scalar(dn, deg_s[:, NB:2 * NB], 1.0, None, ALU.max))
        rsqrt_of(dn, V.last())
        chain(v.tensor_scalar(dn, dn, float(1.0 / np.sqrt(2.0 * MUL)), None, ALU.mult))
        sq, ss = cut(ring, 2100, D, D), cut(small, 50, 2 * NB, 2, NB)
        turned_a, turned_x = cut(ring, 0, 1024, 2, 512), cut(ring, 1024, 1024, 2, 512)
        tn, kp, pr, fi = Marks(), Marks(), Marks(), Marks()

        def o_turn(b):
            T.after(kp.get(b - 1))
            for q in range(4):
                at1 = 3 * P if q == 0 else (q - 1) * P
                pe.transpose(ps[0][:, q * P:(q + 1) * P], acc1[:, b, at1:at1 + P], ident)
            tn[b] = vector_parts(ps[1], b)

        def o_keep(b):
            A.after(tn[b], pr.get(b - 2))
            A.did(a.copy(turned_a[:, b % 2, :], ps[0]))
            kp[b] = A.did(a.copy(turned_x[0:MUL, b % 2, :], ps[1][0:MUL, :]))

        def o_product(b):
            T.after(kp[b], fi.get(b - 2))
            for q in range(4):
                pe.matmul(ps[2 + b % 2][:, q * MUL:(q + 1) * MUL], turned_a[:, b % 2, q * P:(q + 1) * P],
                          w2[:, 0:MUL] if q == 0 else w2[:, MUL:2 * MUL], start=True, stop=True)
            pr[b] = parts_product(ps[2 + b % 2], D, turned_x[:, b % 2, :], wsc)

        def o_end(b):
            V.after(pr[b])
            m = V.did(v.tensor_scalar(o1[:, b, :], ps[2 + b % 2][:, 0:D], dn[:, b:b + 1], None, ALU.mult))
            V.after(m)
            fi[b] = V.did(v.scalar_tensor_tensor(out=o1[:, b, :], in0=ps[2 + b % 2][:, D:2 * D], scalar=0.125,
                                                 in1=o1[:, b, :], op0=ALU.mult, op1=ALU.add))
            A.after(fi[b], A.last())
            m = A.did(a.activation(sq[:, 0:MUL], o1[:, b, 0:MUL], ACT.Square, accum_out=ss[:, 0, b:b + 1]))
            A.after(m)
            A.did(a.activation(sq[:, MUL:D], o1[:, b, MUL:D], ACT.Square, accum_out=ss[:, 1, b:b + 1]))

        pipeline(NB, (0, o_turn), (0, o_keep), (1, o_product), (2, o_end))
        V.after(A.last(), V.last())
        chain(v.tensor_scalar(ss[:, 0, :], ss[:, 0, :], 1.0 / MUL, EPS1, ALU.mult, ALU.add))
        chain(v.tensor_scalar(ss[:, 1, :], ss[:, 1, :], 1.0 / (3 * MUL), EPS1, ALU.mult, ALU.add))
        rsqrt_of(small[:, 50:50 + 2 * NB], V.last())
        for b in range(NB):
            ov = o1[:, b, MUL:D].rearrange("p (d u) -> p d u", d=3)
            xv = x3[:, b, MUL:D].rearrange("p (u d) -> p d u", d=3)
            V.did(v.scalar_tensor_tensor(out=o1[:, b, 0:MUL], in0=o1[:, b, 0:MUL], scalar=ss[:, 0, b:b + 1],
                                         in1=gain_s, op0=ALU.mult, op1=ALU.mult))
            m = V.did(v.scalar_tensor_tensor(out=ov, in0=ov, scalar=ss[:, 1, b:b + 1], in1=rows(gain_v, 3, MUL),
                                             op0=ALU.mult, op1=ALU.mult))
            V.after(m)
            V.did(v.tensor_tensor(x3[:, b, 0:MUL], x3[:, b, 0:MUL], o1[:, b, 0:MUL], ALU.add))
            V.did(v.tensor_tensor(xv, xv, ov, ALU.add))
        layernorm()
        barrier()

        alpha = cut(big, 0, NCD * H, NCD, H)
        h_at = NCD * H
        hdst = cut(big, h_at, NB * TW, NB, TW)
        hsrc = cut(acc, 0, NB * TW, NB, TW)
        wexp = cut(acc, NB * TW, 16 * D, 16, D)
        w_att, w_att_t = cut(wts, 0, 512, 2, D), cut(wts, 512, 512, 2, D)
        a_src, a_dst, bias = wts[:, 1024:1280], wts[:, 1280:1536], wts[:, 1536:1792]
        top, top_t = small[:, 0:2 * NBD], small[:, 2 * NBD:4 * NBD]
        m_z = V.did(v.memset(wexp, 0.0))
        load(w_att, two("L2_gnn_W"))
        load(a_src, t["L2_gnn_a_src"].rearrange("(o h) d -> o (h d)", o=1).to_broadcast([P, D]))
        load(a_dst, t["L2_gnn_a_dst"].rearrange("(o h) d -> o (h d)", o=1).to_broadcast([P, D]))
        m_weights = load(bias, everywhere("L2_gnn_bias", D))
        ew_out = landing("ew_out")
        with nc.allow_non_contiguous_dma("the transposed edge weights, once"):
            ew_out.started(sp.dma_start(ew_dram[0:3, :], t["L2_gnn_edge_W"].rearrange("n f -> f n")))
        m = ew_out.started(sp.dma_start(ew_dram[3:4, :], t["L2_gnn_edge_b"].rearrange("(o n) -> o n", o=1)))
        S.after(m, m_z)
        for k in range(16):
            m_wexp = load(wexp[k * RD + D_EA:k * RD + D_EA + 4, k, :], ew_dram)
        T.after(m_weights)
        V.after(m_weights, m_wexp)
        for ki in range(2):
            for ko in range(2):
                ins = pe.transpose(ps[4 + ki][:, ko * P:(ko + 1) * P], w_att[:, ko, ki * P:(ki + 1) * P], ident)
        V.after(T.did(ins))
        for ki in range(2):
            m = V.did(v.tensor_copy(w_att_t[:, ki, :], ps[4 + ki][:, 0:D]))
        T.after(m)
        logit = ring[:, 2048:2048 + D]

        def attention_tables(b, product):
            A.after((T.sem, T.count), V.last())
            A.did(a.copy(hsrc[:, b, 0:D], product))
            V.after(A.did(a.copy(hdst[:, b, 0:D], product)))
            for a_vec, where in ((a_src, hsrc), (a_dst, hdst)):
                chain(v.tensor_tensor(logit, hdst[:, b, 0:D], a_vec, ALU.mult))
                chain(v.tensor_reduce(where[:, b, D:TW], logit.rearrange("p (h d) -> p h d", h=H), AX.X, ALU.add))
            return V.last()

        linear(x3, w_att_t, attention_tables)
        m_table = write_table(att_table, hsrc, V.last())
        m_top = V.did(v.memset(top, -BIG))
        T.after(m_wexp, V.last())

        R3 = 12
        gather, ag, got_a = gather_rows(att_table, TW, lambda c: recd3i[:, c, D_IDX:D_IDX + 1], R3,
                                        lambda c: [m_table, spilled.get(c - R3), used2.get(c - R3)])
        o = R3 * TW
        oh2_t = cut(ring, o, 8 * P, 8, P)
        o += 8 * P
        rec_t2 = cut(ring, o, 2 * P, 2, P)
        o += 2 * P
        enc = cut(ring, o, 3 * D, 3, D)
        o += 3 * D
        prod2 = cut(ring, o, 2 * D, 2, D)
        o += 2 * D
        miss = cut(ring, o, 4 * SUB, 4, SUB)
        o += 4 * SUB
        red4, lg4, mx = cut(ring, o, 64, 8, H), cut(ring, o + 64, 64, 8, H), cut(ring, o + 128, 16, 2, 8)
        assert o + 144 <= ring.shape[1]
        o = NB * TW + 16 * D
        oh2 = [cut(acc, o + k * 512, 512, 4, P) for k in range(2)]
        spread = cut(acc, o + 1024, 1024, 4, D)
        assert o + 2048 <= acc.shape[1]
        spill = [landing(f"spill{i}") for i in range(R3)]
        spilled, logits, hot2, oht, ohk, rt2, rk2 = Marks(), Marks(), Marks(), Marks(), Marks(), Marks(), Marks()
        hd_at, enc_at, enc_ok, used2, masked, mtop, maxed = Marks(), Marks(), Marks(), Marks(), Marks(), Marks(), Marks()

        def spill_rows(c):
            S.after(got_a[c])
            spilled[c] = spill[c % R3].started(sp.dma_start(rows_spill[c], ag[:, c % R3, 0:D]))

        neg_dl = norm
        m_neg = V.did(v.tensor_scalar(neg_dl, recd3[:, :, D_DL], -1.0, None, ALU.mult))
        A.after(m_neg)

        def one_hots(i, hot, free):
            A.after(free)
            for k in range(4):
                A.did(a.activation(hot[:, k, :], iota, ACT.Abs, bias=neg_dl[:, 4 * i + k:4 * i + k + 1]))
            A.after(A.last())
            hot2[i] = A.did(a.activation(hot, hot, ACT.Relu, bias=1.0, scale=-1.0))

        def one_hot4x(i):
            one_hots(i, oh2[i % 2], oht.get(i - 2))

        def turn_one_hots(i, hot, free, bank_read=None):
            T.after(hot2[i], ohk.get(i - 1), bank_read)
            for k in range(4):
                ins = pe.transpose(ps[0][:, k * P:(k + 1) * P], hot[:, k, :], ident)
            oht[i] = T.did(ins)
            A.after(oht[i], free)
            ohk[i] = A.did(a.copy(oh2_t[:, 4 * (i % 2):4 * (i % 2) + 4, :].rearrange("p k e -> p (k e)"), ps[0]))

        def turn_records(c):
            if c % 16 == 0:
                i = c // 16
                T.after(ohk.get(c // 4 - 1))
                rt2[i] = T.did(pe.transpose(ps[0][:, 0:P], rec_d[:, i * P:(i + 1) * P], ident))
                A.after(rt2[i], enc_at.get(16 * (i - 1) - 1))
                rk2[i] = A.did(a.copy(rec_t2[:, i % 2, :], ps[0][:, 0:P]))

        def node_and_edge_parts(c):
            T.after(rk2[c // 16], enc_ok.get(c - 2))
            enc_at[c] = T.did(pe.matmul(ps[4 + c % 2][:, 0:D], rec_t2[:, (c // 16) % 2, :], wexp[:, c % 16, :],
                                        start=True, stop=True))
            A.after(enc_at[c], used2.get(c - 3))
            enc_ok[c] = A.did(a.activation(enc[:, c % 3, :], ps[4 + c % 2][:, 0:D], ACT.Relu))
            T.after(ohk[c // 4], used2.get(c - 3))
            hd_at[c] = T.did(pe.matmul(ps[1 + c % 3][:, 0:TW], oh2_t[:, c % 8, :],
                                       big[:, bass.ds(blk_t.at(c) * TW + h_at, TW)], start=True, stop=True))

        def edge_product(c):
            hd = ps[1 + c % 3]
            V.after(hd_at[c], enc_ok[c], got_a[c], reduced2.get(c - 2), logits.get(c // 4 - 2))
            made[c] = V.did(v.tensor_tensor(prod2[:, c % 2, :], hd[:, 0:D], enc[:, c % 3, :], ALU.mult))
            used2[c] = V.did(v.tensor_tensor(lg4[:, c % 8, :], hd[:, D:TW], ag[:, c % R3, D:TW], ALU.add))

        def edge_dot(c):
            V.after(made[c], logits.get(c // 4 - 2))
            reduced2[c] = V.did(v.tensor_reduce(
                red4[:, c % 8, :], prod2[:, c % 2, :].rearrange("p (h d) -> p h d", h=H), AX.X, ALU.add))

        def edge_logits(i):
            V.after(masked.get(4 * i - 1), masked.get(4 * i - 2))
            V.did(v.tensor_tensor(miss, rows(iota[:, 0:SUB], 4, SUB),
                                  lanes(recd3[:, 4 * i:4 * i + 4, D_DL32], 4, SUB), ALU.not_equal))
            V.after(V.last())
            V.did(v.tensor_scalar(miss, miss, -BIG, None, ALU.mult))
            V.after(reduced2[4 * i + 3])
            lg = lg4[:, 4 * (i % 2):4 * (i % 2) + 4, :]
            chain(v.tensor_tensor(lg, lg, red4[:, 4 * (i % 2):4 * (i % 2) + 4, :], ALU.add))
            logits[i] = V.did(v.scalar_tensor_tensor(out=alpha[:, 4 * i:4 * i + 4, :], in0=lg, scalar=0.2, in1=lg,
                                                     op0=ALU.mult, op1=ALU.max))
            for q in (V, G):
                q.after(logits[i], mtop.get(4 * i - 1))
            for k in range(4):
                q = G if k % 2 else V
                masked[4 * i + k] = q.did(q.eng.tensor_tensor(
                    spread[:, k, :].rearrange("p (h n) -> p h n", h=H), rows(miss[:, k, :], H, SUB),
                    lanes(alpha[:, 4 * i + k, :], H, SUB), ALU.add))

        made = Marks()
        reduced2 = Marks()

        def turn_masked(c):
            T.after(masked[c], maxed.get(c // 4 - 1))
            for k in range(2):
                ins = pe.transpose(ps[6 + c % 4 // 2][:, (2 * (c % 2) + k) * P:(2 * (c % 2) + k + 1) * P],
                                   spread[:, c % 4, k * P:(k + 1) * P], ident)
            mtop[c] = T.did(ins)

        def node_max(i):
            for k in range(2):
                V.after(mtop[4 * i + 2 * k + 1], m_top, kept.get(4 * i - 5))
                maxed[i] = V.did(v.tensor_reduce(mx[:, i % 2, 4 * k:4 * k + 4],
                                                 ps[6 + k].rearrange("p (k e) -> p k e", e=P), AX.X, ALU.max))

        def keep_max(c):
            V.after(maxed[c // 4], V.last() if c % 4 == 0 else None, kept.get(c - 1))
            here = small[:, bass.ds(b32_v.at(c) * 2, 2)]
            kept[c] = V.did(v.tensor_tensor(here, here, mx[:, c // 4 % 2, 2 * (c % 4):2 * (c % 4) + 2], ALU.max))

        kept = Marks()

        def four(stage):
            def all4(i):
                for c in range(4 * i, 4 * i + 4):
                    stage(c)
            return all4

        def turns(i):
            turn_records(4 * i)
            turn_one_hots(i, oh2[i % 2], hd_at.get(4 * i - 5), rk2[i // 4])

        pipeline(NCD, (0, gather), (3, spill_rows), (2, every(4, one_hot4x, 0)), (4, every(4, turns, 0)),
                 (8, node_and_edge_parts), (9, edge_product), (10, edge_dot), (11, every(4, edge_logits, 3)),
                 (14, every(4, four(turn_masked), 3)), (17, every(4, node_max, 3)), (21, keep_max))
        barrier()

        top4 = top.rearrange("p (b s k) -> p b s k", s=4, k=2)
        top_t4 = top_t.rearrange("p (b k q) -> p b k q", k=2, q=4)
        for q in range(4):
            for s in range(4):
                V.did(v.tensor_copy(top_t4[s * SUB:(s + 1) * SUB, :, :, q], top4[q * SUB:(q + 1) * SUB, :, s, :]))
        m_top = V.last()
        m_zero = V.did(v.memset(hsrc, 0.0))
        RB = 16
        hs = cut(acc, NB * TW + 2048, RB * D, RB, D)
        spill += [landing(f"spill{i}") for i in range(R3, RB)]
        o = 0
        oh2_t = cut(ring, o, 8 * P, 8, P)
        o += 8 * P
        msg = cut(ring, o, 8 * TW, 8, TW)
        o += 8 * TW
        below = cut(ring, o, 8 * H, 8, H)
        assert o + 8 * H + 2048 <= ring.shape[1]
        oh3 = [cut(acc, NB * TW + k * 512, 512, 4, P) for k in range(4)]
        oh3 += [cut(ring, o + 8 * H + k * 512, 512, 4, P) for k in range(4)]
        back = Marks()
        hot2.clear(), oht.clear(), ohk.clear()
        tops, lows, exps, msgs, sum2, added2 = Marks(), Marks(), Marks(), Marks(), Marks(), Marks()
        blk_v.first = blk_t.first = None

        def read_rows(c):
            S.after(msgs.get(c - RB))
            back[c] = spill[c % RB].started(sp.dma_start(hs[:, c % RB, :], rows_spill[c]))

        def one_hot_b(i):
            one_hots(i, oh3[i % 8], sum2.get(4 * i - 29))

        def gather_tops(c):
            T.after(ohk[c // 4], lows.get(c // 4 - 2), m_top)
            tops[c] = T.did(pe.matmul(ps[2 + c // 4 % 2][:, (c % 4) * H:(c % 4 + 1) * H], oh2_t[:, c % 8, :],
                                      small[:, bass.ds(blk_t.at(c) * H + 2 * NBD, H)], start=True, stop=True))

        def exponents(i):
            low = below[:, 4 * (i % 2):4 * (i % 2) + 4, :]
            V.after(tops[4 * i + 3], exps.get(i - 2))
            lows[i] = V.did(v.tensor_tensor(low, alpha[:, 4 * i:4 * i + 4, :],
                                            ps[2 + i % 2][:, 0:4 * H].rearrange("p (c h) -> p c h", h=H),
                                            ALU.subtract))
            V.after(lows[i])
            m = V.did(v.tensor_scalar(low, low, 0.0, None, ALU.min))
            A.after(m, sum2.get(4 * i - 5))
            exps[i] = A.did(a.activation(msg[:, 4 * (i % 2):4 * (i % 2) + 4, D:TW], low, ACT.Exp))

        def weighted(c):
            q = G if c % 2 else V
            q.after(exps[c // 4], back[c], sum2.get(c - 8))
            msgs[c] = q.did(q.eng.tensor_tensor(msg[:, c % 8, 0:D].rearrange("p (h d) -> p h d", h=H),
                                                hs[:, c % RB, :].rearrange("p (h d) -> p h d", h=H),
                                                lanes(msg[:, c % 8, D:TW], H, HD), ALU.mult))

        def sum_messages(c):
            T.after(msgs[c], added2.get(c - 4))
            sum2[c] = T.did(pe.matmul(ps[4 + c % 4][:, 0:TW], oh3[c // 4 % 8][:, c % 4, :], msg[:, c % 8, :],
                                      start=True, stop=True))

        def add_messages(c):
            V.after(sum2[c], added2.get(c - 1), m_zero)
            here = acc[:, bass.ds(blk_v.at(c) * TW, TW)]
            added2[c] = V.did(v.tensor_tensor(here, here, ps[4 + c % 4][:, 0:TW], ALU.add))

        def turns_b(i):
            turn_one_hots(i, oh3[i % 8], tops.get(4 * i - 5))

        pipeline(NCD, (0, read_rows), (0, every(4, one_hot_b, 0)), (4, every(4, turns_b, 0)), (8, gather_tops),
                 (10, every(4, exponents, 3)), (14, weighted), (15, sum_messages), (18, add_messages))
        V.after(V.last())
        den = ring[:, 0:NB * H].rearrange("p (b h) -> p b h", h=H)
        barrier()
        chain(v.tensor_scalar(den, hsrc[:, :, D:TW], 1e-10, None, ALU.max))
        chain(v.reciprocal(den, den))
        for b in range(NB):
            o2 = hsrc[:, b, 0:D]
            m = V.did(v.tensor_tensor(o2.rearrange("p (h d) -> p h d", h=H), o2.rearrange("p (h d) -> p h d", h=H),
                                      lanes(den[:, b, :], H, HD), ALU.mult))
            V.did(v.tensor_tensor(x3[:, b, :], x3[:, b, :], bias, ALU.add))
            V.after(V.last())
            V.did(v.tensor_tensor(x3[:, b, :], x3[:, b, :], o2, ALU.add))
        layernorm()
        barrier()

        w3, b3 = cut(wts, 0, 512, 2, D), wts[:, 512:512 + D]
        load(w3, two("L3_gnn_W"))
        m_weights = load(b3, everywhere("L3_gnn_b", D))
        dinv = small[:, 0:NB]
        scaled = cut(big, 0, NB * D, NB, D)
        chain(v.tensor_scalar(dinv, deg_d[:, NB:2 * NB], 1.0, None, ALU.add))
        rsqrt_of(dinv, V.last())
        T.after(m_weights)
        V.after(m_weights)

        def scale_rows(b, product):
            chain(v.tensor_tensor(scaled[:, b, :], product, b3, ALU.add))
            return chain(v.tensor_scalar(scaled[:, b, :], scaled[:, b, :], dinv[:, b:b + 1], None, ALU.mult))

        linear(x3, w3, scale_rows)
        m_table = write_table(scaled_table, scaled, V.last())
        m_zero = V.did(v.memset(acc0, 0.0))
        R4 = 12
        gather, sg, got4 = gather_rows(scaled_table, D, lambda c: idx_s[:, c:c + 1], R4,
                                       lambda c: [m_table, sum4.get(c - R4)])
        oh4 = cut(ring, R4 * D, 4 * P, 4, P)
        sum4, oh4_at, added4 = Marks(), Marks(), Marks()
        blk_s.first = None

        def one_hot4(c):
            V.after(sum4.get(c - 4))
            oh4_at[c] = V.did(v.tensor_scalar(oh4[:, c % 4, :], iota, sl_s[:, c:c + 1], None, ALU.is_equal))

        def sums4(c):
            u = c // GS
            T.after(oh4_at[c], got4[c], added4.get(u - 4) if c % GS == 0 else None)
            sum4[c] = T.did(pe.matmul(ps[4 + u % 4][:, 0:D], oh4[:, c % 4, :], sg[:, c % R4, :],
                                      start=(c % GS == 0), stop=(c % GS == GS - 1)))

        def add4(c):
            if c % GS == GS - 1:
                u = c // GS
                V.after(sum4[c], added4.get(u - 1), m_zero)
                here = acc[:, bass.ds(blk_s.at(u) * D, D)]
                added4[u] = V.did(v.tensor_tensor(here, here, ps[4 + u % 4][:, 0:D], ALU.add))

        barrier()
        pipeline(NCS, (0, gather), (5, one_hot4), (6, sums4), (8, add4))
        barrier()
        for b in range(NB):
            m = V.did(v.tensor_tensor(acc0[:, b, :], acc0[:, b, :], scaled[:, b, :], ALU.add))
            V.after(m)
            V.did(v.scalar_tensor_tensor(out=x3[:, b, :], in0=acc0[:, b, :], scalar=dinv[:, b:b + 1],
                                         in1=x3[:, b, :], op0=ALU.mult, op1=ALU.add))
        m = layernorm()
        S.after(m)
        stored = landing("stored")
        stored.started(sp.dma_start(out[0:(NB - 1) * P, :].rearrange("(b p) k -> p b k", p=P), x3[:, 0:NB - 1, :]))
        S.after(stored.started(sp.dma_start(out[(NB - 1) * P:N, :], x3[0:LAST, NB - 1, :])))
        barrier()


_INS = ['x', 'src', 'dst', 'edge_attr_3', 'edge_attr_4', 'edge_attr_8', 'edge_weight', 'L0_gnn_W6', 'L0_gnn_b6',
        'L0_gnn_W7', 'L0_gnn_b7', 'L0_gnn_Wp', 'L0_gnn_bp', 'L1_gnn_w1_s', 'L1_gnn_w1_v', 'L1_gnn_wsc_s',
        'L1_gnn_wsc_v', 'L1_gnn_w2_s', 'L1_gnn_w2_v', 'L1_gnn_fc_w1', 'L1_gnn_fc_w2', 'L1_gnn_fc_w3', 'L1_gnn_g_s',
        'L1_gnn_g_v', 'L2_gnn_W', 'L2_gnn_a_src', 'L2_gnn_a_dst', 'L2_gnn_edge_W', 'L2_gnn_edge_b', 'L2_gnn_bias',
        'L3_gnn_W', 'L3_gnn_b']


def kernel(**inputs):
    import concourse.bacc as bacc
    from concourse.bass_utils import run_bass_kernel_spmd

    nc = bacc.Bacc("TRN2", target_bir_lowering=False, num_devices=1)
    arrays, tensors = Marks(), Marks()
    for name in _INS:
        arr = np.ascontiguousarray(inputs[name])
        arrays[f"in_{name}"] = arr
        tensors[name] = nc.dram_tensor(f"in_{name}", arr.shape, mybir.dt.from_np(arr.dtype), kind="ExternalInput").ap()
    result = nc.dram_tensor("result", (N, D), F32, kind="ExternalOutput").ap()
    program(nc, tensors, result)
    r = run_bass_kernel_spmd(nc, [arrays], core_ids=[0])
    return r.results[0]["result"]
```
